# Optimizing a Trainium2 kernel written in Bass

```python
import numpy as np
import jax
import jax.numpy as jnp

def _softmax(x, axis=-1):
    return jax.nn.softmax(x, axis=axis)

def _gelu(x):
    return jax.nn.gelu(x, approximate=True)

def _silu(x):
    return jax.nn.silu(x)

def _sigmoid(x):
    return jax.nn.sigmoid(x)

def _layernorm(x, axis=-1, eps=1e-05):
    m = jnp.mean(x, axis=axis, keepdims=True)
    v = jnp.var(x, axis=axis, keepdims=True)
    return (x - m) / jnp.sqrt(v + eps)

def _scatter_add(tgt, idx, src, axis=0):
    return tgt.at[idx].add(src)

def _segment_sum(src, seg, n):
    return jax.ops.segment_sum(src, seg, n)
kernel_name = 'mk_conv_seq_d2_conv_nchw256_r2_78722a'

def setup_inputs(seed: int=0):
    np.random.seed(seed)
    _w = jnp.asarray

    def _rec_inputs():
        import jax
        import jax.numpy as jnp
        _gk = jax.random.key(seed)
        x = -0.0003929 + 0.9999 * jax.random.normal(jax.random.fold_in(_gk, 1), (16, 128, 32, 32), jnp.float32)
        return x
    x = _rec_inputs()

    def _L0_conv_setup():
        import jax, jax.numpy as jnp
        import numpy as np
        WS = 8
        C = 128
        NH = 8
        FF = 512
        EPS = 1e-05

        def _rel_pos_index(ws):
            coords = np.stack(np.meshgrid(np.arange(ws), np.arange(ws), indexing='ij')).reshape(2, -1)
            rel = (coords[:, :, None] - coords[:, None, :]).transpose(1, 2, 0)
            rel[:, :, 0] += ws - 1
            rel[:, :, 1] += ws - 1
            rel[:, :, 0] *= 2 * ws - 1
            return rel.sum(-1)

        def _ln(x, g, b):
            m = x.mean(-1, keepdims=True)
            v = jnp.var(x, axis=-1, keepdims=True)
            return (x - m) / jnp.sqrt(v + EPS) * g + b

        def _swin_block(tok, h, w, ln1_g, ln1_b, qkv_w, qkv_b, proj_w, proj_b, rpb_table, rpi, ln2_g, ln2_b, w1, b1, w2, b2):
            b = tok.shape[0]
            N = WS * WS
            hd = C // NH
            t = _ln(tok, ln1_g, ln1_b).reshape(b, h // WS, WS, w // WS, WS, C)
            t = t.transpose(0, 1, 3, 2, 4, 5).reshape(-1, N, C)
            qkv = (t @ qkv_w.T + qkv_b).reshape(-1, N, 3, NH, hd).transpose(2, 0, 3, 1, 4)
            q, k, v = (qkv[0], qkv[1], qkv[2])
            scale = hd ** (-0.5)
            attn = jnp.einsum('whnd,whmd->whnm', q * scale, k)
            bias = rpb_table[rpi].transpose(2, 0, 1)
            attn = jax.nn.softmax(attn + bias, axis=-1)
            out = jnp.einsum('whnm,whmd->whnd', attn, v).transpose(0, 2, 1, 3).reshape(-1, N, C)
            out = out @ proj_w.T + proj_b
            out = out.reshape(b, h // WS, w // WS, WS, WS, C).transpose(0, 1, 3, 2, 4, 5).reshape(b, h * w, C)
            tok = tok + out
            t2 = _ln(tok, ln2_g, ln2_b)
            t2 = jax.nn.gelu(t2 @ w1.T + b1, approximate=False) @ w2.T + b2
            return tok + t2
        key = jax.random.key(seed)
        ks = jax.random.split(key, 8)
        s = 0.02
        return {'x': jax.random.normal(ks[0], (16, C, 32, 32), jnp.float32), 'ln1_g': jnp.ones((C,), jnp.float32), 'ln1_b': jnp.zeros((C,), jnp.float32), 'qkv_w': jax.random.normal(ks[1], (3 * C, C), jnp.float32) * s, 'qkv_b': jnp.zeros((3 * C,), jnp.float32), 'proj_w': jax.random.normal(ks[2], (C, C), jnp.float32) * s, 'proj_b': jnp.zeros((C,), jnp.float32), 'rpb_table': jax.random.normal(ks[3], ((2 * WS - 1) ** 2, NH), jnp.float32) * s, 'ln2_g': jnp.ones((C,), jnp.float32), 'ln2_b': jnp.zeros((C,), jnp.float32), 'w1': jax.random.normal(ks[4], (FF, C), jnp.float32) * s, 'b1': jnp.zeros((FF,), jnp.float32), 'w2': jax.random.normal(ks[5], (C, FF), jnp.float32) * s, 'b2': jnp.zeros((C,), jnp.float32), 'rpi': jnp.asarray(_rel_pos_index(WS), jnp.int32)}
    _L0_conv_all = _L0_conv_setup()
    _L0_conv_in = {k: v for k, v in _L0_conv_all.items() if k in ('ln1_g', 'ln1_b', 'qkv_w', 'qkv_b', 'proj_w', 'proj_b', 'rpb_table', 'ln2_g', 'ln2_b', 'w1', 'b1', 'w2', 'b2', 'rpi')}
    del _L0_conv_all

    def _L1_conv_setup():
        import jax, jax.numpy as jnp
        import numpy as np
        B, DIM, H, W = (8, 128, 32, 32)

        def conv2d(x, w, b=None, pad=(0, 0), dil=(1, 1), groups=1):
            out = jax.lax.conv_general_dilated(x, w, window_strides=(1, 1), padding=[(pad[0], pad[0]), (pad[1], pad[1])], rhs_dilation=dil, dimension_numbers=('NCHW', 'OIHW', 'NCHW'), feature_group_count=groups)
            return out if b is None else out + b[None, :, None, None]

        def gap(x):
            return jnp.mean(x, axis=(2, 3), keepdims=True)

        def _fgm(x, w1, b1, w2, b2, alpha, beta, boost):
            x1 = conv2d(x, w1, b1)
            x2 = conv2d(x, w2, b2)
            x2_fft = jnp.fft.fft2(x2)
            h, w = (x.shape[-2], x.shape[-1])
            fh = jnp.fft.fftfreq(h)[:, None]
            fw = jnp.fft.fftfreq(w)[None, :]
            mask = (jnp.sqrt(fh ** 2 + fw ** 2) > 0.3).astype(jnp.float32)[None, None]
            enhanced = x2_fft * (1.0 + boost[None] * mask)
            out = jnp.abs(jnp.fft.ifft2(x1 * enhanced))
            return out * alpha[None] + x * beta[None]

        def _forward(x, in_w, in_b, out_w, out_b, dilh_w, dilv_w, pyr_w, pyr_b, fuse_w, fuse_b, dw11_w, dw11_b, cr_w, cr_b, batt_w1, batt_b1, batt_w2, batt_b2, conv_w, conv_b, fac_w, fac_b, fgm_w1, fgm_b1, fgm_w2, fgm_b2, fgm_alpha, fgm_beta, fgm_boost, vis_w, vis_b, base_weights):
            dim = x.shape[1]
            out0 = jax.nn.gelu(conv2d(x, in_w, in_b), approximate=False)
            x_att = conv2d(gap(out0), fac_w, fac_b)
            x_fft = jnp.fft.fft2(out0) * x_att
            x_fca = jnp.abs(jnp.fft.ifft2(x_fft))
            x_att2 = conv2d(gap(x_fca), conv_w, conv_b)
            x_sca = x_att2 * x_fca
            x_sca = _fgm(x_sca, fgm_w1, fgm_b1, fgm_w2, fgm_b2, fgm_alpha, fgm_beta, fgm_boost)
            h_out = conv2d(out0, dilh_w, None, pad=(0, 33), dil=(1, 11), groups=dim)
            h_out = conv2d(h_out, cr_w[0], cr_b[0], pad=(1, 1), groups=dim)
            v_out = conv2d(out0, dilv_w, None, pad=(33, 0), dil=(11, 1), groups=dim)
            v_out = conv2d(v_out, cr_w[1], cr_b[1], pad=(1, 1), groups=dim)
            dils = (1, 6, 12, 20)
            feats = [conv2d(out0, pyr_w[i], pyr_b[i], pad=(d, d), dil=(d, d), groups=dim // 4) for i, d in enumerate(dils)]
            pyr = jnp.concatenate(feats, axis=1)
            pyr = conv2d(pyr, fuse_w, fuse_b, groups=dim)
            pyr = conv2d(pyr, cr_w[2], cr_b[2], pad=(1, 1), groups=dim)
            point = conv2d(out0, dw11_w, dw11_b, groups=dim)
            a = jax.nn.relu(conv2d(gap(out0), batt_w1, batt_b1))
            adaptive = jax.nn.sigmoid(conv2d(a, batt_w2, batt_b2))[:, :, 0, 0]
            edge = jax.nn.sigmoid(conv2d(out0, vis_w, vis_b, pad=(1, 1)))
            base = jax.nn.softmax(base_weights)
            comb = jax.nn.softmax(base[None] * adaptive, axis=1)
            cw = comb[:, :, None, None]
            out = x + cw[:, 0:1] * (1.0 + edge) * h_out + cw[:, 1:2] * (1.0 + edge) * v_out + cw[:, 2:3] * (1.0 - 0.3 * edge) * pyr + cw[:, 3:4] * point + cw[:, 4:5] * x_sca
            out = jax.nn.relu(out)
            return conv2d(out, out_w, out_b)
        key = jax.random.key(seed)
        ks = iter(jax.random.split(key, 32))

        def rnd(shape, s=0.02):
            return jax.random.normal(next(ks), shape, jnp.float32) * s
        d4, d8 = (DIM // 4, DIM // 8)
        return {'x': rnd((B, DIM, H, W), 1.0), 'in_w': rnd((DIM, DIM, 1, 1)), 'in_b': rnd((DIM,), 0.01), 'out_w': rnd((DIM, DIM, 1, 1)), 'out_b': rnd((DIM,), 0.01), 'dilh_w': rnd((DIM, 1, 1, 7)), 'dilv_w': rnd((DIM, 1, 7, 1)), 'pyr_w': rnd((4, d4, 4, 3, 3)), 'pyr_b': rnd((4, d4), 0.01), 'fuse_w': rnd((DIM, 1, 1, 1)), 'fuse_b': rnd((DIM,), 0.01), 'dw11_w': rnd((DIM, 1, 1, 1)), 'dw11_b': rnd((DIM,), 0.01), 'cr_w': rnd((3, DIM, 1, 3, 3)), 'cr_b': rnd((3, DIM), 0.01), 'batt_w1': rnd((d8, DIM, 1, 1)), 'batt_b1': rnd((d8,), 0.01), 'batt_w2': rnd((5, d8, 1, 1)), 'batt_b2': rnd((5,), 0.01), 'conv_w': rnd((DIM, DIM, 1, 1)), 'conv_b': rnd((DIM,), 0.01), 'fac_w': rnd((DIM, DIM, 1, 1)), 'fac_b': rnd((DIM,), 0.01), 'fgm_w1': rnd((DIM, DIM, 1, 1)), 'fgm_b1': rnd((DIM,), 0.01), 'fgm_w2': rnd((DIM, DIM, 1, 1)), 'fgm_b2': rnd((DIM,), 0.01), 'fgm_alpha': rnd((DIM, 1, 1), 0.1), 'fgm_beta': jnp.ones((DIM, 1, 1), jnp.float32), 'fgm_boost': jnp.full((DIM, 1, 1), 0.5, jnp.float32), 'vis_w': rnd((1, DIM, 3, 3)), 'vis_b': rnd((1,), 0.01), 'base_weights': jnp.array([3.5, 3.5, 0.8, 0.1, 1.0], jnp.float32)}
    _L1_conv_all = _L1_conv_setup()
    _L1_conv_in = {k: v for k, v in _L1_conv_all.items() if k in ('in_w', 'in_b', 'out_w', 'out_b', 'dilh_w', 'dilv_w', 'pyr_w', 'pyr_b', 'fuse_w', 'fuse_b', 'dw11_w', 'dw11_b', 'cr_w', 'cr_b', 'batt_w1', 'batt_b1', 'batt_w2', 'batt_b2', 'conv_w', 'conv_b', 'fac_w', 'fac_b', 'fgm_w1', 'fgm_b1', 'fgm_w2', 'fgm_b2', 'fgm_alpha', 'fgm_beta', 'fgm_boost', 'vis_w', 'vis_b', 'base_weights')}
    del _L1_conv_all
    return {'x': x, 'L0_conv_ln1_g': _L0_conv_in['ln1_g'], 'L0_conv_ln1_b': _L0_conv_in['ln1_b'], 'L0_conv_qkv_w': _L0_conv_in['qkv_w'], 'L0_conv_qkv_b': _L0_conv_in['qkv_b'], 'L0_conv_proj_w': _L0_conv_in['proj_w'], 'L0_conv_proj_b': _L0_conv_in['proj_b'], 'L0_conv_rpb_table': _L0_conv_in['rpb_table'], 'L0_conv_ln2_g': _L0_conv_in['ln2_g'], 'L0_conv_ln2_b': _L0_conv_in['ln2_b'], 'L0_conv_w1': _L0_conv_in['w1'], 'L0_conv_b1': _L0_conv_in['b1'], 'L0_conv_w2': _L0_conv_in['w2'], 'L0_conv_b2': _L0_conv_in['b2'], 'L0_conv_rpi': _L0_conv_in['rpi'], 'L1_conv_in_w': _L1_conv_in['in_w'], 'L1_conv_in_b': _L1_conv_in['in_b'], 'L1_conv_out_w': _L1_conv_in['out_w'], 'L1_conv_out_b': _L1_conv_in['out_b'], 'L1_conv_dilh_w': _L1_conv_in['dilh_w'], 'L1_conv_dilv_w': _L1_conv_in['dilv_w'], 'L1_conv_pyr_w': _L1_conv_in['pyr_w'], 'L1_conv_pyr_b': _L1_conv_in['pyr_b'], 'L1_conv_fuse_w': _L1_conv_in['fuse_w'], 'L1_conv_fuse_b': _L1_conv_in['fuse_b'], 'L1_conv_dw11_w': _L1_conv_in['dw11_w'], 'L1_conv_dw11_b': _L1_conv_in['dw11_b'], 'L1_conv_cr_w': _L1_conv_in['cr_w'], 'L1_conv_cr_b': _L1_conv_in['cr_b'], 'L1_conv_batt_w1': _L1_conv_in['batt_w1'], 'L1_conv_batt_b1': _L1_conv_in['batt_b1'], 'L1_conv_batt_w2': _L1_conv_in['batt_w2'], 'L1_conv_batt_b2': _L1_conv_in['batt_b2'], 'L1_conv_conv_w': _L1_conv_in['conv_w'], 'L1_conv_conv_b': _L1_conv_in['conv_b'], 'L1_conv_fac_w': _L1_conv_in['fac_w'], 'L1_conv_fac_b': _L1_conv_in['fac_b'], 'L1_conv_fgm_w1': _L1_conv_in['fgm_w1'], 'L1_conv_fgm_b1': _L1_conv_in['fgm_b1'], 'L1_conv_fgm_w2': _L1_conv_in['fgm_w2'], 'L1_conv_fgm_b2': _L1_conv_in['fgm_b2'], 'L1_conv_fgm_alpha': _L1_conv_in['fgm_alpha'], 'L1_conv_fgm_beta': _L1_conv_in['fgm_beta'], 'L1_conv_fgm_boost': _L1_conv_in['fgm_boost'], 'L1_conv_vis_w': _L1_conv_in['vis_w'], 'L1_conv_vis_b': _L1_conv_in['vis_b'], 'L1_conv_base_weights': _L1_conv_in['base_weights']}

def reference(x, L0_conv_ln1_g, L0_conv_ln1_b, L0_conv_qkv_w, L0_conv_qkv_b, L0_conv_proj_w, L0_conv_proj_b, L0_conv_rpb_table, L0_conv_ln2_g, L0_conv_ln2_b, L0_conv_w1, L0_conv_b1, L0_conv_w2, L0_conv_b2, L0_conv_rpi, L1_conv_in_w, L1_conv_in_b, L1_conv_out_w, L1_conv_out_b, L1_conv_dilh_w, L1_conv_dilv_w, L1_conv_pyr_w, L1_conv_pyr_b, L1_conv_fuse_w, L1_conv_fuse_b, L1_conv_dw11_w, L1_conv_dw11_b, L1_conv_cr_w, L1_conv_cr_b, L1_conv_batt_w1, L1_conv_batt_b1, L1_conv_batt_w2, L1_conv_batt_b2, L1_conv_conv_w, L1_conv_conv_b, L1_conv_fac_w, L1_conv_fac_b, L1_conv_fgm_w1, L1_conv_fgm_b1, L1_conv_fgm_w2, L1_conv_fgm_b2, L1_conv_fgm_alpha, L1_conv_fgm_beta, L1_conv_fgm_boost, L1_conv_vis_w, L1_conv_vis_b, L1_conv_base_weights):
    import jax
    import jax.numpy as jnp

    def _L0_conv_ref(x, ln1_g, ln1_b, qkv_w, qkv_b, proj_w, proj_b, rpb_table, ln2_g, ln2_b, w1, b1, w2, b2, rpi):
        import jax, jax.numpy as jnp
        import numpy as np
        WS = 8
        C = 128
        NH = 8
        FF = 512
        EPS = 1e-05

        def _rel_pos_index(ws):
            coords = np.stack(np.meshgrid(np.arange(ws), np.arange(ws), indexing='ij')).reshape(2, -1)
            rel = (coords[:, :, None] - coords[:, None, :]).transpose(1, 2, 0)
            rel[:, :, 0] += ws - 1
            rel[:, :, 1] += ws - 1
            rel[:, :, 0] *= 2 * ws - 1
            return rel.sum(-1)

        def _ln(x, g, b):
            m = x.mean(-1, keepdims=True)
            v = jnp.var(x, axis=-1, keepdims=True)
            return (x - m) / jnp.sqrt(v + EPS) * g + b

        def _swin_block(tok, h, w, ln1_g, ln1_b, qkv_w, qkv_b, proj_w, proj_b, rpb_table, rpi, ln2_g, ln2_b, w1, b1, w2, b2):
            b = tok.shape[0]
            N = WS * WS
            hd = C // NH
            t = _ln(tok, ln1_g, ln1_b).reshape(b, h // WS, WS, w // WS, WS, C)
            t = t.transpose(0, 1, 3, 2, 4, 5).reshape(-1, N, C)
            qkv = (t @ qkv_w.T + qkv_b).reshape(-1, N, 3, NH, hd).transpose(2, 0, 3, 1, 4)
            q, k, v = (qkv[0], qkv[1], qkv[2])
            scale = hd ** (-0.5)
            attn = jnp.einsum('whnd,whmd->whnm', q * scale, k)
            bias = rpb_table[rpi].transpose(2, 0, 1)
            attn = jax.nn.softmax(attn + bias, axis=-1)
            out = jnp.einsum('whnm,whmd->whnd', attn, v).transpose(0, 2, 1, 3).reshape(-1, N, C)
            out = out @ proj_w.T + proj_b
            out = out.reshape(b, h // WS, w // WS, WS, WS, C).transpose(0, 1, 3, 2, 4, 5).reshape(b, h * w, C)
            tok = tok + out
            t2 = _ln(tok, ln2_g, ln2_b)
            t2 = jax.nn.gelu(t2 @ w1.T + b1, approximate=False) @ w2.T + b2
            return tok + t2
        b, c, h, w = x.shape
        tok = x.transpose(0, 2, 3, 1).reshape(b, h * w, c)
        tok = _swin_block(tok, h, w, ln1_g, ln1_b, qkv_w, qkv_b, proj_w, proj_b, rpb_table, rpi, ln2_g, ln2_b, w1, b1, w2, b2)
        return tok.reshape(b, h, w, c).transpose(0, 3, 1, 2)

    def _L1_conv_ref(x, in_w, in_b, out_w, out_b, dilh_w, dilv_w, pyr_w, pyr_b, fuse_w, fuse_b, dw11_w, dw11_b, cr_w, cr_b, batt_w1, batt_b1, batt_w2, batt_b2, conv_w, conv_b, fac_w, fac_b, fgm_w1, fgm_b1, fgm_w2, fgm_b2, fgm_alpha, fgm_beta, fgm_boost, vis_w, vis_b, base_weights):
        import jax, jax.numpy as jnp
        import numpy as np
        B, DIM, H, W = (8, 128, 32, 32)

        def conv2d(x, w, b=None, pad=(0, 0), dil=(1, 1), groups=1):
            out = jax.lax.conv_general_dilated(x, w, window_strides=(1, 1), padding=[(pad[0], pad[0]), (pad[1], pad[1])], rhs_dilation=dil, dimension_numbers=('NCHW', 'OIHW', 'NCHW'), feature_group_count=groups)
            return out if b is None else out + b[None, :, None, None]

        def gap(x):
            return jnp.mean(x, axis=(2, 3), keepdims=True)

        def _fgm(x, w1, b1, w2, b2, alpha, beta, boost):
            x1 = conv2d(x, w1, b1)
            x2 = conv2d(x, w2, b2)
            x2_fft = jnp.fft.fft2(x2)
            h, w = (x.shape[-2], x.shape[-1])
            fh = jnp.fft.fftfreq(h)[:, None]
            fw = jnp.fft.fftfreq(w)[None, :]
            mask = (jnp.sqrt(fh ** 2 + fw ** 2) > 0.3).astype(jnp.float32)[None, None]
            enhanced = x2_fft * (1.0 + boost[None] * mask)
            out = jnp.abs(jnp.fft.ifft2(x1 * enhanced))
            return out * alpha[None] + x * beta[None]

        def _forward(x, in_w, in_b, out_w, out_b, dilh_w, dilv_w, pyr_w, pyr_b, fuse_w, fuse_b, dw11_w, dw11_b, cr_w, cr_b, batt_w1, batt_b1, batt_w2, batt_b2, conv_w, conv_b, fac_w, fac_b, fgm_w1, fgm_b1, fgm_w2, fgm_b2, fgm_alpha, fgm_beta, fgm_boost, vis_w, vis_b, base_weights):
            dim = x.shape[1]
            out0 = jax.nn.gelu(conv2d(x, in_w, in_b), approximate=False)
            x_att = conv2d(gap(out0), fac_w, fac_b)
            x_fft = jnp.fft.fft2(out0) * x_att
            x_fca = jnp.abs(jnp.fft.ifft2(x_fft))
            x_att2 = conv2d(gap(x_fca), conv_w, conv_b)
            x_sca = x_att2 * x_fca
            x_sca = _fgm(x_sca, fgm_w1, fgm_b1, fgm_w2, fgm_b2, fgm_alpha, fgm_beta, fgm_boost)
            h_out = conv2d(out0, dilh_w, None, pad=(0, 33), dil=(1, 11), groups=dim)
            h_out = conv2d(h_out, cr_w[0], cr_b[0], pad=(1, 1), groups=dim)
            v_out = conv2d(out0, dilv_w, None, pad=(33, 0), dil=(11, 1), groups=dim)
            v_out = conv2d(v_out, cr_w[1], cr_b[1], pad=(1, 1), groups=dim)
            dils = (1, 6, 12, 20)
            feats = [conv2d(out0, pyr_w[i], pyr_b[i], pad=(d, d), dil=(d, d), groups=dim // 4) for i, d in enumerate(dils)]
            pyr = jnp.concatenate(feats, axis=1)
            pyr = conv2d(pyr, fuse_w, fuse_b, groups=dim)
            pyr = conv2d(pyr, cr_w[2], cr_b[2], pad=(1, 1), groups=dim)
            point = conv2d(out0, dw11_w, dw11_b, groups=dim)
            a = jax.nn.relu(conv2d(gap(out0), batt_w1, batt_b1))
            adaptive = jax.nn.sigmoid(conv2d(a, batt_w2, batt_b2))[:, :, 0, 0]
            edge = jax.nn.sigmoid(conv2d(out0, vis_w, vis_b, pad=(1, 1)))
            base = jax.nn.softmax(base_weights)
            comb = jax.nn.softmax(base[None] * adaptive, axis=1)
            cw = comb[:, :, None, None]
            out = x + cw[:, 0:1] * (1.0 + edge) * h_out + cw[:, 1:2] * (1.0 + edge) * v_out + cw[:, 2:3] * (1.0 - 0.3 * edge) * pyr + cw[:, 3:4] * point + cw[:, 4:5] * x_sca
            out = jax.nn.relu(out)
            return conv2d(out, out_w, out_b)
        return _forward(x, in_w, in_b, out_w, out_b, dilh_w, dilv_w, pyr_w, pyr_b, fuse_w, fuse_b, dw11_w, dw11_b, cr_w, cr_b, batt_w1, batt_b1, batt_w2, batt_b2, conv_w, conv_b, fac_w, fac_b, fgm_w1, fgm_b1, fgm_w2, fgm_b2, fgm_alpha, fgm_beta, fgm_boost, vis_w, vis_b, base_weights)

    def _gn(v, G=32, eps=1e-05):
        B_, C_, H_, W_ = v.shape
        g = v.reshape(B_, G, C_ // G, H_, W_)
        m = jnp.mean(g, axis=(2, 3, 4), keepdims=True)
        s = jnp.var(g, axis=(2, 3, 4), keepdims=True)
        return ((g - m) / jnp.sqrt(s + eps)).reshape(v.shape)

    def _ln_c(v, eps=1e-06):
        m = jnp.mean(v, axis=1, keepdims=True)
        s = jnp.var(v, axis=1, keepdims=True)
        return (v - m) / jnp.sqrt(s + eps)

    def _ln_t(v, eps=1e-05):
        m = jnp.mean(v, axis=-1, keepdims=True)
        s = jnp.var(v, axis=-1, keepdims=True)
        return (v - m) / jnp.sqrt(s + eps)

    def _to_tokens(v):
        B_, C_, H_, W_ = v.shape
        return v.reshape(B_, C_, H_ * W_).transpose(0, 2, 1)

    def _from_tokens(t, like):
        B_, C_, H_, W_ = like.shape
        return t.transpose(0, 2, 1).reshape(B_, C_, H_, W_)
    x = _L0_conv_ref(x, L0_conv_ln1_g, L0_conv_ln1_b, L0_conv_qkv_w, L0_conv_qkv_b, L0_conv_proj_w, L0_conv_proj_b, L0_conv_rpb_table, L0_conv_ln2_g, L0_conv_ln2_b, L0_conv_w1, L0_conv_b1, L0_conv_w2, L0_conv_b2, L0_conv_rpi)
    x = _L1_conv_ref(x, L1_conv_in_w, L1_conv_in_b, L1_conv_out_w, L1_conv_out_b, L1_conv_dilh_w, L1_conv_dilv_w, L1_conv_pyr_w, L1_conv_pyr_b, L1_conv_fuse_w, L1_conv_fuse_b, L1_conv_dw11_w, L1_conv_dw11_b, L1_conv_cr_w, L1_conv_cr_b, L1_conv_batt_w1, L1_conv_batt_b1, L1_conv_batt_w2, L1_conv_batt_b2, L1_conv_conv_w, L1_conv_conv_b, L1_conv_fac_w, L1_conv_fac_b, L1_conv_fgm_w1, L1_conv_fgm_b1, L1_conv_fgm_w2, L1_conv_fgm_b2, L1_conv_fgm_alpha, L1_conv_fgm_beta, L1_conv_fgm_boost, L1_conv_vis_w, L1_conv_vis_b, L1_conv_base_weights)
    return x

_drawn_inputs = setup_inputs


def setup_inputs(seed=0):
    import zlib

    import numpy as np

    out = dict(_drawn_inputs(seed))
    spreads = {'L0_conv_ln1_g': (1.0, 0.6),
     'L0_conv_ln1_b': (0.0, 0.8),
     'L0_conv_qkv_b': (0.0, 0.314),
     'L0_conv_proj_b': (0.0, 0.1),
     'L0_conv_ln2_g': (1.0, 0.6),
     'L0_conv_ln2_b': (0.0, 0.8),
     'L0_conv_b1': (0.0, 0.333),
     'L0_conv_b2': (0.0, 0.1),
     'L1_conv_fgm_beta': (1.0, 0.6),
     'L1_conv_fgm_boost': (0.5, 0.6)}
    factors = {'L0_conv_qkv_w': 6.69,
     'L0_conv_rpb_table': 8.0,
     'L1_conv_in_w': 8.0,
     'L1_conv_in_b': 8.0,
     'L1_conv_dilh_w': 64.0,
     'L1_conv_dilv_w': 64.0,
     'L1_conv_pyr_w': 64.0,
     'L1_conv_pyr_b': 64.0,
     'L1_conv_fuse_w': 64.0,
     'L1_conv_fuse_b': 64.0,
     'L1_conv_dw11_w': 64.0,
     'L1_conv_dw11_b': 200.0,
     'L1_conv_cr_w': 64.0,
     'L1_conv_cr_b': 200.0,
     'L1_conv_batt_w1': 8.0,
     'L1_conv_batt_b1': 174.424,
     'L1_conv_batt_w2': 57.305,
     'L1_conv_batt_b2': 200.0,
     'L1_conv_conv_w': 8.0,
     'L1_conv_conv_b': 8.0,
     'L1_conv_fac_w': 8.0,
     'L1_conv_fac_b': 8.0,
     'L1_conv_fgm_w1': 8.0,
     'L1_conv_fgm_b1': 64.0,
     'L1_conv_fgm_w2': 8.0,
     'L1_conv_fgm_b2': 64.0,
     'L1_conv_fgm_alpha': 8.0,
     'L1_conv_vis_w': 64.0,
     'L1_conv_base_weights': 8.0,
     'L1_conv_out_b': 8.0}
    for name, (base, spread) in spreads.items():
        noise = np.random.default_rng([zlib.crc32(name.encode()), seed]).standard_normal(out[name].shape)
        drawn = base * np.exp(spread * noise) if base else spread * noise
        out[name] = jnp.asarray(drawn.astype(out[name].dtype))
    for name, factor in factors.items():
        out[name] = (out[name] * factor).astype(out[name].dtype)
    return out
```

```python
from contextlib import ExitStack

import numpy as np
import concourse.bass as bass
from concourse import mybir

F32 = mybir.dt.float32
I32 = mybir.dt.int32
ALU = mybir.AluOpType
ACT = mybir.ActivationFunctionType
AX = mybir.AxisListType

IMAGES, C, SIDE = 16, 128, 32
TOK = SIDE * SIDE
P = 128
CH = TOK // P
HALF = TOK // 2
WS, HEADS = 8, 8
WT = WS * WS
HD = C // HEADS
WIN = TOK // WT
PAIRS = WIN // 2
HP = HEADS // 2
FF = 512
FC = FF // P
LN_EPS = 1e-5
DILS = (1, 6, 12, 20)
PAD = max(DILS)
SP = SIDE + 2 * PAD
S1 = SIDE + 2
AXIS_DIL, AXIS_TAPS = 11, 7
REL = (2 * WS - 1) ** 2
BATT = C // 8
ROUTES = 5


def layout(*entries):
    at, where = 0, {}
    for name, width in entries:
        where[name] = (at, width)
        at += width
    return where, at


COLS, NCOLS = layout(
    ("ln1_g", 1), ("ln1_b", 1), ("q_b", 1), ("k_b", 1), ("v_b", 1), ("ln2_g", 1), ("ln2_b", 1),
    ("b1", FC), ("b2", 1), ("in_b", 1), ("out_b", 1), ("fac_b", 1), ("conv_b", 1), ("alpha", 1),
    ("beta", 1), ("fuse_w", 1), ("fuse_b", 1), ("dw_w", 1), ("dw_b", 1), ("pyr_b", 1), ("vis_b", 1),
    ("batt_b1", 1), ("dilh", AXIS_TAPS), ("dilv", AXIS_TAPS), ("cr_w", 27), ("cr_b", 3))
ROWS, NROWS = layout(("proj_b", C), ("fgm_b1", C), ("fgm_b2", C), ("boost", C), ("batt_b2", ROUTES),
                     ("base", ROUTES))
MATS, NMATS = layout(
    ("qkv", 3 * C), ("proj", C), ("w1", FF), ("w2", FF), ("in", C), ("out", C), ("fac", C),
    ("conv", C), ("fgm1", C), ("fgm2", C), ("vis", 9), ("batt1", BATT), ("batt2", ROUTES),
    ("pyr", len(DILS) * 9 * 32), ("table", 2 * HEADS))
CONS, NCONS = layout(
    ("ident", P), ("sel", 4 * P), ("dft_h", P), ("dft_w0", P), ("dft_w", P), ("even0", P),
    ("even", P), ("odd0", P), ("odd", P), ("idft_h", P), ("head_mask", HEADS), ("high", CH), ("iota", 2))


def shape_constants():
    n = SIDE
    ang = 2 * np.pi * np.outer(np.arange(n), np.arange(n)) / n
    cos, sin = np.cos(ang), np.sin(ang)
    pack = np.zeros((n, n))
    pack[:, 0], pack[:, 1] = 1, cos[:, 16]
    pack[:, 2::2], pack[:, 3::2] = cos[:, 1:16], -sin[:, 1:16]
    unpack = np.zeros((n, n))
    unpack[0], unpack[1] = 1, cos[16]
    unpack[2::2], unpack[3::2] = 2 * cos[1:16], -2 * sin[1:16]
    unpack /= n
    full = np.block([[cos, -sin], [sin, cos]])
    inv = np.block([[cos, sin], [-sin, cos]]) / n

    def diag(*blocks):
        size = sum(len(b) for b in blocks)
        out, at = np.zeros((size, size)), 0
        for b in blocks:
            out[at:at + len(b), at:at + len(b)] = b
            at += len(b)
        return out

    inv_odd = np.concatenate([-inv[n:], inv[:n]])
    unpack_odd = np.zeros((n, n))
    unpack_odd[2::2], unpack_odd[3::2] = -unpack[3::2], unpack[2::2]
    c = np.zeros((P, NCONS))

    def put(name, value):
        at, width = CONS[name]
        c[:, at:at + width] = value

    put("ident", np.eye(P))
    sel = np.zeros((P, 4, P))
    for q in range(4):
        sel[32 * q, q] = 1
    put("sel", sel.reshape(P, -1))
    put("dft_h", diag(pack, pack, pack, pack))
    put("dft_w0", diag(pack, pack, full))
    put("dft_w", diag(full, full))
    put("even0", 0.5 * diag(unpack, unpack, inv))
    put("even", 0.5 * diag(inv, inv))
    put("odd0", 0.5 * diag(unpack_odd, unpack_odd, inv_odd))
    put("odd", 0.5 * diag(inv_odd, inv_odd))
    idft = diag(unpack, unpack, unpack, unpack).reshape(P, 4, n)
    put("idft_h", idft.transpose(0, 2, 1).reshape(P, P))
    put("head_mask", np.arange(P)[:, None] // HD == np.arange(HEADS)[None])
    freq = np.minimum(np.arange(n), n - np.arange(n)) / n
    packed_k = np.array([0, 16] + [k for k in range(1, 16) for _ in range(2)])
    high = np.zeros((CH, 2, 2, n))
    for g in range(CH):
        for s in range(2):
            for r in range(2):
                kh = 2 * g + s
                kw = np.arange(n)
                if kh == 0:
                    kh, kw = 16 * r, packed_k
                high[g, s, r] = np.sqrt(freq[kh] ** 2 + freq[kw] ** 2) > 0.3
    put("high", high.reshape(CH, P).T)
    put("iota", np.stack([np.arange(P), np.arange(P) + P], 1))
    return c.astype(np.float32)


def swin_conv_kernel(nc, x, cols, rows, mats, cons, rel_index, out):
    with ExitStack() as ctx:
        def sb(name, *free, dt=F32):
            return ctx.enter_context(nc.sbuf_tensor(name, [P, *free], dt))

        def sem(name):
            return ctx.enter_context(nc.semaphore(name))

        cons_sb, cols_sb, mats_sb = sb("cons_sb", NCONS), sb("cols_sb", NCOLS), sb("mats_sb", NMATS)
        rows_sb = sb("rows_sb", NROWS)

        def con(name):
            at, width = CONS[name]
            return cons_sb[:, at:at + width]

        def col(name, k=0):
            return cols_sb[:, COLS[name][0] + k:COLS[name][0] + k + 1]

        def row(name):
            at, width = ROWS[name]
            return rows_sb[:, at:at + width]

        def mat(name):
            at, width = MATS[name]
            return mats_sb[:, at:at + width]

        ident = con("ident")
        w_qkv, w_proj, w_up, w_down = mat("qkv"), mat("proj"), mat("w1"), mat("w2")
        w_pyr = mat("pyr").rearrange("p (d t o) -> p d t o", d=len(DILS), t=9)
        ones = sb("ones", P)
        eps = sb("eps", 1)
        fold_b = sb("fold_b", 3 + FC)
        fuse_bias = sb("fuse_bias", 1)
        w_vis = sb("w_vis", 9, 32)
        proj_shift = sb("proj_shift", P)
        two_b1 = sb("two_b1", P)
        rel_bias = sb("rel_bias", HEADS * WT)
        boost = sb("boost", CH, C)
        base = sb("base", ROUTES)
        dc_b2 = sb("dc_b2", P)
        tiny = sb("tiny", 8)

        x_in = sb("x_in", TOK)
        xw = sb("xw", TOK)
        attn_out = xw
        xT = sb("xT", CH, C)
        x1T = xT
        resT = sb("resT", CH, C)
        nT = sb("nT", CH, C)
        nC = sb("nC", TOK)
        qC, kC = sb("qC", TOK), sb("kC", TOK)
        k_heads = sb("k_heads", WIN, HEADS, WT)
        hidden = k_heads[:, 0:8].rearrange("p a h k -> p (a h k)").rearrange("p (f t) -> p f t", f=FC)
        v_pair = sb("v_pair", WIN, HP, 2, HD)
        score = sb("score", 2, HEADS, WT)
        prob = sb("prob", 2, HEADS * WT)
        probT = sb("probT", 2, HP, P)
        stats, mv = sb("stats", CH, 6), sb("mv", CH, 2)
        std, rstd = sb("std", CH), sb("rstd", CH)
        row_max, row_sum, row_inv = sb("row_max", 2, HEADS), sb("row_sum", 2, HEADS), sb("row_inv", 2, HEADS)
        xm = sb("xm", TOK)
        act = sb("act", SP, SP)
        hor, ver, pyr = sb("hor", S1, S1), sb("ver", S1, S1), sb("pyr", S1, S1)
        hv, py = sb("hv", SIDE, SIDE), sb("py", SIDE, SIDE)
        xs = sb("xs", TOK)
        xe, xo = sb("xe", TOK), sb("xo", TOK)
        fft = sb("fft", 4, TOK)
        fa, fb, fc, fd = (fft[:, k] for k in range(4))
        relu = fb
        edge_half, edge = sb("edge_half", 256), sb("edge", SIDE, SIDE)
        gated = sb("gated", SIDE, SIDE)
        y_out = sb("y_out", TOK)
        sums = sb("sums", 4)
        vec = sb("vec", 16)
        batt_wide = sb("batt_wide", P)
        route = sb("route", 4, ROUTES)
        cr_scaled = sb("cr_scaled", 3, 9)
        cr_bias = sb("cr_bias", 3)
        mix = sb("mix", 8)

        bank = [ctx.enter_context(nc.psum_tensor(f"bank{i}", [P, HALF], F32)) for i in range(8)]

        loaded = sem("loaded")
        weights_raw_used = sem("weights_raw_used")
        fold_ps = sem("fold_ps")
        folded = sem("folded")
        v_wide_ready = sem("v_wide_ready")
        shift_ps = sem("shift_ps")
        setup_exp = sem("setup_exp")
        setup_z = sem("setup_z")
        zeroed = sem("zeroed")
        onehot_ready = sem("onehot_ready")
        onehot_used = sem("onehot_used")
        rel_ps = sem("rel_ps")
        setup_dve = sem("setup_dve")
        x_loaded = sem("x_loaded")
        stored = sem("stored")
        pool_turns = sem("pool_turns")
        xw_ready = sem("xw_ready")
        xT_ps = sem("xT_ps")
        xT_sb = sem("xT_sb")
        ln1_var = sem("ln1_var")
        ln1_std = sem("ln1_std")
        nT_sb = sem("nT_sb")
        res_sb = sem("res_sb")
        nT_ps = sem("nT_ps")
        nC_sb = sem("nC_sb")
        q_ps = sem("q_ps")
        k_ps = sem("k_ps")
        q_sb = sem("q_sb")
        k_sb = sem("k_sb")
        kh_sb = sem("kh_sb")
        v_ps = sem("v_ps")
        v_sb = sem("v_sb")
        s_ps = sem("s_ps")
        s_biased = sem("s_biased")
        s_max = sem("s_max")
        s_sub = sem("s_sub")
        s_exp = sem("s_exp")
        s_inv = sem("s_inv")
        p_sb = sem("p_sb")
        pT_ps = sem("pT_ps")
        pT_sb = sem("pT_sb")
        o_ps = sem("o_ps")
        o_sb = sem("o_sb")
        proj_ps = sem("proj_ps")
        x1_sb = sem("x1_sb")
        ln2_var = sem("ln2_var")
        ln2_std = sem("ln2_std")
        n2T_sb = sem("n2T_sb")
        n2T_ps = sem("n2T_ps")
        n2C_sb = sem("n2C_sb")
        up_ps = sem("up_ps")
        up_sb = sem("up_sb")
        down_ps = sem("down_ps")
        xm_sb = sem("xm_sb")
        in_ps = sem("in_ps")
        act_sb = sem("act_sb")
        abs_sb = sem("abs_sb")
        gap_sb = sem("gap_sb")
        gap_ps = sem("gap_ps")
        mid_sb = sem("mid_sb")
        mid_ps = sem("mid_ps")
        route_z = sem("route_z")
        route_e = sem("route_e")
        route_d = sem("route_d")
        route_f = sem("route_f")
        cw_sb = sem("cw_sb")
        xs_sb = sem("xs_sb")
        edge_ps = sem("edge_ps")
        edge_sig = sem("edge_sig")
        eb_ps = sem("eb_ps")
        edge_sb = sem("edge_sb")
        pyr_ps = sem("pyr_ps")
        pyr_sb = sem("pyr_sb")
        xe_sb = sem("xe_sb")
        xo_sb = sem("xo_sb")
        x2_ps = sem("x2_ps")
        x2_sb = sem("x2_sb")
        h_ps = sem("h_ps")
        h_sb = sem("h_sb")
        t_ps = sem("t_ps")
        t_sb = sem("t_sb")
        r1_ps = sem("r1_ps")
        r1_sb = sem("r1_sb")
        w_ps = sem("w_ps")
        w_sb = sem("w_sb")
        r2_ps = sem("r2_ps")
        ge_sb = sem("ge_sb")
        go_sb = sem("go_sb")
        axis_sb = sem("axis_sb")
        base_sb = sem("base_sb")
        ae_ps = sem("ae_ps")
        ae_sb = sem("ae_sb")
        ao_ps = sem("ao_ps")
        ao_sb = sem("ao_sb")
        te_ps = sem("te_ps")
        te_sb = sem("te_sb")
        to_ps = sem("to_ps")
        to_sb = sem("to_sb")
        be_ps = sem("be_ps")
        be_sb = sem("be_sb")
        bo_ps = sem("bo_ps")
        bo_sb = sem("bo_sb")
        sq_sb = sem("sq_sb")
        mag_sb = sem("mag_sb")
        hv_sb = sem("hv_sb")
        py_sb = sem("py_sb")
        gated_sb = sem("gated_sb")
        mixed_sb = sem("mixed_sb")
        relu_sb = sem("relu_sb")
        out_ps = sem("out_ps")
        out_sb = sem("out_sb")

        def grid(ap):
            return ap.rearrange("p (h w) -> p h w", w=SIDE)

        def natural_windows(ap, a):
            return ap.rearrange("p (a r b s) -> p a b r s", a=4, r=WS, b=4)[:, a]

        def windows(ap, a):
            return ap[:, 256 * a:256 * a + 256].rearrange("p (b r s) -> p b r s", b=4, r=WS)

        xs_hw = xs.rearrange("p (w h) -> p h w", w=SIDE)
        act_in = act[:, PAD:PAD + SIDE, PAD:PAD + SIDE]

        block = ctx.enter_context(nc.Block())
        LOADS = 5

        @block.sync
        def _(sp):
            sp.dma_start(cons_sb[:], cons).then_inc(loaded, 16)
            sp.dma_start(mats_sb[:], mats).then_inc(loaded, 16)
            sp.dma_start(cols_sb[:], cols).then_inc(loaded, 16)
            sp.dma_start(rows_sb[:], rows.broadcast_to([P, NROWS])).then_inc(loaded, 16)
            sp.dma_start(k_heads[:, 0:8].rearrange("p a h k -> p (a h k)").bitcast(I32),
                         rel_index.broadcast_to([P, WT * WT])).then_inc(loaded, 16)
            sp.dma_start(x_in[:], x[0]).then_inc(x_loaded, 16)

            def load(i):
                sp.wait_ge(xw_ready, i)
                sp.dma_start(x_in[:], x[i]).then_inc(x_loaded, 16)

            def store(n):
                sp.wait_ge(out_sb, 2 * n + 2)
                sp.dma_start(out[n], y_out[:]).then_inc(stored, 16)

            load(1)
            with sp.Fori(0, IMAGES - 2) as n:
                load(n + 2)
                store(n)
            store(IMAGES - 2)
            store(IMAGES - 1)
            sp.wait_ge(stored, 16 * IMAGES)

        @block.tensor
        def _(pe):
            pe.wait_ge(loaded, 16 * LOADS)
            for k in range(3):
                pe.matmul(bank[0][:, k:k + 1], w_qkv[:, k * C:(k + 1) * C], col("ln1_b"), start=True, stop=True)
            for f in range(FC):
                last = pe.matmul(bank[0][:, 3 + f:4 + f], w_up[:, f * P:(f + 1) * P], col("ln2_b"),
                                 start=True, stop=True)
            last.then_inc(fold_ps, 1)
            pe.wait_ge(v_wide_ready, 1)
            pe.matmul(bank[1][:, 0:P], y_out[:, 0:P], w_proj, start=True, stop=True).then_inc(shift_ps, 1)
            table = mat("table").rearrange("p (c h) -> p c h", c=2)
            oh = [k_heads[:, 8:16].rearrange("p a h k -> p (a h k)"), fft[:].rearrange("p a t -> p (a t)")]
            rel_bank = bank[2].rearrange("p (h k) -> p h k", h=HEADS)
            pe.wait_ge(onehot_ready, 2)
            for key in range(WT):
                for w in range(2):
                    for c in range(2):
                        last = pe.matmul(rel_bank[64 * w:64 * w + 64, :, key], oh[c][:, key * WT:(key + 1) * WT],
                                         table[:, c], start=(c == 0), stop=(c == 1))
            last.then_inc(rel_ps, 1)
            pe.wait_ge(setup_dve, 1)

            def turn4(dst, src, k):
                for c in range(4):
                    at = (4 * k + c) * P
                    last = pe.transpose(dst[:, c * P:(c + 1) * P], src[:, at:at + P], ident)
                return last

            def multiply4(dst, src, k, weights, first=None):
                for c in range(4):
                    at = (4 * k + c) * P
                    rhs = first if first is not None and at == 0 else weights
                    last = pe.matmul(dst[:, c * P:(c + 1) * P], src[:, at:at + P], rhs, start=True, stop=True)
                return last

            nT_flat = nT[:].rearrange("p c d -> p (c d)")

            def x_transposes(i):
                pe.wait_ge(xw_ready, i + 1)
                pe.wait_ge(up_sb, 8 * i)
                pe.wait_ge(xm_sb, 2 * i)
                for k in range(2):
                    turn4(bank[k], xw, k).then_inc(xT_ps, 1)

            def n_transposes(i):
                for k in range(2):
                    pe.wait_ge(nT_sb, 2 * i + k + 1)
                    turn4(bank[2 + k], nT_flat, k).then_inc(nT_ps, 1)

            def queries_keys(i):
                for k in range(2):
                    pe.wait_ge(xT_sb, 2 * i + k + 1)
                    pe.wait_ge(nC_sb, 2 * i + k + 1)
                    pe.matmul(bank[k][:], w_qkv[:, 0:C], nC[:, HALF * k:HALF * k + HALF],
                              start=True, stop=True).then_inc(q_ps, 1)
                for k in range(2):
                    pe.matmul(bank[2 + k][:], w_qkv[:, C:2 * C], nC[:, HALF * k:HALF * k + HALF],
                              start=True, stop=True).then_inc(k_ps, 1)

            def v(i):
                wv = w_qkv[:, 2 * C:3 * C].rearrange("p (g e d) -> p e g d", g=HP, e=2)
                for k in range(2):
                    pe.wait_ge(q_sb, 2 * i + k + 1)
                    for w in range(8):
                        t = nC[:, (8 * k + w) * WT:(8 * k + w + 1) * WT]
                        for e in range(2):
                            last = pe.matmul(bank[k][64 * e:64 * e + 64, w * 64:w * 64 + 64], t, wv[:, e],
                                             start=True, stop=True)
                    last.then_inc(v_ps, 1)

            def scores(i, j):
                if j == 0:
                    pe.wait_ge(kh_sb, i + 1)
                    pe.wait_ge(q_sb, 2 * i + 2)
                if j < 2:
                    pe.wait_ge(k_sb, 2 * i + j + 1)
                else:
                    pe.wait_ge(s_biased, 8 * i + j - 1)
                for e in range(2):
                    w = 2 * j + e
                    last = pe.matmul(bank[2 + j % 2][64 * e:64 * e + 64, :], qC[:, w * WT:(w + 1) * WT],
                                     k_heads[:, w].rearrange("p h k -> p (h k)"), start=True, stop=True)
                last.then_inc(s_ps, 1)

            def prob_transposes(i, j):
                pe.wait_ge(p_sb, 8 * i + j + 1)
                if j == 0:
                    pe.wait_ge(v_sb, 2 * i + 2)
                else:
                    pe.wait_ge(pT_sb, 8 * i + j)
                for g in range(HP):
                    last = pe.transpose(bank[0][:, g * P:(g + 1) * P], prob[:, j % 2, g * P:(g + 1) * P], ident)
                last.then_inc(pT_ps, 1)

            def values(i, j):
                pe.wait_ge(pT_sb, 8 * i + j + 1)
                if j == 4:
                    pe.wait_ge(o_sb, 2 * i + 1)
                for e in range(2):
                    w = 2 * j + e
                    for g in range(HP):
                        last = pe.matmul(bank[1][32 * g:32 * g + 32, (w % 8) * WT:(w % 8 + 1) * WT],
                                         v_pair[:, w, g].rearrange("p e d -> p (e d)"),
                                         probT[:, j % 2, g, e * WT:(e + 1) * WT], start=True, stop=True)
                last.then_inc(o_ps, 1)

            def project(i):
                for k in range(2):
                    pe.wait_ge(o_sb, 2 * i + k + 1)
                    pe.wait_ge(s_biased, 8 * i + 7 + k)
                    multiply4(bank[2 + k], attn_out, k, w_proj).then_inc(proj_ps, 1)

            def n2_transposes(i):
                for k in range(2):
                    pe.wait_ge(n2T_sb, 2 * i + k + 1)
                    pe.wait_ge(pT_sb, 8 * i + 8)
                    turn4(bank[k], nT_flat, k).then_inc(n2T_ps, 1)

            def mlp(i):
                def up(t):
                    k, f = divmod(t, FC)
                    b = (2, 3, 0, 1, 2, 3, 1, 2)[t]
                    if t < 2:
                        pe.wait_ge(x1_sb, 2 * i + t + 1)
                    elif t < 4:
                        pe.wait_ge(n2C_sb, 2 * i + t - 1)
                    else:
                        pe.wait_ge(up_sb, 8 * i + (1, 2, 4, 5)[t - 4])
                    pe.wait_ge(n2C_sb, 2 * i + k + 1)
                    pe.matmul(bank[b][:], w_up[:, f * P:(f + 1) * P], nC[:, HALF * k:HALF * k + HALF],
                              start=True, stop=True).then_inc(up_ps, 1)

                def down(k):
                    b = (0, 3)[k]
                    pe.wait_ge(up_sb, 8 * i + 4 + 4 * k)
                    for c in range(4):
                        pe.matmul(bank[b][:, c * P:(c + 1) * P], x1T[:, 4 * k + c], ident, is_transpose=True,
                                  start=(c == 0), stop=False)
                    for f in range(FC):
                        last = pe.matmul(bank[b][:], w_down[:, f * P:(f + 1) * P],
                                         hidden[:, f, HALF * k:HALF * k + HALF], start=False, stop=(f == FC - 1))
                    last.then_inc(down_ps, 1)

                for t in range(6):
                    up(t)
                down(0)
                up(6)
                up(7)
                down(1)

            def in_conv(n):
                for k in range(2):
                    pe.wait_ge(xm_sb, 2 * n + k + 1)
                    pe.wait_ge(out_sb, 2 * n)
                    pe.matmul(bank[4 + k][:], mat("in"), xm[:, HALF * k:HALF * k + HALF],
                              start=True, stop=True).then_inc(in_ps, 1)

            def tap(rows0, nrows, dil, t):
                y, x_ = rows0 + PAD + (t // 3 - 1) * dil, PAD + (t % 3 - 1) * dil
                return act[:, y:y + nrows, x_:x_ + SIDE]

            def edge_conv(n):
                pe.wait_ge(act_sb, 2 * n + 2)
                pe.wait_ge(bo_sb, 2 * n)
                for t in range(9):
                    for q in range(4):
                        last = pe.matmul(bank[7][32 * q:32 * q + 32, 0:256], w_vis[:, t], tap(8 * q, 8, 1, t),
                                         start=(t == 0), stop=(t == 8))
                last.then_inc(edge_ps, 1)

            def gap_products(n):
                pe.wait_ge(gap_sb, n + 1)
                pe.matmul(bank[6][:, 0:1], mat("fac"), vec[:, 0:1], start=True, stop=True)
                pe.matmul(bank[6][0:BATT, 1:2], mat("batt1"), vec[:, 0:1], start=True, stop=True)\
                  .then_inc(gap_ps, 1)

            def mid_products(n):
                pe.wait_ge(mid_sb, n + 1)
                pe.matmul(bank[6][:, 2:3], mat("conv"), vec[:, 5:6], start=True, stop=True)
                pe.matmul(bank[6][:, 8:8 + ROUTES], batt_wide[0:BATT, :], mat("batt2")[0:BATT], start=True,
                          stop=True).then_inc(mid_ps, 1)

            def edge_spread(n):
                sel = con("sel").rearrange("p (q m) -> p q m", q=4)
                pe.wait_ge(edge_sig, n + 1)
                for k in range(2):
                    pe.wait_ge(act_sb, 2 * n + 2)
                    for q in range(2):
                        last = pe.matmul(bank[4 + k][:, 256 * q:256 * q + 256], sel[:, 2 * k + q], edge_half[:],
                                         start=True, stop=True)
                    last.then_inc(eb_ps, 1)

            def pyramid(n, k):
                if k == 0:
                    pe.wait_ge(xs_sb, n + 1)
                    pe.wait_ge(route_z, n + 1)
                else:
                    pe.wait_ge(edge_sig, n + 1)
                for t in range(9):
                    for d, dil in enumerate(DILS):
                        last = pe.matmul(bank[6 + k][32 * d:32 * d + 32, :], w_pyr[:, d, t], tap(16 * k, 16, dil, t),
                                         start=(t == 0), stop=(t == 8))
                last.then_inc(pyr_ps, 1)

            def x2_conv(n):
                for k in range(2):
                    pe.wait_ge(edge_sb, 2 * n + k + 1)
                    pe.wait_ge(xs_sb, n + 1)
                    multiply4(bank[4 + k], xs, k, mat("fgm2")).then_inc(x2_ps, 1)

            def dft_rows(n):
                for k in range(2):
                    pe.wait_ge(x2_sb, 2 * n + k + 1)
                    pe.wait_ge(pyr_sb, 2 * n + k + 1)
                    multiply4(bank[6 + k], fa, k, con("dft_h")).then_inc(h_ps, 1)

            def turn_spectrum(n):
                for k in range(2):
                    pe.wait_ge(h_sb, 2 * n + 2)
                    turn4(bank[4 + k], fb, k).then_inc(t_ps, 1)

            def r_even(n):
                for k in range(2):
                    pe.wait_ge(xe_sb, n + 1)
                    pe.wait_ge(h_sb, 2 * n + k + 1)
                    multiply4(bank[6 + k], xe, k, mat("fgm1")).then_inc(r1_ps, 1)

            def dft_columns(n):
                for k in range(2):
                    pe.wait_ge(t_sb, 2 * n + k + 1)
                    if k == 0:
                        pe.matmul(bank[4][:, 0:P], con("dft_w0"), fa[:, 0:P], start=True, stop=True)
                        last = pe.matmul(bank[4][:, P:4 * P], con("dft_w"), fa[:, P:4 * P], start=True, stop=True)
                    else:
                        last = pe.matmul(bank[5][:], con("dft_w"), fa[:, 4 * P:8 * P], start=True, stop=True)
                    last.then_inc(w_ps, 1)

            def r_odd(n):
                for k in range(2):
                    pe.wait_ge(xo_sb, n + 1)
                    pe.wait_ge(r1_sb, 2 * n + k + 1)
                    multiply4(bank[6 + k], xo, k, mat("fgm1")).then_inc(r2_ps, 1)

            def inverse_even(n):
                for k in range(2):
                    pe.wait_ge(ge_sb, n + 1)
                    pe.wait_ge(w_sb, 2 * n + 2)
                    multiply4(bank[4 + k], fc, k, con("even"), con("even0")).then_inc(ae_ps, 1)

            def inverse_odd(n):
                for k in range(2):
                    pe.wait_ge(go_sb, 2 * n + k + 1)
                    multiply4(bank[6 + k], fd, k, con("odd"), con("odd0")).then_inc(ao_ps, 1)

            def turn_even(n):
                for k in range(2):
                    pe.wait_ge(ae_sb, 2 * n + 2)
                    turn4(bank[4 + k], fa, k).then_inc(te_ps, 1)

            def turn_odd(n):
                for k in range(2):
                    pe.wait_ge(ao_sb, 2 * n + 2)
                    turn4(bank[6 + k], fb, k).then_inc(to_ps, 1)

            def last_even(n):
                for k in range(2):
                    pe.wait_ge(te_sb, 2 * n + k + 1)
                    multiply4(bank[4 + k], fc, k, con("idft_h")).then_inc(be_ps, 1)

            def last_odd(n):
                for k in range(2):
                    pe.wait_ge(to_sb, 2 * n + k + 1)
                    multiply4(bank[6 + k], fd, k, con("idft_h")).then_inc(bo_ps, 1)

            def out_conv(n):
                for k in range(2):
                    pe.wait_ge(relu_sb, n + 1)
                    pe.wait_ge(be_sb, 2 * n + k + 1)
                    pe.matmul(bank[4 + k][:], mat("out"), relu[:, HALF * k:HALF * k + HALF],
                              start=True, stop=True).then_inc(out_ps, 1)

            def conv_early(n, j):
                if j == 0:
                    pyramid(n, 0)
                elif j == 1:
                    pyramid(n, 1)
                elif j == 2:
                    dft_rows(n)
                elif j == 3:
                    r_even(n)
                elif j == 4:
                    r_odd(n)
                elif j == 5:
                    inverse_odd(n)
                elif j == 6:
                    turn_odd(n)
                elif j == 7:
                    last_odd(n)

            def conv_late(n, j):
                if j == 1:
                    x2_conv(n)
                elif j == 2:
                    turn_spectrum(n)
                elif j == 3:
                    dft_columns(n)
                elif j == 4:
                    inverse_even(n)
                elif j == 5:
                    turn_even(n)
                elif j == 6:
                    last_even(n)

            def swin_only(i):
                x_transposes(i)
                n_transposes(i)
                queries_keys(i)
                v(i)
                scores(i, 0)
                scores(i, 1)
                for j in range(PAIRS):
                    prob_transposes(i, j)
                    if j + 2 < PAIRS:
                        scores(i, j + 2)
                    values(i, j)
                project(i)
                n2_transposes(i)
                mlp(i)

            def both(n, i):
                in_conv(n)
                x_transposes(i)
                edge_conv(n)
                gap_products(n)
                n_transposes(i)
                mid_products(n)
                queries_keys(i)
                edge_spread(n)
                v(i)
                scores(i, 0)
                scores(i, 1)
                for j in range(PAIRS):
                    conv_early(n, j)
                    prob_transposes(i, j)
                    if j + 2 < PAIRS:
                        scores(i, j + 2)
                    conv_late(n, j)
                    values(i, j)
                project(i)
                n2_transposes(i)
                mlp(i)
                out_conv(n)

            def conv_only(n):
                in_conv(n)
                edge_conv(n)
                gap_products(n)
                mid_products(n)
                edge_spread(n)
                for j in range(PAIRS):
                    conv_early(n, j)
                    conv_late(n, j)
                out_conv(n)

            swin_only(0)
            with pe.Fori(0, IMAGES - 1) as n:
                both(n, n + 1)
            conv_only(IMAGES - 1)

        @block.vector
        def _(dve):
            dve.memset(ones[:], 1.0)
            dve.memset(eps[:], LN_EPS)
            dve.memset(y_out[:, P:2 * P], 0.0)
            dve.wait_ge(loaded, 16 * LOADS)
            index = k_heads[:, 0:8].rearrange("p a h k -> p (a h k)").bitcast(I32)
            oh = [k_heads[:, 8:16].rearrange("p a h k -> p (a h k)"), fft[:].rearrange("p a t -> p (a t)")]
            for c in range(2):
                at = CONS["iota"][0] + c
                dve.tensor_scalar(oh[c], index, cons_sb[:, at:at + 1], None, ALU.is_equal)\
                   .then_inc(onehot_ready, 1)
            dve.tensor_copy(w_vis[:], mat("vis").unsqueeze(2).broadcast_to([P, 9, 32]))
            dve.tensor_scalar(fuse_bias[:], col("pyr_b"), col("fuse_w"), col("fuse_b"), ALU.mult, ALU.add)
            dve.tensor_scalar(two_b1[:], row("fgm_b1"), 2.0, None, ALU.mult)
            dve.tensor_scalar(dc_b2[:], row("fgm_b2"), float(TOK), None, ALU.mult)
            for g in range(CH):
                at = CONS["high"][0] + g
                dve.tensor_scalar(boost[:, g], row("boost"), cons_sb[:, at:at + 1], 1.0, ALU.mult, ALU.add)
            dve.tensor_reduce(tiny[:, 0:1], row("base"), AX.X, ALU.max)
            dve.drain()
            dve.tensor_scalar(base[:], row("base"), tiny[:, 0:1], None, ALU.subtract).then_inc(setup_z, 1)
            dve.wait_ge(fold_ps, 1)
            scale = float(HD) ** -0.5
            dve.tensor_scalar(fold_b[:, 0:1], bank[0][:, 0:1], col("q_b"), scale, ALU.add, ALU.mult)
            dve.tensor_scalar(fold_b[:, 1:2], bank[0][:, 1:2], col("k_b"), None, ALU.add)
            dve.tensor_scalar(fold_b[:, 2:3], bank[0][:, 2:3], col("v_b"), None, ALU.add)
            dve.tensor_tensor(fold_b[:, 3:3 + FC], bank[0][:, 3:3 + FC],
                              cols_sb[:, COLS["b1"][0]:COLS["b1"][0] + FC], ALU.add)
            dve.drain()
            dve.tensor_scalar(y_out[:, 0:P], ones[:], fold_b[:, 2:3], None, ALU.mult)\
               .then_inc(v_wide_ready, 1)
            dve.tensor_scalar(w_qkv[:, 0:C], w_qkv[:, 0:C], col("ln1_g"), scale, ALU.mult, ALU.mult)
            dve.tensor_scalar(w_qkv[:, C:3 * C], w_qkv[:, C:3 * C], col("ln1_g"), None, ALU.mult)
            dve.tensor_scalar(w_up, w_up, col("ln2_g"), None, ALU.mult)
            dve.wait_ge(setup_exp, 1)
            dve.tensor_reduce(tiny[:, 1:2], base[:], AX.X, ALU.add)
            dve.drain()
            dve.reciprocal(tiny[:, 2:3], tiny[:, 1:2])
            dve.drain()
            dve.tensor_scalar(base[:], base[:], tiny[:, 2:3], None, ALU.mult)
            dve.wait_ge(shift_ps, 1)
            dve.tensor_tensor(proj_shift[:], bank[1][:, 0:P], row("proj_b"), ALU.add)
            dve.wait_ge(rel_ps, 1)
            dve.tensor_copy(rel_bias[:], bank[2][:])
            dve.drain()
            dve.sem_inc(setup_dve, 1)

            def norm_stats(source, done):
                for c in range(CH):
                    dve.bn_stats(stats[:, c], source(c))
                dve.drain()
                for c in range(CH):
                    last = dve.bn_aggr(mv[:, c], stats[:, c])
                last.then_inc(done, 1)

            def normalise(source, done):
                dve.reciprocal(rstd[:], std[:])
                dve.drain()
                for c in range(CH):
                    last = dve.tensor_scalar(nT[:, c], source[:, c], mv[:, c, 0:1], rstd[:, c:c + 1],
                                             ALU.subtract, ALU.mult)
                    if c % 4 == 3:
                        last.then_inc(done, 1)

            def norm1_stats(i):
                dve.wait_ge(xT_sb, 2 * i + 2)
                norm_stats(lambda c: xT[:, c], ln1_var)

            def norm1(i):
                dve.wait_ge(ln1_std, i + 1)
                dve.wait_ge(xT_sb, 2 * i + 2)
                dve.wait_ge(n2T_ps, 2 * i)
                normalise(xT, nT_sb)

            def keys(i):
                for k in range(2):
                    dve.wait_ge(k_ps, 2 * i + k + 1)
                    dve.wait_ge(kh_sb, i)
                    dve.tensor_scalar(kC[:, HALF * k:HALF * k + HALF], bank[2 + k][:], fold_b[:, 1:2], None,
                                      ALU.add).then_inc(k_sb, 1)

            def bias_max(i, j):
                dve.wait_ge(s_ps, 8 * i + j + 1)
                if j >= 2:
                    dve.wait_ge(p_sb, 8 * i + j - 1)
                dve.tensor_tensor(score[:, j % 2].rearrange("p h k -> p (h k)"), bank[2 + j % 2][:], rel_bias[:],
                                  ALU.add).then_inc(s_biased, 1)
                dve.drain()
                dve.tensor_reduce(row_max[:, j % 2], score[:, j % 2], AX.X, ALU.max).then_inc(s_max, 1)

            def row_sums(i, j):
                dve.wait_ge(s_exp, 8 * i + j + 1)
                dve.tensor_reduce(row_sum[:, j % 2], score[:, j % 2], AX.X, ALU.add)
                dve.drain()
                dve.reciprocal(row_inv[:, j % 2], row_sum[:, j % 2]).then_inc(s_inv, 1)

            def residual1(i):
                for k in range(2):
                    dve.wait_ge(proj_ps, 2 * i + k + 1)
                    dve.wait_ge(res_sb, i + 1)
                    dve.tensor_tensor(x1T[:, 4 * k:4 * k + 4].rearrange("p c d -> p (c d)"), bank[2 + k][:],
                                      resT[:, 4 * k:4 * k + 4].rearrange("p c d -> p (c d)"), ALU.add)\
                       .then_inc(x1_sb, 1)

            def norm2(i):
                dve.drain()
                norm_stats(lambda c: x1T[:, c], ln2_var)
                dve.wait_ge(ln2_std, i + 1)
                normalise(x1T, n2T_sb)

            def swin_out(i):
                for k in range(2):
                    b = (0, 3)[k]
                    dve.wait_ge(down_ps, 2 * i + k + 1)
                    dve.wait_ge(in_ps, 2 * i)
                    for a in range(2):
                        last = dve.tensor_scalar(natural_windows(xm[:], 2 * k + a), windows(bank[b][:], a),
                                                 col("b2"), None, ALU.add)
                    last.then_inc(xm_sb, 1)

            def gap(n):
                dve.wait_ge(act_sb, 2 * n + 2)
                dve.tensor_scalar(vec[:, 0:1], sums[:, 0:1], sums[:, 1:2], 1.0 / TOK, ALU.add, ALU.mult)\
                   .then_inc(gap_sb, 1)

            def attention_vectors(n):
                dve.wait_ge(gap_ps, n + 1)
                dve.wait_ge(abs_sb, n + 1)
                dve.tensor_scalar(vec[:, 1:2], bank[6][:, 0:1], col("fac_b"), None, ALU.add)
                dve.tensor_scalar(vec[0:BATT, 4:5], bank[6][0:BATT, 1:2], col("batt_b1")[0:BATT], 0.0,
                                  ALU.add, ALU.max)
                dve.drain()
                dve.tensor_scalar(vec[:, 2:3], vec[:, 1:2], -1.0, None, ALU.mult)
                dve.tensor_scalar(batt_wide[0:BATT], ones[0:BATT], vec[0:BATT, 4:5], None, ALU.mult)
                dve.drain()
                dve.tensor_tensor(vec[:, 3:4], vec[:, 1:2], vec[:, 2:3], ALU.max)
                dve.drain()
                dve.tensor_scalar(vec[:, 5:6], sums[:, 2:3], vec[:, 3:4], 1.0 / TOK, ALU.mult, ALU.mult)\
                   .then_inc(mid_sb, 1)

            def scaled_input(n):
                dve.wait_ge(mid_ps, n + 1)
                dve.tensor_tensor(route[:, 0], bank[6][:, 8:8 + ROUTES], row("batt_b2"), ALU.add)\
                   .then_inc(route_z, 1)
                dve.tensor_scalar(vec[:, 6:7], bank[6][:, 2:3], col("conv_b"), vec[:, 3:4], ALU.add, ALU.mult)
                dve.drain()
                dve.tensor_scalar(xs[:], xs[:], vec[:, 6:7], None, ALU.mult).then_inc(xs_sb, 1)

            def route_logits(n):
                dve.wait_ge(route_e, n + 1)
                dve.tensor_tensor(route[:, 2], route[:, 1], base[:], ALU.mult)
                dve.drain()
                dve.tensor_reduce(vec[:, 7:8], route[:, 2], AX.X, ALU.max)
                dve.drain()
                dve.tensor_scalar(route[:, 0], route[:, 2], vec[:, 7:8], None, ALU.subtract)\
                   .then_inc(route_d, 1)

            def route_weights(n):
                dve.wait_ge(route_f, n + 1)
                dve.tensor_reduce(vec[:, 8:9], route[:, 1], AX.X, ALU.add)
                dve.drain()
                dve.reciprocal(vec[:, 9:10], vec[:, 8:9])
                dve.drain()
                cw = route[:, 3]
                dve.tensor_scalar(cw, route[:, 1], vec[:, 9:10], None, ALU.mult)
                dve.drain()
                dve.wait_ge(hv_sb, n)
                at = COLS["cr_w"][0]
                dve.tensor_tensor(cr_scaled[:], cols_sb[:, at:at + 27].rearrange("p (a t) -> p a t", a=3),
                                  cw[:, 0:3].unsqueeze(2).broadcast_to([P, 3, 9]), ALU.mult)
                at = COLS["cr_b"][0]
                dve.tensor_tensor(cr_bias[:], cols_sb[:, at:at + 3], cw[:, 0:3], ALU.mult)
                dve.tensor_tensor(mix[:, 0:1], col("dw_w"), cw[:, 3:4], ALU.mult)
                dve.tensor_tensor(mix[:, 1:2], col("dw_b"), cw[:, 3:4], ALU.mult)
                dve.tensor_tensor(mix[:, 2:3], col("alpha"), cw[:, 4:5], ALU.mult)
                dve.tensor_tensor(mix[:, 3:4], col("beta"), cw[:, 4:5], ALU.mult)
                dve.drain()
                dve.tensor_tensor(mix[:, 4:5], cr_bias[:, 0:1], cr_bias[:, 1:2], ALU.add).then_inc(cw_sb, 1)

            def taps(n, which):
                for t in which:
                    a, k = divmod(t, 9)
                    src = (hor, ver, pyr)[a][:, k // 3:k // 3 + SIDE, k % 3:k % 3 + SIDE]
                    dst = (hv, hv, py)[a]
                    dve.drain()
                    if t == 9:
                        dve.wait_ge(axis_sb, 2 * n + 2)
                    if t == 0:
                        dve.wait_ge(axis_sb, 2 * n + 1)
                        dve.wait_ge(relu_sb, n)
                    if t == 18:
                        dve.wait_ge(pyr_sb, 2 * n + 2)
                        dve.wait_ge(base_sb, n)
                    if t in (0, 18):
                        bias = mix[:, 4:5] if t == 0 else cr_bias[:, 2:3]
                        last = dve.tensor_scalar(dst[:], src, cr_scaled[:, a, k:k + 1], bias, ALU.mult, ALU.add)
                    else:
                        last = dve.scalar_tensor_tensor(dst[:], src, cr_scaled[:, a, k:k + 1], dst[:], ALU.mult,
                                                        ALU.add)
                    if t == 17:
                        last.then_inc(hv_sb, 1)
                    if t == 26:
                        last.then_inc(py_sb, 1)

            def boosted(n):
                for k in range(2):
                    dve.wait_ge(w_ps, 2 * n + k + 1)
                    dve.wait_ge(t_ps, 2 * n + 2)
                    last = dve.tensor_tensor(fb[:, HALF * k:HALF * k + HALF], bank[4 + k][:],
                                             boost[:, 4 * k:4 * k + 4].rearrange("p g c -> p (g c)"), ALU.mult)
                last.then_inc(w_sb, 1)
                dve.drain()
                dve.tensor_tensor(fb[0:1, 0:C], fb[0:1, 0:C], dc_b2[0:1], ALU.add).then_inc(w_sb, 1)

            def odd_product(n):
                for k in range(2):
                    h = slice(HALF * k, HALF * k + HALF)
                    dve.wait_ge(r2_ps, 2 * n + k + 1)
                    dve.tensor_tensor(fd[:, h], bank[6 + k][:], fb[:, h], ALU.mult).then_inc(go_sb, 1)

            def mixture(n):
                dve.wait_ge(base_sb, n + 1)
                dve.scalar_tensor_tensor(hv[:], act_in, mix[:, 0:1], hv[:], ALU.mult, ALU.add)
                dve.drain()
                dve.scalar_tensor_tensor(hv[:], xs_hw, mix[:, 3:4], hv[:], ALU.mult, ALU.add)
                dve.drain()
                dve.wait_ge(mag_sb, n + 1)
                dve.scalar_tensor_tensor(hv[:], grid(fa), mix[:, 2:3], hv[:], ALU.mult, ALU.add)
                dve.drain()
                dve.tensor_tensor(hv[:], hv[:], gated[:], ALU.add).then_inc(mixed_sb, 1)

            def conv_slot(n, j):
                if j == 3:
                    boosted(n)
                if j == 4:
                    odd_product(n)
                taps(n, range(27 * j // PAIRS, 27 * (j + 1) // PAIRS))

            def swin_only(i):
                norm1_stats(i)
                norm1(i)
                keys(i)
                bias_max(i, 0)
                for j in range(PAIRS):
                    if j + 1 < PAIRS:
                        bias_max(i, j + 1)
                    row_sums(i, j)
                residual1(i)
                norm2(i)
                swin_out(i)

            def both(n, i):
                gap(n)
                norm1_stats(i)
                attention_vectors(n)
                norm1(i)
                scaled_input(n)
                route_logits(n)
                keys(i)
                route_weights(n)
                bias_max(i, 0)
                for j in range(PAIRS):
                    if j + 1 < PAIRS:
                        bias_max(i, j + 1)
                    row_sums(i, j)
                    conv_slot(n, j)
                residual1(i)
                norm2(i)
                mixture(n)
                swin_out(i)

            def conv_only(n):
                gap(n)
                attention_vectors(n)
                scaled_input(n)
                route_logits(n)
                route_weights(n)
                for j in range(PAIRS):
                    conv_slot(n, j)
                mixture(n)

            swin_only(0)
            with dve.Fori(0, IMAGES - 1) as n:
                both(n, n + 1)
            conv_only(IMAGES - 1)

        @block.scalar
        def _(act_):
            act_.wait_ge(setup_z, 1)
            act_.activation(base[:], base[:], ACT.Exp).then_inc(setup_exp, 1)
            act_.wait_ge(setup_dve, 1)
            act_.wait_ge(zeroed, 1)

            def to_windows(i):
                act_.wait_ge(x_loaded, 16 * i + 16)
                act_.wait_ge(proj_ps, 2 * i)
                for a in range(4):
                    last = act_.activation(windows(xw[:], a), natural_windows(x_in[:], a), ACT.Copy)
                last.then_inc(xw_ready, 1)

            def x_copy(i):
                for k in range(2):
                    act_.wait_ge(xT_ps, 2 * i + k + 1)
                    act_.wait_ge(down_ps, 2 * i)
                    act_.activation(xT[:, 4 * k:4 * k + 4].rearrange("p c d -> p (c d)"), bank[k][:], ACT.Copy)\
                        .then_inc(xT_sb, 1)

            def deviation1(i):
                act_.wait_ge(ln1_var, i + 1)
                act_.activation(std[:], mv[:, :, 1], ACT.Sqrt, bias=eps[:]).then_inc(ln1_std, 1)

            def deviation2(i):
                act_.wait_ge(ln2_var, i + 1)
                act_.activation(std[:], mv[:, :, 1], ACT.Sqrt, bias=eps[:]).then_inc(ln2_std, 1)

            def copy(dst, src):
                return act_.activation(dst, src, ACT.Copy)

            def half(ap, k):
                return ap[:, HALF * k:HALF * k + HALF]

            def n_copy(i):
                for k in range(2):
                    act_.wait_ge(nT_ps, 2 * i + k + 1)
                    copy(half(nC, k), bank[2 + k][:]).then_inc(nC_sb, 1)

            def n2_copy(i):
                for k in range(2):
                    act_.wait_ge(n2T_ps, 2 * i + k + 1)
                    copy(half(nC, k), bank[k][:]).then_inc(n2C_sb, 1)

            def queries(i):
                for k in range(2):
                    act_.wait_ge(q_ps, 2 * i + k + 1)
                    act_.activation(qC[:, HALF * k:HALF * k + HALF], bank[k][:], ACT.Identity, bias=fold_b[:, 0:1])\
                        .then_inc(q_sb, 1)

            def v_copy(i):
                for k in range(2):
                    act_.wait_ge(v_ps, 2 * i + k + 1)
                    for e in range(2):
                        dst = v_pair[64 * e:64 * e + 64, 8 * k:8 * k + 8, :, e].rearrange("p w g d -> p (w g) d")
                        src = bank[k][64 * e:64 * e + 64, :].rearrange("p (w d) -> p w d", d=HD)
                        last = act_.activation(dst, src, ACT.Copy)
                    last.then_inc(v_sb, 1)

            def exponent(i, j):
                act_.wait_ge(s_sub, 8 * i + j + 1)
                act_.activation(score[:, j % 2].rearrange("p h k -> p (h k)"),
                                score[:, j % 2].rearrange("p h k -> p (h k)"), ACT.Exp).then_inc(s_exp, 1)

            def prob_copy(i, j):
                act_.wait_ge(pT_ps, 8 * i + j + 1)
                act_.activation(probT[:, j % 2].rearrange("p g t -> p (g t)"), bank[0][:], ACT.Copy)\
                    .then_inc(pT_sb, 1)

            def attention_copy(i, k):
                act_.wait_ge(o_ps, 8 * i + 4 * k + 4)
                act_.activation(attn_out[:, HALF * k:HALF * k + HALF], bank[1][:], ACT.Copy).then_inc(o_sb, 1)

            def mlp_gelu(i):
                for t in range(2 * FC):
                    k, f = divmod(t, FC)
                    act_.wait_ge(up_ps, 8 * i + t + 1)
                    act_.activation(hidden[:, f, HALF * k:HALF * k + HALF], bank[(2, 3, 0, 1, 2, 3, 1, 2)[t]][:],
                                    ACT.Gelu, bias=fold_b[:, 3 + f:4 + f]).then_inc(up_sb, 1)

            def in_gelu(n):
                for k in range(2):
                    act_.wait_ge(in_ps, 2 * n + k + 1)
                    act_.activation(act[:, PAD + 16 * k:PAD + 16 * k + 16, PAD:PAD + SIDE],
                                    bank[4 + k].rearrange("p (h w) -> p h w", w=SIDE), ACT.Gelu, bias=col("in_b"),
                                    accum_out=sums[:, k:k + 1]).then_inc(act_sb, 1)

            def magnitudes(n):
                act_.drain()
                act_.wait_ge(mixed_sb, n)
                act_.activation(xs_hw, act_in, ACT.Abs, accum_out=sums[:, 2:3]).then_inc(abs_sb, 1)

            def edge_sigmoid(n):
                act_.wait_ge(edge_ps, n + 1)
                act_.activation(edge_half[:], bank[7][:, 0:256], ACT.Sigmoid, bias=col("vis_b"))\
                    .then_inc(edge_sig, 1)

            def route_exponents(n):
                act_.wait_ge(route_z, n + 1)
                act_.activation(route[:, 1], route[:, 0], ACT.Sigmoid).then_inc(route_e, 1)
                act_.wait_ge(route_d, n + 1)
                act_.activation(route[:, 1], route[:, 0], ACT.Exp).then_inc(route_f, 1)

            def edge_copy(n):
                for k in range(2):
                    act_.wait_ge(eb_ps, 2 * n + k + 1)
                    act_.wait_ge(gated_sb, n)
                    act_.activation(edge[:, 16 * k:16 * k + 16], bank[4 + k].rearrange("p (h w) -> p h w", w=SIDE),
                                    ACT.Copy).then_inc(edge_sb, 1)

            def pyr_copy(n, k):
                act_.wait_ge(pyr_ps, 2 * n + k + 1)
                act_.wait_ge(py_sb, n)
                act_.activation(pyr[:, 1 + 16 * k:17 + 16 * k, 1:1 + SIDE],
                                bank[6 + k].rearrange("p (h w) -> p h w", w=SIDE), ACT.Identity, bias=fuse_bias[:],
                                scale=col("fuse_w")).then_inc(pyr_sb, 1)

            def other_order(dst, k):
                return dst.rearrange("c (a b) -> c b a", b=SIDE)[:, 16 * k:16 * k + 16]

            def rows_of(ps):
                return ps.rearrange("c (b a) -> c b a", a=SIDE)

            def square(dst, ps, k):
                to = dst.rearrange("c (h j w) -> c j h w", j=CH, w=4)[:, 4 * k:4 * k + 4]
                return act_.activation(to, ps.rearrange("c (j h w) -> c j h w", j=4, w=4), ACT.Square)

            def x2_copy(n):
                for k in range(2):
                    act_.wait_ge(x2_ps, 2 * n + k + 1)
                    copy(half(fa, k), bank[4 + k][:]).then_inc(x2_sb, 1)

            def row_spectrum_copy(n):
                for k in range(2):
                    act_.wait_ge(h_ps, 2 * n + k + 1)
                    copy(other_order(fb, k), rows_of(bank[6 + k])).then_inc(h_sb, 1)

            def spectrum_turn_copy(n):
                for k in range(2):
                    act_.wait_ge(t_ps, 2 * n + k + 1)
                    copy(half(fa, k), bank[4 + k][:]).then_inc(t_sb, 1)

            def r_even_copy(n):
                for k in range(2):
                    act_.wait_ge(r1_ps, 2 * n + k + 1)
                    copy(half(fc, k), bank[6 + k][:]).then_inc(r1_sb, 1)

            def inverse_even_copy(n):
                for k in range(2):
                    act_.wait_ge(ae_ps, 2 * n + k + 1)
                    copy(other_order(fa, k), rows_of(bank[4 + k])).then_inc(ae_sb, 1)

            def inverse_odd_copy(n):
                act_.wait_ge(go_sb, 2 * n + 2)
                for k in range(2):
                    act_.wait_ge(ao_ps, 2 * n + k + 1)
                    copy(other_order(fb, k), rows_of(bank[6 + k])).then_inc(ao_sb, 1)

            def turn_even_copy(n):
                for k in range(2):
                    act_.wait_ge(te_ps, 2 * n + k + 1)
                    copy(half(fc, k), bank[4 + k][:]).then_inc(te_sb, 1)

            def turn_odd_copy(n):
                for k in range(2):
                    act_.wait_ge(to_ps, 2 * n + k + 1)
                    copy(half(fd, k), bank[6 + k][:]).then_inc(to_sb, 1)

            def square_even(n):
                for k in range(2):
                    act_.wait_ge(be_ps, 2 * n + k + 1)
                    square(fa, bank[4 + k], k).then_inc(be_sb, 1)

            def square_odd(n):
                for k in range(2):
                    act_.wait_ge(bo_ps, 2 * n + k + 1)
                    square(fb, bank[6 + k], k).then_inc(bo_sb, 1)

            def magnitude(n):
                act_.wait_ge(sq_sb, n + 1)
                act_.activation(fa, fa, ACT.Sqrt).then_inc(mag_sb, 1)

            def rectify(n):
                act_.wait_ge(mixed_sb, n + 1)
                act_.activation(grid(relu), hv[:], ACT.Relu, bias=mix[:, 1:2]).then_inc(relu_sb, 1)

            def out_copy(n):
                for k in range(2):
                    act_.wait_ge(out_ps, 2 * n + k + 1)
                    act_.wait_ge(stored, 16 * n)
                    act_.activation(y_out[:, HALF * k:HALF * k + HALF], bank[4 + k][:], ACT.Identity,
                                    bias=col("out_b")).then_inc(out_sb, 1)

            def conv_early(n, j):
                if j < 2:
                    pyr_copy(n, j)
                elif j == 2:
                    row_spectrum_copy(n)
                elif j == 3:
                    r_even_copy(n)
                elif j == 5:
                    inverse_odd_copy(n)
                elif j == 6:
                    turn_odd_copy(n)
                elif j == 7:
                    square_odd(n)

            def conv_late(n, j):
                if j == 1:
                    x2_copy(n)
                elif j == 2:
                    spectrum_turn_copy(n)
                elif j == 4:
                    inverse_even_copy(n)
                elif j == 5:
                    turn_even_copy(n)
                elif j == 6:
                    square_even(n)

            def swin_only(i):
                to_windows(i)
                x_copy(i)
                deviation1(i)
                n_copy(i)
                queries(i)
                v_copy(i)
                exponent(i, 0)
                for j in range(PAIRS):
                    if j + 1 < PAIRS:
                        exponent(i, j + 1)
                    prob_copy(i, j)
                    if j == 4:
                        attention_copy(i, 0)
                attention_copy(i, 1)
                deviation2(i)
                n2_copy(i)
                mlp_gelu(i)

            def both(n, i):
                to_windows(i)
                in_gelu(n)
                magnitudes(n)
                x_copy(i)
                deviation1(i)
                n_copy(i)
                edge_sigmoid(n)
                route_exponents(n)
                queries(i)
                edge_copy(n)
                v_copy(i)
                exponent(i, 0)
                for j in range(PAIRS):
                    conv_early(n, j)
                    if j + 1 < PAIRS:
                        exponent(i, j + 1)
                    prob_copy(i, j)
                    if j == 4:
                        attention_copy(i, 0)
                    conv_late(n, j)
                attention_copy(i, 1)
                magnitude(n)
                deviation2(i)
                n2_copy(i)
                mlp_gelu(i)
                rectify(n)
                out_copy(n)

            def conv_only(n):
                in_gelu(n)
                magnitudes(n)
                edge_sigmoid(n)
                route_exponents(n)
                edge_copy(n)
                for j in range(PAIRS):
                    conv_early(n, j)
                    conv_late(n, j)
                magnitude(n)
                rectify(n)
                out_copy(n)

            swin_only(0)
            with act_.Fori(0, IMAGES - 1) as n:
                both(n, n + 1)
            conv_only(IMAGES - 1)

        @block.gpsimd
        def _(pool):
            pool.memset(act[:], 0.0)
            for padded in (hor, ver, pyr):
                pool.memset(padded[:], 0.0)
            pool.memset(v_pair[:], 0.0)
            pool.drain()
            pool.sem_inc(zeroed, 1)
            pool.wait_ge(setup_dve, 1)

            def residual_in(i):
                pool.wait_ge(xT_sb, 2 * i + 2)
                pool.sem_inc(pool_turns)
                pool.wait_ge(x1_sb, 2 * i)
                pool.sem_inc(pool_turns)
                pool.tensor_tensor(resT[:], xT[:], proj_shift[:].unsqueeze(1).broadcast_to([P, CH, C]), ALU.add)\
                    .then_inc(res_sb, 1)

            def key_heads(i):
                pool.wait_ge(k_sb, 2 * i + 2)
                pool.sem_inc(pool_turns)
                pool.wait_ge(down_ps, 2 * i)
                pool.sem_inc(pool_turns)
                for h in range(HEADS):
                    at = CONS["head_mask"][0] + h
                    last = pool.tensor_scalar(k_heads[:, :, h], kC.rearrange("p (w k) -> p w k", w=WIN),
                                              cons_sb[:, at:at + 1], 1.0, ALU.mult, ALU.mult)
                last.then_inc(kh_sb, 1)

            def less_max(i, j):
                pool.wait_ge(s_max, 8 * i + j + 1)
                pool.sem_inc(pool_turns)
                pool.tensor_tensor(score[:, j % 2], score[:, j % 2],
                                   row_max[:, j % 2].unsqueeze(2).broadcast_to([P, HEADS, WT]), ALU.subtract)\
                    .then_inc(s_sub, 1)

            def normalise(i, j):
                pool.wait_ge(s_inv, 8 * i + j + 1)
                pool.sem_inc(pool_turns)
                if j >= 2:
                    pool.wait_ge(pT_ps, 8 * i + j - 1)
                    pool.sem_inc(pool_turns)
                pool.tensor_tensor(prob[:, j % 2].rearrange("p (h k) -> p h k", h=HEADS), score[:, j % 2],
                                   row_inv[:, j % 2].unsqueeze(2).broadcast_to([P, HEADS, WT]), ALU.mult)\
                    .then_inc(p_sb, 1)

            def axis_conv(n, a):
                pool.wait_ge(act_sb, 2 * n + 2)
                pool.sem_inc(pool_turns)
                pool.wait_ge(mixed_sb, n)
                pool.sem_inc(pool_turns)
                mid = AXIS_TAPS // 2
                dst, name = ((hor, "dilh"), (ver, "dilv"))[a]
                body = dst[:, 1:1 + SIDE, 1:1 + SIDE]
                last = pool.tensor_scalar(body, act_in, col(name, mid), 1.0, ALU.mult, ALU.mult)
                for t in range(AXIS_TAPS):
                    off = AXIS_DIL * (t - mid)
                    if off == 0 or abs(off) >= SIDE:
                        continue
                    lo, hi = max(0, -off), min(SIDE, SIDE - off)
                    if a == 0:
                        part = (slice(None), slice(None), slice(lo, hi))
                        of = act_in[:, :, lo + off:hi + off]
                    else:
                        part = (slice(None), slice(lo, hi))
                        of = act_in[:, lo + off:hi + off]
                    pool.drain()
                    pool.tensor_scalar(gated[part], of, col(name, t), 1.0, ALU.mult, ALU.mult)
                    pool.drain()
                    last = pool.tensor_tensor(body[part], body[part], gated[part], ALU.add)
                last.then_inc(axis_sb, 1)

            def mirrored(dst, op):
                d = dst.rearrange("p (a r k) -> p a r k", a=16, r=2)
                rows_, back, two = xs_hw[:, 1:16], xs_hw[:, 31:16:-1], xs_hw[:, 0:17:16]
                pool.tensor_tensor(d[:, 1:16, :, 1:32], rows_[:, :, 1:32].unsqueeze(2).broadcast_to([P, 15, 2, 31]),
                                   back[:, :, 31:0:-1].unsqueeze(2).broadcast_to([P, 15, 2, 31]), op)
                pool.tensor_tensor(d[:, 1:16, :, 0], rows_[:, :, 0:1].broadcast_to([P, 15, 2]),
                                   back[:, :, 0:1].broadcast_to([P, 15, 2]), op)
                m = d[:, 0, :, 2:32].rearrange("p r (m u) -> p r m u", u=2)
                pool.tensor_tensor(m, two[:, :, 1:16].unsqueeze(3).broadcast_to([P, 2, 15, 2]),
                                   two[:, :, 31:16:-1].unsqueeze(3).broadcast_to([P, 2, 15, 2]), op)
                return pool.tensor_tensor(d[:, 0, :, 0:2], two[:, :, 0:17:16], two[:, :, 0:17:16], op)

            def even_odd(n):
                pool.wait_ge(xs_sb, n + 1)
                pool.sem_inc(pool_turns)
                pool.wait_ge(r2_ps, 2 * n)
                pool.sem_inc(pool_turns)
                mirrored(xe[:], ALU.add).then_inc(xe_sb, 1)
                mirrored(xo[:], ALU.subtract).then_inc(xo_sb, 1)

            def even_bias(n):
                pool.wait_ge(r1_sb, 2 * n + 2)
                pool.sem_inc(pool_turns)
                f = fc.rearrange("p (g c) -> p g c", g=CH)
                pool.tensor_tensor(f, f, two_b1[:].unsqueeze(1).broadcast_to([P, CH, C]), ALU.add)

            def even_product(n):
                pool.wait_ge(w_sb, 2 * n + 2)
                pool.sem_inc(pool_turns)
                pool.drain()
                pool.tensor_tensor(fc, fc, fb, ALU.mult).then_inc(ge_sb, 1)

            def gate(n):
                pool.wait_ge(py_sb, n + 1)
                pool.sem_inc(pool_turns)
                pool.wait_ge(hv_sb, n + 1)
                pool.sem_inc(pool_turns)
                pool.wait_ge(edge_sb, 2 * n + 2)
                pool.sem_inc(pool_turns)
                pool.tensor_scalar(gated[:], py[:], -0.3, 1.0, ALU.mult, ALU.mult)
                pool.drain()
                pool.tensor_tensor(gated[:], gated[:], hv[:], ALU.add)
                pool.drain()
                pool.tensor_tensor(gated[:], gated[:], edge[:], ALU.mult).then_inc(gated_sb, 1)
                pool.drain()
                pool.tensor_tensor(hv[:], hv[:], py[:], ALU.add)
                pool.drain()
                pool.tensor_tensor(hv[:], hv[:], grid(xm[:]), ALU.add).then_inc(base_sb, 1)

            def square_sum(n):
                pool.wait_ge(be_sb, 2 * n + 2)
                pool.sem_inc(pool_turns)
                pool.wait_ge(bo_sb, 2 * n + 2)
                pool.sem_inc(pool_turns)
                pool.tensor_tensor(fa, fa, fb, ALU.add).then_inc(sq_sb, 1)

            def swin_only(i):
                residual_in(i)
                key_heads(i)
                less_max(i, 0)
                for j in range(PAIRS):
                    if j + 1 < PAIRS:
                        less_max(i, j + 1)
                    normalise(i, j)

            def both(n, i):
                residual_in(i)
                axis_conv(n, 0)
                key_heads(i)
                less_max(i, 0)
                for j in range(PAIRS):
                    if j + 1 < PAIRS:
                        less_max(i, j + 1)
                    normalise(i, j)
                    if j == 0:
                        even_odd(n)
                    elif j == 1:
                        axis_conv(n, 1)
                    elif j == 3:
                        even_bias(n)
                        even_product(n)
                square_sum(n)
                gate(n)

            def conv_only(n):
                axis_conv(n, 0)
                even_odd(n)
                axis_conv(n, 1)
                even_bias(n)
                even_product(n)
                square_sum(n)
                gate(n)

            swin_only(0)
            with pool.Fori(0, IMAGES - 1) as n:
                both(n, n + 1)
            conv_only(IMAGES - 1)


def kernel(**inputs):
    import concourse.bacc as bacc
    from concourse.bass_utils import run_bass_kernel_spmd

    a = {k: np.asarray(v) for k, v in inputs.items()}
    swin = {k[8:]: v for k, v in a.items() if k.startswith("L0_conv_")}
    conv = {k[8:]: v for k, v in a.items() if k.startswith("L1_conv_")}

    cols = np.zeros((P, NCOLS), np.float32)

    def put(name, value):
        value = value.reshape(value.shape[0], -1)
        cols[:value.shape[0], COLS[name][0]:COLS[name][0] + value.shape[1]] = value

    put("ln1_g", swin["ln1_g"])
    put("ln1_b", swin["ln1_b"])
    for k, name in enumerate(("q_b", "k_b", "v_b")):
        put(name, swin["qkv_b"][k * C:(k + 1) * C])
    put("ln2_g", swin["ln2_g"])
    put("ln2_b", swin["ln2_b"])
    put("b1", swin["b1"].reshape(FC, P).T)
    put("b2", swin["b2"])
    for name in ("in_b", "out_b", "fac_b", "conv_b", "fuse_w", "fuse_b", "cr_b"):
        put(name, conv[name].T if name == "cr_b" else conv[name])
    put("alpha", conv["fgm_alpha"])
    put("beta", conv["fgm_beta"])
    put("dw_w", conv["dw11_w"])
    put("dw_b", conv["dw11_b"])
    put("pyr_b", conv["pyr_b"].reshape(-1))
    put("vis_b", np.repeat(conv["vis_b"], P))
    put("batt_b1", conv["batt_b1"])
    put("dilh", conv["dilh_w"])
    put("dilv", conv["dilv_w"])
    put("cr_w", conv["cr_w"].reshape(3, C, 9).transpose(1, 0, 2))
    rows = np.concatenate([swin["proj_b"], conv["fgm_b1"], conv["fgm_b2"], conv["fgm_boost"].reshape(-1),
                           conv["batt_b2"], conv["base_weights"]])[None]
    pyr = np.zeros((C, len(DILS), 9, 32), np.float32)
    for o in range(32):
        pyr[4 * o:4 * o + 4, :, :, o] = conv["pyr_w"][:, o].reshape(len(DILS), 4, 9).transpose(1, 0, 2)
    batt2 = np.zeros((P, ROUTES), np.float32)
    batt2[:BATT] = conv["batt_w2"].reshape(ROUTES, BATT).T
    table = np.zeros((2 * P, HEADS), np.float32)
    table[:REL] = swin["rpb_table"]
    mats = np.concatenate([
        swin["qkv_w"].T, swin["proj_w"].T, swin["w1"].T,
        swin["w2"].reshape(C, FC, P).transpose(2, 1, 0).reshape(P, -1),
        conv["in_w"].reshape(C, C).T, conv["out_w"].reshape(C, C).T, conv["fac_w"].reshape(C, C).T,
        conv["conv_w"].reshape(C, C).T, conv["fgm_w1"].reshape(C, C).T, conv["fgm_w2"].reshape(C, C).T,
        conv["vis_w"].reshape(C, 9), conv["batt_w1"].reshape(BATT, C).T, batt2, pyr.reshape(C, -1),
        table.reshape(2, P, HEADS).transpose(1, 0, 2).reshape(P, -1)], 1)
    arrays = {
        "x_dram": np.ascontiguousarray(a["x"].reshape(IMAGES, C, TOK)),
        "cols_dram": cols,
        "rows_dram": np.ascontiguousarray(rows),
        "mats_dram": np.ascontiguousarray(mats),
        "cons_dram": shape_constants(),
        "rel_dram": np.ascontiguousarray(swin["rpi"].T.reshape(1, WT * WT)),
    }
    nc = bacc.Bacc("TRN2", target_bir_lowering=False, num_devices=1)
    args = [nc.dram_tensor(k, v.shape, mybir.dt.from_np(v.dtype), kind="ExternalInput").ap()
            for k, v in arrays.items()]
    args.append(nc.dram_tensor("out_dram", (IMAGES, C, TOK), F32, kind="ExternalOutput").ap())
    x_, cols_, rows_, mats_, cons_, rel_, out_ = args
    swin_conv_kernel(nc, x_, cols_, rows_, mats_, cons_, rel_, out_)
    result = run_bass_kernel_spmd(nc, [arrays], core_ids=[0])
    return result.results[0]["out_dram"].reshape(IMAGES, C, SIDE, SIDE)
```

```python
from contextlib import ExitStack

import numpy as np
import concourse.bass as bass
from concourse import mybir

F32 = mybir.dt.float32
I32 = mybir.dt.int32
ALU = mybir.AluOpType
ACT = mybir.ActivationFunctionType
AX = mybir.AxisListType

IMAGES, C, SIDE = 16, 128, 32
TOK = SIDE * SIDE
P = 128
CH = TOK // P
HALF = TOK // 2
WS, HEADS = 8, 8
WT = WS * WS
HD = C // HEADS
WIN = TOK // WT
PAIRS = WIN // 2
HP = HEADS // 2
FF = 512
FC = FF // P
LN_EPS = 1e-5
DILS = (1, 6, 12, 20)
PAD = max(DILS)
SP = SIDE + 2 * PAD
S1 = SIDE + 2
AXIS_DIL, AXIS_TAPS = 11, 7
REL = (2 * WS - 1) ** 2
BATT = C // 8
ROUTES = 5


def layout(*entries):
    at, where = 0, {}
    for name, width in entries:
        where[name] = (at, width)
        at += width
    return where, at


COLS, NCOLS = layout(
    ("ln1_g", 1), ("ln1_b", 1), ("q_b", 1), ("k_b", 1), ("v_b", 1), ("ln2_g", 1), ("ln2_b", 1),
    ("b1", FC), ("b2", 1), ("in_b", 1), ("out_b", 1), ("fac_b", 1), ("conv_b", 1), ("alpha", 1),
    ("beta", 1), ("fuse_w", 1), ("fuse_b", 1), ("dw_w", 1), ("dw_b", 1), ("pyr_b", 1), ("vis_b", 1),
    ("batt_b1", 1), ("dilh", AXIS_TAPS), ("dilv", AXIS_TAPS), ("cr_w", 27), ("cr_b", 3))
ROWS, NROWS = layout(("proj_b", C), ("fgm_b1", C), ("fgm_b2", C), ("boost", C), ("batt_b2", ROUTES),
                     ("base", ROUTES))
MATS, NMATS = layout(
    ("qkv", 3 * C), ("proj", C), ("w1", FF), ("w2", FF), ("in", C), ("out", C), ("fac", C),
    ("conv", C), ("fgm1", C), ("fgm2", C), ("vis", 9), ("batt1", BATT), ("batt2", ROUTES),
    ("pyr", len(DILS) * 9 * 32), ("table", 2 * HEADS))
CONS, NCONS = layout(
    ("ident", P), ("sel", 4 * P), ("dft_h", P), ("dft_w0", P), ("dft_w", P), ("even0", P),
    ("even", P), ("odd0", P), ("odd", P), ("idft_h", P), ("head_mask", HEADS), ("high", CH), ("iota", 2))


def shape_constants():
    n = SIDE
    ang = 2 * np.pi * np.outer(np.arange(n), np.arange(n)) / n
    cos, sin = np.cos(ang), np.sin(ang)
    pack = np.zeros((n, n))
    pack[:, 0], pack[:, 1] = 1, cos[:, 16]
    pack[:, 2::2], pack[:, 3::2] = cos[:, 1:16], -sin[:, 1:16]
    unpack = np.zeros((n, n))
    unpack[0], unpack[1] = 1, cos[16]
    unpack[2::2], unpack[3::2] = 2 * cos[1:16], -2 * sin[1:16]
    unpack /= n
    full = np.block([[cos, -sin], [sin, cos]])
    inv = np.block([[cos, sin], [-sin, cos]]) / n

    def diag(*blocks):
        size = sum(len(b) for b in blocks)
        out, at = np.zeros((size, size)), 0
        for b in blocks:
            out[at:at + len(b), at:at + len(b)] = b
            at += len(b)
        return out

    inv_odd = np.concatenate([-inv[n:], inv[:n]])
    unpack_odd = np.zeros((n, n))
    unpack_odd[2::2], unpack_odd[3::2] = -unpack[3::2], unpack[2::2]
    c = np.zeros((P, NCONS))

    def put(name, value):
        at, width = CONS[name]
        c[:, at:at + width] = value

    put("ident", np.eye(P))
    sel = np.zeros((P, 4, P))
    for q in range(4):
        sel[32 * q, q] = 1
    put("sel", sel.reshape(P, -1))
    put("dft_h", diag(pack, pack, pack, pack))
    put("dft_w0", diag(pack, pack, full))
    put("dft_w", diag(full, full))
    put("even0", 0.5 * diag(unpack, unpack, inv))
    put("even", 0.5 * diag(inv, inv))
    put("odd0", 0.5 * diag(unpack_odd, unpack_odd, inv_odd))
    put("odd", 0.5 * diag(inv_odd, inv_odd))
    idft = diag(unpack, unpack, unpack, unpack).reshape(P, 4, n)
    put("idft_h", idft.transpose(0, 2, 1).reshape(P, P))
    put("head_mask", np.arange(P)[:, None] // HD == np.arange(HEADS)[None])
    freq = np.minimum(np.arange(n), n - np.arange(n)) / n
    packed_k = np.array([0, 16] + [k for k in range(1, 16) for _ in range(2)])
    high = np.zeros((CH, 2, 2, n))
    for g in range(CH):
        for s in range(2):
            for r in range(2):
                kh = 2 * g + s
                kw = np.arange(n)
                if kh == 0:
                    kh, kw = 16 * r, packed_k
                high[g, s, r] = np.sqrt(freq[kh] ** 2 + freq[kw] ** 2) > 0.3
    put("high", high.reshape(CH, P).T)
    put("iota", np.stack([np.arange(P), np.arange(P) + P], 1))
    return c.astype(np.float32)


def swin_conv_kernel(nc, x, cols, rows, mats, cons, rel_index, out):
    with ExitStack() as ctx:
        def sb(name, *free, dt=F32):
            return ctx.enter_context(nc.sbuf_tensor(name, [P, *free], dt))

        def sem(name):
            return ctx.enter_context(nc.semaphore(name))

        cons_sb, cols_sb, mats_sb = sb("cons_sb", NCONS), sb("cols_sb", NCOLS), sb("mats_sb", NMATS)
        rows_sb = sb("rows_sb", NROWS)

        def con(name):
            at, width = CONS[name]
            return cons_sb[:, at:at + width]

        def col(name, k=0):
            return cols_sb[:, COLS[name][0] + k:COLS[name][0] + k + 1]

        def row(name):
            at, width = ROWS[name]
            return rows_sb[:, at:at + width]

        def mat(name):
            at, width = MATS[name]
            return mats_sb[:, at:at + width]

        ident = con("ident")
        w_qkv, w_proj, w_up, w_down = mat("qkv"), mat("proj"), mat("w1"), mat("w2")
        w_pyr = mat("pyr").rearrange("p (d t o) -> p d t o", d=len(DILS), t=9)
        ones = sb("ones", P)
        eps = sb("eps", 1)
        cut_bias = sb("cut_bias", 1)
        first_gelu = sb("first_gelu", 1)
        fold_b = sb("fold_b", 3 + FC)
        fuse_bias = sb("fuse_bias", 1)
        w_vis = sb("w_vis", 9, 32)
        proj_shift = sb("proj_shift", P)
        two_b1 = sb("two_b1", P)
        rel_bias = sb("rel_bias", HEADS * WT)
        boost = sb("boost", CH, C)
        base = sb("base", ROUTES)
        dc_b2 = sb("dc_b2", P)
        tiny = sb("tiny", 8)

        x_in = sb("x_in", TOK)
        xw = sb("xw", TOK)
        attn_out = xw
        xT = sb("xT", CH, C)
        x1T = xT
        resT = sb("resT", CH, C)
        nT = sb("nT", CH, C)
        nC = sb("nC", TOK)
        qC, kC = sb("qC", TOK), sb("kC", TOK)
        k_heads = sb("k_heads", WIN, HEADS, WT)
        hidden = k_heads[:, 0:8].rearrange("p a h k -> p (a h k)").rearrange("p (f t) -> p f t", f=FC)
        v_pair = sb("v_pair", WIN, HP, 2, HD)
        score = sb("score", 3, HEADS, WT)
        prob = sb("prob", 2, HEADS * WT)
        probT = sb("probT", 2, HP, P)
        stats, mv = sb("stats", CH, 6), sb("mv", CH, 2)
        std, rstd = sb("std", CH), sb("rstd", CH)
        row_max, row_sum, row_inv = sb("row_max", 3, HEADS), sb("row_sum", 3, HEADS), sb("row_inv", 3, HEADS)
        parts = (kC, nC, kC, nC, kC, k_heads[:, 14:16].rearrange("p w h k -> p (w h k)"), kC,
                 k_heads[:, 14:16].rearrange("p w h k -> p (w h k)"), kC)
        xm = sb("xm", TOK)
        act = sb("act", SP, SP)
        hor, ver, pyr = sb("hor", S1, S1), sb("ver", S1, S1), sb("pyr", S1, S1)
        hv, py = sb("hv", SIDE, SIDE), sb("py", SIDE, SIDE)
        xs = sb("xs", TOK)
        xe, xo = sb("xe", TOK), sb("xo", TOK)
        fft = sb("fft", 4, TOK)
        fa, fb, fc, fd = (fft[:, k] for k in range(4))
        relu = fb
        edge_half, edge = sb("edge_half", 256), sb("edge", SIDE, SIDE)
        axis_part = sb("axis_part", SIDE, SIDE)
        edge_cut = axis_part
        y_out = sb("y_out", TOK)
        sums = sb("sums", 4)
        vec = sb("vec", 16)
        batt_wide = sb("batt_wide", P)
        route = sb("route", 4, ROUTES)
        cr_scaled = sb("cr_scaled", 3, 9)
        cr_bias = sb("cr_bias", 3)
        mix = sb("mix", 8)

        bank = [ctx.enter_context(nc.psum_tensor(f"bank{i}", [P, HALF], F32)) for i in range(8)]

        loaded = sem("loaded")
        weights_raw_used = sem("weights_raw_used")
        fold_ps = sem("fold_ps")
        folded = sem("folded")
        v_wide_ready = sem("v_wide_ready")
        shift_ps = sem("shift_ps")
        setup_exp = sem("setup_exp")
        setup_z = sem("setup_z")
        zeroed = sem("zeroed")
        onehot_ready = sem("onehot_ready")
        onehot_used = sem("onehot_used")
        rel_ps = sem("rel_ps")
        setup_dve = sem("setup_dve")
        x_loaded = sem("x_loaded")
        stored = sem("stored")
        pool_turns = sem("pool_turns")
        xw_ready = sem("xw_ready")
        xT_ps = sem("xT_ps")
        xT_sb = sem("xT_sb")
        ln1_var = sem("ln1_var")
        ln1_std = sem("ln1_std")
        nT_sb = sem("nT_sb")
        res_sb = sem("res_sb")
        nT_ps = sem("nT_ps")
        nC_sb = sem("nC_sb")
        q_ps = sem("q_ps")
        k_ps = sem("k_ps")
        q_sb = sem("q_sb")
        k_sb = sem("k_sb")
        kh_dve = sem("kh_dve")
        kh_act = sem("kh_act")
        v_ps = sem("v_ps")
        v_sb = sem("v_sb")
        s_ps = sem("s_ps")
        s_biased = sem("s_biased")
        s_max = sem("s_max")
        s_sub = sem("s_sub")
        s_exp = sem("s_exp")
        s_inv = sem("s_inv")
        p_sb = sem("p_sb")
        pT_ps = sem("pT_ps")
        pT_sb = sem("pT_sb")
        o_ps = sem("o_ps")
        o_sb = sem("o_sb")
        proj_ps = sem("proj_ps")
        x1_sb = sem("x1_sb")
        ln2_var = sem("ln2_var")
        ln2_std = sem("ln2_std")
        n2T_sb = sem("n2T_sb")
        n2T_ps = sem("n2T_ps")
        n2C_sb = sem("n2C_sb")
        up_ps = sem("up_ps")
        up_sb = sem("up_sb")
        down_ps = sem("down_ps")
        xm_sb = sem("xm_sb")
        in_ps = sem("in_ps")
        act_sb = sem("act_sb")
        abs_sb = sem("abs_sb")
        gap_sb = sem("gap_sb")
        gap_ps = sem("gap_ps")
        mid_sb = sem("mid_sb")
        mid_ps = sem("mid_ps")
        route_z = sem("route_z")
        route_e = sem("route_e")
        route_d = sem("route_d")
        route_f = sem("route_f")
        cw_sb = sem("cw_sb")
        xs_sb = sem("xs_sb")
        edge_ps = sem("edge_ps")
        edge_sig = sem("edge_sig")
        eb_ps = sem("eb_ps")
        edge_sb = sem("edge_sb")
        pyr_ps = sem("pyr_ps")
        pyr_sb = sem("pyr_sb")
        xe_sb = sem("xe_sb")
        xo_sb = sem("xo_sb")
        x2_ps = sem("x2_ps")
        x2_sb = sem("x2_sb")
        h_ps = sem("h_ps")
        h_sb = sem("h_sb")
        t_ps = sem("t_ps")
        t_sb = sem("t_sb")
        r1_ps = sem("r1_ps")
        r1_sb = sem("r1_sb")
        w_ps = sem("w_ps")
        w_sb = sem("w_sb")
        r2_ps = sem("r2_ps")
        ge_sb = sem("ge_sb")
        go_sb = sem("go_sb")
        axis_sb = sem("axis_sb")
        xm_mixed = sem("xm_mixed")
        pyramid_gated = sem("pyramid_gated")
        cut_sb = sem("cut_sb")
        ae_ps = sem("ae_ps")
        ae_sb = sem("ae_sb")
        ao_ps = sem("ao_ps")
        ao_sb = sem("ao_sb")
        te_ps = sem("te_ps")
        te_sb = sem("te_sb")
        to_ps = sem("to_ps")
        to_sb = sem("to_sb")
        be_ps = sem("be_ps")
        be_sb = sem("be_sb")
        bo_ps = sem("bo_ps")
        bo_sb = sem("bo_sb")
        sq_sb = sem("sq_sb")
        mag_sb = sem("mag_sb")
        hv_sb = sem("hv_sb")
        py_sb = sem("py_sb")
        part_sb = sem("part_sb")
        part_added = sem("part_added")
        gated_sb = sem("gated_sb")
        mixed_sb = sem("mixed_sb")
        relu_sb = sem("relu_sb")
        out_ps = sem("out_ps")
        out_sb = sem("out_sb")

        def grid(ap):
            return ap.rearrange("p (h w) -> p h w", w=SIDE)

        def natural_windows(ap, a):
            return ap.rearrange("p (a r b s) -> p a b r s", a=4, r=WS, b=4)[:, a]

        def windows(ap, a):
            return ap[:, 256 * a:256 * a + 256].rearrange("p (b r s) -> p b r s", b=4, r=WS)

        xs_hw = xs.rearrange("p (w h) -> p h w", w=SIDE)
        act_in = act[:, PAD:PAD + SIDE, PAD:PAD + SIDE]

        DVE_HEADS, ACT_HEADS = range(0, 5), range(5, HEADS)

        def head_mask(h):
            at = CONS["head_mask"][0] + h
            return cons_sb[:, at:at + 1]

        block = ctx.enter_context(nc.Block())
        LOADS = 5
        PYR_TAPS = (0, 0, 2, 3, 4, 4, 5, 6, 7, 9)
        SLOT_TAPS = (1, 2, 4, 6, 7, 8, 9, 10, 11)

        @block.sync
        def _(sp):
            sp.dma_start(cons_sb[:], cons).then_inc(loaded, 16)
            sp.dma_start(mats_sb[:], mats).then_inc(loaded, 16)
            sp.dma_start(cols_sb[:], cols).then_inc(loaded, 16)
            sp.dma_start(rows_sb[:], rows.broadcast_to([P, NROWS])).then_inc(loaded, 16)
            sp.dma_start(k_heads[:, 0:8].rearrange("p a h k -> p (a h k)").bitcast(I32),
                         rel_index.broadcast_to([P, WT * WT])).then_inc(loaded, 16)
            sp.dma_start(x_in[:], x[0]).then_inc(x_loaded, 16)

            def load(i):
                sp.wait_ge(xw_ready, i)
                sp.dma_start(x_in[:], x[i]).then_inc(x_loaded, 16)

            def store(n):
                sp.wait_ge(out_sb, 2 * n + 2)
                sp.dma_start(out[n], y_out[:]).then_inc(stored, 16)

            load(1)
            with sp.Fori(0, IMAGES - 2) as n:
                load(n + 2)
                store(n)
            store(IMAGES - 2)
            store(IMAGES - 1)
            sp.wait_ge(stored, 16 * IMAGES)

        @block.tensor
        def _(pe):
            pe.wait_ge(loaded, 16 * LOADS)
            for k in range(3):
                pe.matmul(bank[0][:, k:k + 1], w_qkv[:, k * C:(k + 1) * C], col("ln1_b"), start=True, stop=True)
            for f in range(FC):
                last = pe.matmul(bank[0][:, 3 + f:4 + f], w_up[:, f * P:(f + 1) * P], col("ln2_b"),
                                 start=True, stop=True)
            last.then_inc(fold_ps, 1)
            pe.wait_ge(v_wide_ready, 1)
            pe.matmul(bank[1][:, 0:P], y_out[:, 0:P], w_proj, start=True, stop=True).then_inc(shift_ps, 1)
            table = mat("table").rearrange("p (c h) -> p c h", c=2)
            oh = [k_heads[:, 8:16].rearrange("p a h k -> p (a h k)"), fft[:].rearrange("p a t -> p (a t)")]
            rel_bank = bank[2].rearrange("p (h k) -> p h k", h=HEADS)
            pe.wait_ge(onehot_ready, 2)
            for key in range(WT):
                for w in range(2):
                    for c in range(2):
                        last = pe.matmul(rel_bank[64 * w:64 * w + 64, :, key], oh[c][:, key * WT:(key + 1) * WT],
                                         table[:, c], start=(c == 0), stop=(c == 1))
            last.then_inc(rel_ps, 1)
            pe.wait_ge(setup_dve, 1)

            def turn4(dst, src, k):
                for c in range(4):
                    at = (4 * k + c) * P
                    last = pe.transpose(dst[:, c * P:(c + 1) * P], src[:, at:at + P], ident)
                return last

            def multiply4(dst, src, k, weights, first=None):
                for c in range(4):
                    at = (4 * k + c) * P
                    rhs = first if first is not None and at == 0 else weights
                    last = pe.matmul(dst[:, c * P:(c + 1) * P], src[:, at:at + P], rhs, start=True, stop=True)
                return last

            nT_flat = nT[:].rearrange("p c d -> p (c d)")

            def x_transposes(i):
                pe.wait_ge(xw_ready, i + 1)
                pe.wait_ge(up_sb, 8 * i)
                pe.wait_ge(xm_sb, 2 * i)
                for k in range(2):
                    turn4(bank[k], xw, k).then_inc(xT_ps, 1)

            def n_transposes(i):
                for k in range(2):
                    pe.wait_ge(nT_sb, 2 * i + k + 1)
                    turn4(bank[2 + k], nT_flat, k).then_inc(nT_ps, 1)

            def queries_keys(i):
                for k in range(2):
                    pe.wait_ge(xT_sb, 2 * i + k + 1)
                    pe.wait_ge(nC_sb, 2 * i + k + 1)
                    pe.matmul(bank[k][:], w_qkv[:, 0:C], nC[:, HALF * k:HALF * k + HALF],
                              start=True, stop=True).then_inc(q_ps, 1)
                for k in range(2):
                    pe.matmul(bank[2 + k][:], w_qkv[:, C:2 * C], nC[:, HALF * k:HALF * k + HALF],
                              start=True, stop=True).then_inc(k_ps, 1)

            def v(i):
                wv = w_qkv[:, 2 * C:3 * C].rearrange("p (g e d) -> p e g d", g=HP, e=2)
                for k in range(2):
                    pe.wait_ge(q_sb, 2 * i + k + 1)
                    for w in range(8):
                        t = nC[:, (8 * k + w) * WT:(8 * k + w + 1) * WT]
                        for e in range(2):
                            last = pe.matmul(bank[k][64 * e:64 * e + 64, w * 64:w * 64 + 64], t, wv[:, e],
                                             start=True, stop=True)
                    last.then_inc(v_ps, 1)

            def scores(i, j):
                if j == 0:
                    pe.wait_ge(kh_dve, i + 1)
                    pe.wait_ge(kh_act, i + 1)
                    pe.wait_ge(q_sb, 2 * i + 2)
                if j < 2:
                    pe.wait_ge(k_sb, 2 * i + j + 1)
                else:
                    pe.wait_ge(s_biased, 8 * i + j - 1)
                for e in range(2):
                    w = 2 * j + e
                    last = pe.matmul(bank[2 + j % 2][64 * e:64 * e + 64, :], qC[:, w * WT:(w + 1) * WT],
                                     k_heads[:, w].rearrange("p h k -> p (h k)"), start=True, stop=True)
                last.then_inc(s_ps, 1)

            def prob_transposes(i, j):
                pe.wait_ge(p_sb, 8 * i + j + 1)
                if j == 0:
                    pe.wait_ge(v_sb, 2 * i + 2)
                else:
                    pe.wait_ge(pT_sb, 8 * i + j)
                for g in range(HP):
                    last = pe.transpose(bank[0][:, g * P:(g + 1) * P], prob[:, j % 2, g * P:(g + 1) * P], ident)
                last.then_inc(pT_ps, 1)

            def values(i, j):
                pe.wait_ge(pT_sb, 8 * i + j + 1)
                if j == 4:
                    pe.wait_ge(o_sb, 2 * i + 1)
                for e in range(2):
                    w = 2 * j + e
                    for g in range(HP):
                        last = pe.matmul(bank[1][32 * g:32 * g + 32, (w % 8) * WT:(w % 8 + 1) * WT],
                                         v_pair[:, w, g].rearrange("p e d -> p (e d)"),
                                         probT[:, j % 2, g, e * WT:(e + 1) * WT], start=True, stop=True)
                last.then_inc(o_ps, 1)

            def project(i, k):
                pe.wait_ge(o_sb, 2 * i + k + 1)
                pe.wait_ge(s_biased, 8 * i + 7 + k)
                multiply4(bank[2 + k], attn_out, k, w_proj).then_inc(proj_ps, 1)

            def n2_transposes(i, k):
                pe.wait_ge(n2T_sb, 2 * i + k + 1)
                pe.wait_ge(pT_sb, 8 * i + 8)
                pe.wait_ge(o_sb, 2 * i + 2)
                turn4(bank[k], nT_flat, k).then_inc(n2T_ps, 1)

            def mlp(i):
                def up(t):
                    k, f = divmod(t, FC)
                    b = (2, 3, 0, 1, 2, 3, 1, 2)[t]
                    if t < 2:
                        pe.wait_ge(x1_sb, 2 * i + t + 1)
                    elif t < 4:
                        pe.wait_ge(n2C_sb, 2 * i + t - 1)
                    else:
                        pe.wait_ge(up_sb, 8 * i + (1, 2, 4, 5)[t - 4])
                    pe.wait_ge(n2C_sb, 2 * i + k + 1)
                    pe.matmul(bank[b][:], w_up[:, f * P:(f + 1) * P], nC[:, HALF * k:HALF * k + HALF],
                              start=True, stop=True).then_inc(up_ps, 1)

                def down(k):
                    b = (0, 3)[k]
                    pe.wait_ge(up_sb, 8 * i + 4 + 4 * k)
                    for c in range(4):
                        pe.matmul(bank[b][:, c * P:(c + 1) * P], x1T[:, 4 * k + c], ident, is_transpose=True,
                                  start=(c == 0), stop=False)
                    for f in range(FC):
                        last = pe.matmul(bank[b][:], w_down[:, f * P:(f + 1) * P],
                                         hidden[:, f, HALF * k:HALF * k + HALF], start=False, stop=(f == FC - 1))
                    last.then_inc(down_ps, 1)

                for t in range(3):
                    up(t)
                n2_transposes(i, 1)
                for t in range(3, 6):
                    up(t)
                down(0)
                up(6)
                up(7)
                down(1)

            def in_conv(n):
                for k in range(2):
                    pe.wait_ge(xm_sb, 2 * n + k + 1)
                    pe.wait_ge(bo_sb, 2 * n)
                    pe.matmul(bank[4 + k][:], mat("in"), xm[:, HALF * k:HALF * k + HALF],
                              start=True, stop=True).then_inc(in_ps, 1)

            def tap(rows0, nrows, dil, t):
                y, x_ = rows0 + PAD + (t // 3 - 1) * dil, PAD + (t % 3 - 1) * dil
                return act[:, y:y + nrows, x_:x_ + SIDE]

            def edge_conv(n):
                pe.wait_ge(act_sb, 2 * n + 2)
                pe.wait_ge(out_sb, 2 * n)
                for t in range(9):
                    for q in range(4):
                        last = pe.matmul(bank[7][32 * q:32 * q + 32, 0:256], w_vis[:, t], tap(8 * q, 8, 1, t),
                                         start=(t == 0), stop=(t == 8))
                last.then_inc(edge_ps, 1)

            def gap_products(n):
                pe.wait_ge(gap_sb, n + 1)
                pe.matmul(bank[6][:, 0:1], mat("fac"), vec[:, 0:1], start=True, stop=True)
                pe.matmul(bank[6][0:BATT, 1:2], mat("batt1"), vec[:, 0:1], start=True, stop=True)\
                  .then_inc(gap_ps, 1)

            def mid_products(n):
                pe.wait_ge(mid_sb, n + 1)
                pe.matmul(bank[6][:, 2:3], mat("conv"), vec[:, 5:6], start=True, stop=True)
                pe.matmul(bank[6][:, 8:8 + ROUTES], batt_wide[0:BATT, :], mat("batt2")[0:BATT], start=True,
                          stop=True).then_inc(mid_ps, 1)

            def edge_spread(n):
                sel = con("sel").rearrange("p (q m) -> p q m", q=4)
                pe.wait_ge(edge_sig, n + 1)
                pe.wait_ge(route_z, n + 1)
                pe.wait_ge(xs_sb, n + 1)
                for k in range(2):
                    for q in range(2):
                        last = pe.matmul(bank[6 + k][:, 256 * q:256 * q + 256], sel[:, 2 * k + q], edge_half[:],
                                         start=True, stop=True)
                    last.then_inc(eb_ps, 1)

            def pyramid(n, k, taps):
                pe.wait_ge(act_sb, 2 * n + 2)
                for t in taps:
                    for d, dil in enumerate(DILS):
                        last = pe.matmul(bank[4 + k][32 * d:32 * d + 32, :], w_pyr[:, d, t], tap(16 * k, 16, dil, t),
                                         start=(t == 0), stop=(t == 8))
                if taps[-1] == 8:
                    last.then_inc(pyr_ps, 1)

            def x2_conv(n):
                for k in range(2):
                    pe.wait_ge(edge_sb, 2 * n + k + 1)
                    pe.wait_ge(xs_sb, n + 1)
                    multiply4(bank[6 + k], xs, k, mat("fgm2")).then_inc(x2_ps, 1)

            def dft_rows(n):
                for k in range(2):
                    pe.wait_ge(x2_sb, 2 * n + k + 1)
                    pe.wait_ge(pyr_sb, 2 * n + k + 1)
                    multiply4(bank[4 + k], fa, k, con("dft_h")).then_inc(h_ps, 1)

            def turn_spectrum(n):
                for k in range(2):
                    pe.wait_ge(h_sb, 2 * n + 2)
                    turn4(bank[6 + k], fb, k).then_inc(t_ps, 1)

            def r_even(n):
                for k in range(2):
                    pe.wait_ge(xe_sb, n + 1)
                    pe.wait_ge(h_sb, 2 * n + k + 1)
                    multiply4(bank[4 + k], xe, k, mat("fgm1")).then_inc(r1_ps, 1)

            def dft_columns(n):
                for k in range(2):
                    pe.wait_ge(t_sb, 2 * n + k + 1)
                    if k == 0:
                        pe.matmul(bank[6][:, 0:P], con("dft_w0"), fa[:, 0:P], start=True, stop=True)
                        last = pe.matmul(bank[6][:, P:4 * P], con("dft_w"), fa[:, P:4 * P], start=True, stop=True)
                    else:
                        last = pe.matmul(bank[7][:], con("dft_w"), fa[:, 4 * P:8 * P], start=True, stop=True)
                    last.then_inc(w_ps, 1)

            def r_odd(n):
                for k in range(2):
                    pe.wait_ge(xo_sb, n + 1)
                    pe.wait_ge(r1_sb, 2 * n + k + 1)
                    multiply4(bank[4 + k], xo, k, mat("fgm1")).then_inc(r2_ps, 1)

            def inverse_even(n):
                for k in range(2):
                    pe.wait_ge(ge_sb, n + 1)
                    pe.wait_ge(w_sb, 2 * n + 2)
                    multiply4(bank[6 + k], fc, k, con("even"), con("even0")).then_inc(ae_ps, 1)

            def inverse_odd(n):
                for k in range(2):
                    pe.wait_ge(go_sb, 2 * n + k + 1)
                    multiply4(bank[4 + k], fd, k, con("odd"), con("odd0")).then_inc(ao_ps, 1)

            def turn_even(n):
                for k in range(2):
                    pe.wait_ge(ae_sb, 2 * n + 2)
                    turn4(bank[6 + k], fa, k).then_inc(te_ps, 1)

            def turn_odd(n):
                for k in range(2):
                    pe.wait_ge(ao_sb, 2 * n + 2)
                    turn4(bank[4 + k], fb, k).then_inc(to_ps, 1)

            def last_even(n):
                for k in range(2):
                    pe.wait_ge(te_sb, 2 * n + k + 1)
                    multiply4(bank[6 + k], fc, k, con("idft_h")).then_inc(be_ps, 1)

            def last_odd(n):
                for k in range(2):
                    pe.wait_ge(to_sb, 2 * n + k + 1)
                    multiply4(bank[4 + k], fd, k, con("idft_h")).then_inc(bo_ps, 1)

            def out_conv(n):
                for k in range(2):
                    pe.wait_ge(relu_sb, n + 1)
                    pe.wait_ge(be_sb, 2 * n + k + 1)
                    pe.matmul(bank[6 + k][:], mat("out"), relu[:, HALF * k:HALF * k + HALF],
                              start=True, stop=True).then_inc(out_ps, 1)

            def conv_early(n, j):
                if j == 0:
                    pyramid(n, 1, range(0, 4))
                elif j == 1:
                    pyramid(n, 1, range(4, 9))
                elif j == 2:
                    dft_rows(n)
                elif j == 3:
                    r_even(n)
                elif j == 4:
                    r_odd(n)
                elif j == 6:
                    inverse_odd(n)
                elif j == 7:
                    turn_odd(n)

            def conv_late(n, j):
                if j == 1:
                    x2_conv(n)
                elif j == 2:
                    turn_spectrum(n)
                elif j == 3:
                    dft_columns(n)
                elif j == 5:
                    inverse_even(n)
                elif j == 6:
                    turn_even(n)
                elif j == 7:
                    last_even(n)

            def swin_only(i):
                x_transposes(i)
                n_transposes(i)
                queries_keys(i)
                v(i)
                scores(i, 0)
                scores(i, 1)
                for j in range(PAIRS):
                    if j + 2 < PAIRS:
                        scores(i, j + 2)
                    prob_transposes(i, j)
                    values(i, j)
                project(i, 0)
                project(i, 1)
                n2_transposes(i, 0)
                mlp(i)

            def both(n, i):
                in_conv(n)
                x_transposes(i)
                edge_conv(n)
                gap_products(n)
                pyramid(n, 0, range(0, 3))
                n_transposes(i)
                mid_products(n)
                queries_keys(i)
                edge_spread(n)
                v(i)
                scores(i, 0)
                scores(i, 1)
                pyramid(n, 0, range(3, 9))
                for j in range(PAIRS):
                    if j == PAIRS - 1:
                        project(i, 0)
                    if j + 2 < PAIRS:
                        scores(i, j + 2)
                    conv_early(n, j)
                    prob_transposes(i, j)
                    conv_late(n, j)
                    values(i, j)
                last_odd(n)
                project(i, 1)
                n2_transposes(i, 0)
                mlp(i)
                out_conv(n)

            def conv_only(n):
                in_conv(n)
                edge_conv(n)
                gap_products(n)
                pyramid(n, 0, range(0, 9))
                mid_products(n)
                edge_spread(n)
                for j in range(PAIRS):
                    conv_early(n, j)
                    conv_late(n, j)
                last_odd(n)
                out_conv(n)

            swin_only(0)
            both(0, 1)
            with pe.Fori(1, IMAGES - 1) as n:
                both(n, n + 1)
            conv_only(IMAGES - 1)

        @block.vector
        def _(dve):
            dve.memset(ones[:], 1.0)
            dve.memset(eps[:], LN_EPS)
            dve.memset(cut_bias[:], 1.3)
            dve.memset(y_out[:, P:2 * P], 0.0)
            dve.wait_ge(loaded, 16 * LOADS)
            index = k_heads[:, 0:8].rearrange("p a h k -> p (a h k)").bitcast(I32)
            oh = [k_heads[:, 8:16].rearrange("p a h k -> p (a h k)"), fft[:].rearrange("p a t -> p (a t)")]
            for c in range(2):
                at = CONS["iota"][0] + c
                dve.tensor_scalar(oh[c], index, cons_sb[:, at:at + 1], None, ALU.is_equal)\
                   .then_inc(onehot_ready, 1)
            dve.tensor_copy(w_vis[:], mat("vis").unsqueeze(2).broadcast_to([P, 9, 32]))
            dve.tensor_scalar(fuse_bias[:], col("pyr_b"), col("fuse_w"), col("fuse_b"), ALU.mult, ALU.add)
            dve.tensor_scalar(two_b1[:], row("fgm_b1"), 2.0, None, ALU.mult)
            dve.tensor_scalar(dc_b2[:], row("fgm_b2"), float(TOK), None, ALU.mult)
            for g in range(CH):
                at = CONS["high"][0] + g
                dve.tensor_scalar(boost[:, g], row("boost"), cons_sb[:, at:at + 1], 1.0, ALU.mult, ALU.add)
            dve.tensor_reduce(tiny[:, 0:1], row("base"), AX.X, ALU.max)
            dve.drain()
            dve.tensor_scalar(base[:], row("base"), tiny[:, 0:1], None, ALU.subtract).then_inc(setup_z, 1)
            dve.wait_ge(fold_ps, 1)
            scale = float(HD) ** -0.5
            dve.tensor_scalar(fold_b[:, 0:1], bank[0][:, 0:1], col("q_b"), scale, ALU.add, ALU.mult)
            dve.tensor_scalar(fold_b[:, 1:2], bank[0][:, 1:2], col("k_b"), None, ALU.add)
            dve.tensor_scalar(fold_b[:, 2:3], bank[0][:, 2:3], col("v_b"), None, ALU.add)
            dve.tensor_tensor(fold_b[:, 3:3 + FC], bank[0][:, 3:3 + FC],
                              cols_sb[:, COLS["b1"][0]:COLS["b1"][0] + FC], ALU.add)
            dve.drain()
            dve.tensor_scalar(y_out[:, 0:P], ones[:], fold_b[:, 2:3], None, ALU.mult)\
               .then_inc(v_wide_ready, 1)
            dve.tensor_scalar(w_qkv[:, 0:C], w_qkv[:, 0:C], col("ln1_g"), scale, ALU.mult, ALU.mult)
            dve.tensor_scalar(w_qkv[:, C:3 * C], w_qkv[:, C:3 * C], col("ln1_g"), None, ALU.mult)
            dve.tensor_scalar(w_up, w_up, col("ln2_g"), None, ALU.mult)
            dve.wait_ge(setup_exp, 1)
            dve.tensor_reduce(tiny[:, 1:2], base[:], AX.X, ALU.add)
            dve.drain()
            dve.reciprocal(tiny[:, 2:3], tiny[:, 1:2])
            dve.drain()
            dve.tensor_scalar(base[:], base[:], tiny[:, 2:3], None, ALU.mult)
            dve.wait_ge(shift_ps, 1)
            dve.tensor_tensor(proj_shift[:], bank[1][:, 0:P], row("proj_b"), ALU.add)
            dve.wait_ge(rel_ps, 1)
            dve.tensor_copy(rel_bias[:], bank[2][:])
            dve.drain()
            dve.sem_inc(setup_dve, 1)

            def norm_stats(source, done, chunks=range(CH)):
                for c in chunks:
                    dve.bn_stats(stats[:, c], source(c))
                dve.drain()
                for c in chunks:
                    last = dve.bn_aggr(mv[:, c], stats[:, c])
                last.then_inc(done, 1)

            def normalise(source, done, chunks=range(CH)):
                part = slice(chunks[0], chunks[-1] + 1)
                dve.reciprocal(rstd[:, part], std[:, part])
                dve.drain()
                for c in chunks:
                    last = dve.tensor_scalar(nT[:, c], source[:, c], mv[:, c, 0:1], rstd[:, c:c + 1],
                                             ALU.subtract, ALU.mult)
                    if c % 4 == 3:
                        last.then_inc(done, 1)

            def norm1_stats(i):
                dve.wait_ge(xT_sb, 2 * i + 2)
                norm_stats(lambda c: xT[:, c], ln1_var)

            def norm1(i):
                dve.wait_ge(ln1_std, i + 1)
                dve.wait_ge(xT_sb, 2 * i + 2)
                dve.wait_ge(n2T_ps, 2 * i)
                normalise(xT, nT_sb)

            def keys(i):
                for k in range(2):
                    dve.wait_ge(k_ps, 2 * i + k + 1)
                    dve.wait_ge(kh_act, i)
                    dve.tensor_scalar(kC[:, HALF * k:HALF * k + HALF], bank[2 + k][:], fold_b[:, 1:2], None,
                                      ALU.add).then_inc(k_sb, 1)

            def key_heads(i):
                dve.drain()
                dve.wait_ge(down_ps, 2 * i)
                for h in DVE_HEADS:
                    last = dve.tensor_scalar(k_heads[:, :, h], kC.rearrange("p (w k) -> p w k", w=WIN),
                                             head_mask(h), None, ALU.mult)
                last.then_inc(kh_dve, 1)

            def bias_max(i, j):
                dve.wait_ge(s_ps, 8 * i + j + 1)
                if j >= 3:
                    dve.wait_ge(p_sb, 8 * i + j - 2)
                dve.tensor_tensor(score[:, j % 3].rearrange("p h k -> p (h k)"), bank[2 + j % 2][:], rel_bias[:],
                                  ALU.add).then_inc(s_biased, 1)
                dve.drain()
                dve.tensor_reduce(row_max[:, j % 3], score[:, j % 3], AX.X, ALU.max).then_inc(s_max, 1)

            def row_sums(i, j):
                dve.wait_ge(s_exp, 8 * i + j + 1)
                dve.tensor_reduce(row_sum[:, j % 3], score[:, j % 3], AX.X, ALU.add)
                dve.drain()
                dve.reciprocal(row_inv[:, j % 3], row_sum[:, j % 3]).then_inc(s_inv, 1)

            def residual_stats(i, k):
                dve.wait_ge(proj_ps, 2 * i + k + 1)
                dve.wait_ge(res_sb, i + 1)
                dve.tensor_tensor(x1T[:, 4 * k:4 * k + 4].rearrange("p c d -> p (c d)"), bank[2 + k][:],
                                  resT[:, 4 * k:4 * k + 4].rearrange("p c d -> p (c d)"), ALU.add)\
                   .then_inc(x1_sb, 1)
                dve.drain()
                norm_stats(lambda c: x1T[:, c], ln2_var, range(4 * k, 4 * k + 4))

            def norm2(i, k):
                dve.wait_ge(ln2_std, 2 * i + k + 1)
                normalise(x1T, n2T_sb, range(4 * k, 4 * k + 4))

            def swin_out(i, k):
                dve.wait_ge(down_ps, 2 * i + k + 1)
                dve.wait_ge(in_ps, 2 * i)
                dve.wait_ge(pyramid_gated, i)
                for a in range(2):
                    last = dve.tensor_scalar(natural_windows(xm[:], 2 * k + a), windows(bank[(0, 3)[k]][:], a),
                                             col("b2"), None, ALU.add)
                last.then_inc(xm_sb, 1)

            def gap(n):
                dve.wait_ge(act_sb, 2 * n + 2)
                dve.tensor_scalar(vec[:, 0:1], sums[:, 0:1], sums[:, 1:2], 1.0 / TOK, ALU.add, ALU.mult)\
                   .then_inc(gap_sb, 1)

            def attention_vectors(n):
                dve.wait_ge(gap_ps, n + 1)
                dve.wait_ge(abs_sb, n + 1)
                dve.tensor_scalar(vec[:, 1:2], bank[6][:, 0:1], col("fac_b"), None, ALU.add)
                dve.tensor_scalar(vec[0:BATT, 4:5], bank[6][0:BATT, 1:2], col("batt_b1")[0:BATT], 0.0,
                                  ALU.add, ALU.max)
                dve.drain()
                dve.tensor_scalar(vec[:, 2:3], vec[:, 1:2], -1.0, None, ALU.mult)
                dve.tensor_scalar(batt_wide[0:BATT], ones[0:BATT], vec[0:BATT, 4:5], None, ALU.mult)
                dve.drain()
                dve.tensor_tensor(vec[:, 3:4], vec[:, 1:2], vec[:, 2:3], ALU.max)
                dve.drain()
                dve.tensor_scalar(vec[:, 5:6], sums[:, 2:3], vec[:, 3:4], 1.0 / TOK, ALU.mult, ALU.mult)\
                   .then_inc(mid_sb, 1)

            def scaled_input(n):
                dve.wait_ge(mid_ps, n + 1)
                dve.tensor_tensor(route[:, 0], bank[6][:, 8:8 + ROUTES], row("batt_b2"), ALU.add)\
                   .then_inc(route_z, 1)
                dve.tensor_scalar(vec[:, 6:7], bank[6][:, 2:3], col("conv_b"), vec[:, 3:4], ALU.add, ALU.mult)
                dve.drain()
                dve.tensor_scalar(xs[:], xs[:], vec[:, 6:7], None, ALU.mult).then_inc(xs_sb, 1)

            def route_logits(n):
                dve.wait_ge(route_e, n + 1)
                dve.tensor_tensor(route[:, 2], route[:, 1], base[:], ALU.mult)
                dve.drain()
                dve.tensor_reduce(vec[:, 7:8], route[:, 2], AX.X, ALU.max)
                dve.drain()
                dve.tensor_scalar(route[:, 0], route[:, 2], vec[:, 7:8], None, ALU.subtract)\
                   .then_inc(route_d, 1)

            def route_weights(n):
                dve.wait_ge(route_f, n + 1)
                dve.tensor_reduce(vec[:, 8:9], route[:, 1], AX.X, ALU.add)
                dve.drain()
                dve.reciprocal(vec[:, 9:10], vec[:, 8:9])
                dve.drain()
                cw = route[:, 3]
                dve.tensor_scalar(cw, route[:, 1], vec[:, 9:10], None, ALU.mult)
                dve.drain()
                dve.wait_ge(py_sb, n)
                at = COLS["cr_w"][0]
                dve.tensor_tensor(cr_scaled[:], cols_sb[:, at:at + 27].rearrange("p (a t) -> p a t", a=3),
                                  cw[:, 0:3].unsqueeze(2).broadcast_to([P, 3, 9]), ALU.mult)
                at = COLS["cr_b"][0]
                dve.tensor_tensor(cr_bias[:], cols_sb[:, at:at + 3], cw[:, 0:3], ALU.mult)
                dve.tensor_tensor(mix[:, 0:1], col("dw_w"), cw[:, 3:4], ALU.mult)
                dve.tensor_tensor(mix[:, 1:2], col("dw_b"), cw[:, 3:4], ALU.mult)
                dve.tensor_tensor(mix[:, 2:3], col("alpha"), cw[:, 4:5], ALU.mult)
                dve.tensor_tensor(mix[:, 3:4], col("beta"), cw[:, 4:5], ALU.mult)
                dve.drain()
                dve.tensor_tensor(mix[:, 4:5], cr_bias[:, 0:1], cr_bias[:, 1:2], ALU.add).then_inc(cw_sb, 1)

            def taps(n, which):
                for t in which:
                    a, k = divmod(t, 9)
                    src = (hor, ver)[a][:, k // 3:k // 3 + SIDE, k % 3:k % 3 + SIDE]
                    dve.drain()
                    if t == 9:
                        dve.wait_ge(axis_sb, 2 * n + 2)
                    if t == 0:
                        dve.wait_ge(axis_sb, 2 * n + 1)
                        dve.wait_ge(relu_sb, n)
                        last = dve.tensor_scalar(hv[:], src, cr_scaled[:, a, k:k + 1], mix[:, 4:5], ALU.mult, ALU.add)
                    else:
                        last = dve.scalar_tensor_tensor(hv[:], src, cr_scaled[:, a, k:k + 1], hv[:], ALU.mult,
                                                        ALU.add)
                    if t == 17:
                        last.then_inc(hv_sb, 1)

            def boosted(n):
                for k in range(2):
                    dve.wait_ge(w_ps, 2 * n + k + 1)
                    dve.wait_ge(t_ps, 2 * n + 2)
                    last = dve.tensor_tensor(fb[:, HALF * k:HALF * k + HALF], bank[6 + k][:],
                                             boost[:, 4 * k:4 * k + 4].rearrange("p g c -> p (g c)"), ALU.mult)
                last.then_inc(w_sb, 1)
                dve.drain()
                dve.tensor_tensor(fb[0:1, 0:C], fb[0:1, 0:C], dc_b2[0:1], ALU.add).then_inc(w_sb, 1)

            def odd_product(n):
                dve.drain()
                for k in range(2):
                    h = slice(HALF * k, HALF * k + HALF)
                    dve.wait_ge(r2_ps, 2 * n + k + 1)
                    dve.tensor_tensor(fd[:, h], bank[4 + k][:], fb[:, h], ALU.mult).then_inc(go_sb, 1)

            def mix_input(n):
                dve.wait_ge(abs_sb, n + 1)
                dve.scalar_tensor_tensor(grid(xm[:]), act_in, mix[:, 0:1], grid(xm[:]), ALU.mult, ALU.add)
                dve.drain()
                dve.scalar_tensor_tensor(grid(xm[:]), xs_hw, mix[:, 3:4], grid(xm[:]), ALU.mult, ALU.add)\
                   .then_inc(xm_mixed, 1)

            def mixture(n):
                dve.wait_ge(gated_sb, n + 1)
                dve.wait_ge(mag_sb, n + 1)
                dve.scalar_tensor_tensor(hv[:], grid(fa), mix[:, 2:3], hv[:], ALU.mult, ALU.add)\
                   .then_inc(mixed_sb, 1)

            def conv_slot(n, j):
                if j == 4:
                    boosted(n)
                    odd_product(n)
                taps(n, range(SLOT_TAPS[j], SLOT_TAPS[j + 1]))

            def swin_only(i):
                norm1_stats(i)
                norm1(i)
                keys(i)
                key_heads(i)
                bias_max(i, 0)
                bias_max(i, 1)
                for j in range(PAIRS):
                    row_sums(i, j)
                    if j + 2 < PAIRS:
                        bias_max(i, j + 2)
                residual_stats(i, 0)
                norm2(i, 0)
                residual_stats(i, 1)
                norm2(i, 1)
                swin_out(i, 0)
                swin_out(i, 1)

            def both(n, i):
                gap(n)
                norm1_stats(i)
                attention_vectors(n)
                norm1(i)
                scaled_input(n)
                keys(i)
                key_heads(i)
                route_logits(n)
                route_weights(n)
                mix_input(n)
                taps(n, range(0, SLOT_TAPS[0]))
                bias_max(i, 0)
                bias_max(i, 1)
                for j in range(PAIRS):
                    row_sums(i, j)
                    if j + 2 < PAIRS:
                        bias_max(i, j + 2)
                    conv_slot(n, j)
                residual_stats(i, 0)
                norm2(i, 0)
                residual_stats(i, 1)
                norm2(i, 1)
                taps(n, range(SLOT_TAPS[PAIRS], 18))
                swin_out(i, 0)
                mixture(n)
                swin_out(i, 1)

            def conv_only(n):
                gap(n)
                attention_vectors(n)
                scaled_input(n)
                route_logits(n)
                route_weights(n)
                mix_input(n)
                taps(n, range(0, SLOT_TAPS[0]))
                for j in range(PAIRS):
                    conv_slot(n, j)
                taps(n, range(SLOT_TAPS[PAIRS], 18))
                mixture(n)

            swin_only(0)
            both(0, 1)
            with dve.Fori(1, IMAGES - 1) as n:
                both(n, n + 1)
            conv_only(IMAGES - 1)

        @block.scalar
        def _(act_):
            act_.wait_ge(setup_z, 1)
            act_.activation(base[:], base[:], ACT.Exp).then_inc(setup_exp, 1)
            act_.wait_ge(setup_dve, 1)
            act_.wait_ge(zeroed, 1)

            def to_windows(i):
                act_.wait_ge(x_loaded, 16 * i + 16)
                act_.wait_ge(proj_ps, 2 * i)
                for a in range(4):
                    last = act_.activation(windows(xw[:], a), natural_windows(x_in[:], a), ACT.Copy)
                last.then_inc(xw_ready, 1)

            def x_copy(i):
                for k in range(2):
                    act_.wait_ge(xT_ps, 2 * i + k + 1)
                    act_.wait_ge(down_ps, 2 * i)
                    act_.activation(xT[:, 4 * k:4 * k + 4].rearrange("p c d -> p (c d)"), bank[k][:], ACT.Copy)\
                        .then_inc(xT_sb, 1)

            def deviation1(i):
                act_.wait_ge(ln1_var, i + 1)
                act_.activation(std[:], mv[:, :, 1], ACT.Sqrt, bias=eps[:]).then_inc(ln1_std, 1)

            def deviation2(i, k):
                act_.wait_ge(ln2_var, 2 * i + k + 1)
                act_.activation(std[:, 4 * k:4 * k + 4], mv[:, 4 * k:4 * k + 4, 1], ACT.Sqrt, bias=eps[:])\
                    .then_inc(ln2_std, 1)

            def copy(dst, src):
                return act_.activation(dst, src, ACT.Copy)

            def half(ap, k):
                return ap[:, HALF * k:HALF * k + HALF]

            def n_copy(i):
                for k in range(2):
                    act_.wait_ge(nT_ps, 2 * i + k + 1)
                    copy(half(nC, k), bank[2 + k][:]).then_inc(nC_sb, 1)

            def n2_copy(i, k):
                act_.wait_ge(n2T_ps, 2 * i + k + 1)
                copy(half(nC, k), bank[k][:]).then_inc(n2C_sb, 1)

            def queries(i):
                for k in range(2):
                    act_.wait_ge(q_ps, 2 * i + k + 1)
                    act_.activation(qC[:, HALF * k:HALF * k + HALF], bank[k][:], ACT.Identity, bias=fold_b[:, 0:1])\
                        .then_inc(q_sb, 1)

            def key_heads(i):
                act_.wait_ge(k_sb, 2 * i + 2)
                act_.wait_ge(down_ps, 2 * i)
                for h in ACT_HEADS:
                    last = act_.activation(k_heads[:, :, h], kC.rearrange("p (w k) -> p w k", w=WIN), ACT.Copy,
                                           scale=head_mask(h))
                last.then_inc(kh_act, 1)

            def v_copy(i):
                for k in range(2):
                    act_.wait_ge(v_ps, 2 * i + k + 1)
                    for e in range(2):
                        dst = v_pair[64 * e:64 * e + 64, 8 * k:8 * k + 8, :, e].rearrange("p w g d -> p (w g) d")
                        src = bank[k][64 * e:64 * e + 64, :].rearrange("p (w d) -> p w d", d=HD)
                        last = act_.activation(dst, src, ACT.Copy)
                    last.then_inc(v_sb, 1)

            def exponent(i, j):
                act_.wait_ge(s_sub, 8 * i + j + 1)
                act_.activation(score[:, j % 3].rearrange("p h k -> p (h k)"),
                                score[:, j % 3].rearrange("p h k -> p (h k)"), ACT.Exp).then_inc(s_exp, 1)

            def prob_copy(i, j):
                act_.wait_ge(pT_ps, 8 * i + j + 1)
                act_.activation(probT[:, j % 2].rearrange("p g t -> p (g t)"), bank[0][:], ACT.Copy)\
                    .then_inc(pT_sb, 1)

            def attention_copy(i, k):
                act_.wait_ge(o_ps, 8 * i + 4 * k + 4)
                act_.activation(attn_out[:, HALF * k:HALF * k + HALF], bank[1][:], ACT.Copy).then_inc(o_sb, 1)

            def mlp_gelu(i):
                act_.activation(first_gelu[:], ones[:, 0:1], ACT.Gelu)
                for t in range(2 * FC):
                    k, f = divmod(t, FC)
                    act_.wait_ge(up_ps, 8 * i + t + 1)
                    act_.activation(hidden[:, f, HALF * k:HALF * k + HALF], bank[(2, 3, 0, 1, 2, 3, 1, 2)[t]][:],
                                    ACT.Gelu, bias=fold_b[:, 3 + f:4 + f]).then_inc(up_sb, 1)

            def in_gelu(n):
                for k in range(2):
                    act_.wait_ge(in_ps, 2 * n + k + 1)
                    act_.activation(act[:, PAD + 16 * k:PAD + 16 * k + 16, PAD:PAD + SIDE],
                                    bank[4 + k].rearrange("p (h w) -> p h w", w=SIDE), ACT.Gelu, bias=col("in_b"),
                                    accum_out=sums[:, k:k + 1]).then_inc(act_sb, 1)

            def magnitudes(n):
                act_.drain()
                act_.wait_ge(mixed_sb, n)
                act_.activation(xs_hw, act_in, ACT.Abs, accum_out=sums[:, 2:3]).then_inc(abs_sb, 1)

            def edge_sigmoid(n):
                act_.wait_ge(edge_ps, n + 1)
                act_.activation(edge_half[:], bank[7][:, 0:256], ACT.Sigmoid, bias=col("vis_b"))\
                    .then_inc(edge_sig, 1)

            def route_sigmoid(n):
                act_.wait_ge(route_z, n + 1)
                act_.activation(route[:, 1], route[:, 0], ACT.Sigmoid).then_inc(route_e, 1)

            def route_exponent(n):
                act_.wait_ge(route_d, n + 1)
                act_.activation(route[:, 1], route[:, 0], ACT.Exp).then_inc(route_f, 1)

            def edge_copy(n):
                for k in range(2):
                    act_.wait_ge(eb_ps, 2 * n + k + 1)
                    act_.wait_ge(gated_sb, n)
                    act_.activation(edge[:, 16 * k:16 * k + 16], bank[6 + k].rearrange("p (h w) -> p h w", w=SIDE),
                                    ACT.Identity, bias=ones[:, 0:1]).then_inc(edge_sb, 1)

            def edge_cuts(n):
                act_.drain()
                act_.wait_ge(axis_sb, 2 * n + 2)
                act_.activation(edge_cut[:], edge[:], ACT.Identity, bias=cut_bias[:], scale=-0.3).then_inc(cut_sb, 1)

            def pyr_copy(n, k):
                act_.wait_ge(pyr_ps, 2 * n + k + 1)
                act_.wait_ge(py_sb, n)
                act_.activation(pyr[:, 1 + 16 * k:17 + 16 * k, 1:1 + SIDE],
                                bank[4 + k].rearrange("p (h w) -> p h w", w=SIDE), ACT.Identity, bias=fuse_bias[:],
                                scale=col("fuse_w")).then_inc(pyr_sb, 1)

            def pyr_tap(n, k):
                src = pyr[:, k // 3:k // 3 + SIDE, k % 3:k % 3 + SIDE]
                if k == 0:
                    act_.drain()
                    act_.wait_ge(gated_sb, n)
                    act_.wait_ge(cw_sb, n + 1)
                    act_.activation(py[:], src, ACT.Identity, bias=cr_bias[:, 2:3], scale=cr_scaled[:, 2, 0:1])\
                        .then_inc(part_sb, 1)
                    return
                if k > 2:
                    act_.wait_ge(part_added, 8 * n + k - 2)
                act_.activation(grid(parts[k][:, 0:TOK]), src, ACT.Copy, scale=cr_scaled[:, 2, k:k + 1])\
                    .then_inc(part_sb, 1)

            def other_order(dst, k):
                return dst.rearrange("c (a b) -> c b a", b=SIDE)[:, 16 * k:16 * k + 16]

            def rows_of(ps):
                return ps.rearrange("c (b a) -> c b a", a=SIDE)

            def square(dst, ps, k):
                to = dst.rearrange("c (h j w) -> c j h w", j=CH, w=4)[:, 4 * k:4 * k + 4]
                return act_.activation(to, ps.rearrange("c (j h w) -> c j h w", j=4, w=4), ACT.Square)

            def x2_copy(n):
                for k in range(2):
                    act_.wait_ge(x2_ps, 2 * n + k + 1)
                    copy(half(fa, k), bank[6 + k][:]).then_inc(x2_sb, 1)

            def row_spectrum_copy(n):
                for k in range(2):
                    act_.wait_ge(h_ps, 2 * n + k + 1)
                    copy(other_order(fb, k), rows_of(bank[4 + k])).then_inc(h_sb, 1)

            def spectrum_turn_copy(n):
                for k in range(2):
                    act_.wait_ge(t_ps, 2 * n + k + 1)
                    copy(half(fa, k), bank[6 + k][:]).then_inc(t_sb, 1)

            def r_even_copy(n):
                for k in range(2):
                    act_.wait_ge(r1_ps, 2 * n + k + 1)
                    copy(half(fc, k), bank[4 + k][:]).then_inc(r1_sb, 1)

            def inverse_even_copy(n):
                for k in range(2):
                    act_.wait_ge(ae_ps, 2 * n + k + 1)
                    copy(other_order(fa, k), rows_of(bank[6 + k])).then_inc(ae_sb, 1)

            def inverse_odd_copy(n):
                act_.wait_ge(go_sb, 2 * n + 2)
                for k in range(2):
                    act_.wait_ge(ao_ps, 2 * n + k + 1)
                    copy(other_order(fb, k), rows_of(bank[4 + k])).then_inc(ao_sb, 1)

            def turn_even_copy(n):
                for k in range(2):
                    act_.wait_ge(te_ps, 2 * n + k + 1)
                    copy(half(fc, k), bank[6 + k][:]).then_inc(te_sb, 1)

            def turn_odd_copy(n):
                for k in range(2):
                    act_.wait_ge(to_ps, 2 * n + k + 1)
                    copy(half(fd, k), bank[4 + k][:]).then_inc(to_sb, 1)

            def square_even(n):
                for k in range(2):
                    act_.wait_ge(be_ps, 2 * n + k + 1)
                    square(fa, bank[6 + k], k).then_inc(be_sb, 1)

            def square_odd(n):
                for k in range(2):
                    act_.wait_ge(bo_ps, 2 * n + k + 1)
                    square(fb, bank[4 + k], k).then_inc(bo_sb, 1)

            def magnitude(n):
                act_.wait_ge(sq_sb, n + 1)
                act_.activation(fa, fa, ACT.Sqrt).then_inc(mag_sb, 1)

            def rectify(n):
                act_.wait_ge(mixed_sb, n + 1)
                act_.activation(grid(relu), hv[:], ACT.Relu, bias=mix[:, 1:2]).then_inc(relu_sb, 1)

            def out_copy(n):
                for k in range(2):
                    act_.wait_ge(out_ps, 2 * n + k + 1)
                    act_.wait_ge(stored, 16 * n)
                    act_.activation(y_out[:, HALF * k:HALF * k + HALF], bank[6 + k][:], ACT.Identity,
                                    bias=col("out_b")).then_inc(out_sb, 1)

            def conv_early(n, j):
                if j == 0:
                    pyr_copy(n, 0)
                elif j == 2:
                    row_spectrum_copy(n)
                elif j == 3:
                    r_even_copy(n)
                elif j == 6:
                    inverse_odd_copy(n)
                elif j == 7:
                    turn_odd_copy(n)

            def conv_late(n, j):
                if j == 1:
                    pyr_copy(n, 1)
                    x2_copy(n)
                elif j == 2:
                    spectrum_turn_copy(n)
                elif j == 3:
                    edge_cuts(n)
                elif j == 5:
                    inverse_even_copy(n)
                elif j == 6:
                    turn_even_copy(n)
                elif j == 7:
                    square_even(n)

            def pyr_taps(n, j):
                for k in range(PYR_TAPS[j], PYR_TAPS[j + 1]):
                    pyr_tap(n, k)

            def swin_only(i):
                to_windows(i)
                x_copy(i)
                deviation1(i)
                n_copy(i)
                queries(i)
                key_heads(i)
                v_copy(i)
                exponent(i, 0)
                exponent(i, 1)
                for j in range(PAIRS):
                    prob_copy(i, j)
                    if j + 2 < PAIRS:
                        exponent(i, j + 2)
                    if j == 4:
                        attention_copy(i, 0)
                deviation2(i, 0)
                attention_copy(i, 1)
                n2_copy(i, 0)
                deviation2(i, 1)
                n2_copy(i, 1)
                mlp_gelu(i)

            def both(n, i):
                to_windows(i)
                in_gelu(n)
                magnitudes(n)
                x_copy(i)
                deviation1(i)
                n_copy(i)
                edge_sigmoid(n)
                route_sigmoid(n)
                queries(i)
                key_heads(i)
                route_exponent(n)
                v_copy(i)
                edge_copy(n)
                exponent(i, 0)
                exponent(i, 1)
                for j in range(PAIRS):
                    conv_early(n, j)
                    prob_copy(i, j)
                    if j == 4:
                        attention_copy(i, 0)
                    conv_late(n, j)
                    if j + 2 < PAIRS:
                        exponent(i, j + 2)
                    pyr_taps(n, j)
                deviation2(i, 0)
                attention_copy(i, 1)
                n2_copy(i, 0)
                square_odd(n)
                deviation2(i, 1)
                pyr_taps(n, PAIRS)
                n2_copy(i, 1)
                magnitude(n)
                mlp_gelu(i)
                rectify(n)
                out_copy(n)

            def conv_only(n):
                in_gelu(n)
                magnitudes(n)
                edge_sigmoid(n)
                route_sigmoid(n)
                route_exponent(n)
                edge_copy(n)
                for j in range(PAIRS):
                    conv_early(n, j)
                    conv_late(n, j)
                    pyr_taps(n, j)
                pyr_taps(n, PAIRS)
                square_odd(n)
                magnitude(n)
                rectify(n)
                out_copy(n)

            swin_only(0)
            both(0, 1)
            with act_.Fori(1, IMAGES - 1) as n:
                both(n, n + 1)
            conv_only(IMAGES - 1)

        @block.gpsimd
        def _(pool):
            pool.memset(act[:], 0.0)
            for padded in (hor, ver, pyr):
                pool.memset(padded[:], 0.0)
            pool.memset(v_pair[:], 0.0)
            pool.drain()
            pool.sem_inc(zeroed, 1)
            pool.wait_ge(setup_dve, 1)

            def residual_in(i):
                pool.wait_ge(xT_sb, 2 * i + 2)
                pool.sem_inc(pool_turns)
                pool.wait_ge(x1_sb, 2 * i)
                pool.sem_inc(pool_turns)
                pool.tensor_tensor(resT[:], xT[:], proj_shift[:].unsqueeze(1).broadcast_to([P, CH, C]), ALU.add)\
                    .then_inc(res_sb, 1)

            def less_max(i, j):
                pool.wait_ge(s_max, 8 * i + j + 1)
                pool.sem_inc(pool_turns)
                pool.tensor_tensor(score[:, j % 3], score[:, j % 3],
                                   row_max[:, j % 3].unsqueeze(2).broadcast_to([P, HEADS, WT]), ALU.subtract)\
                    .then_inc(s_sub, 1)

            def normalise(i, j):
                pool.wait_ge(s_inv, 8 * i + j + 1)
                pool.sem_inc(pool_turns)
                if j >= 2:
                    pool.wait_ge(pT_ps, 8 * i + j - 1)
                    pool.sem_inc(pool_turns)
                pool.tensor_tensor(prob[:, j % 2].rearrange("p (h k) -> p h k", h=HEADS), score[:, j % 3],
                                   row_inv[:, j % 3].unsqueeze(2).broadcast_to([P, HEADS, WT]), ALU.mult)\
                    .then_inc(p_sb, 1)

            mid = AXIS_TAPS // 2
            OFFSETS = [0] + [AXIS_DIL * (t - mid) for t in range(AXIS_TAPS)
                             if t != mid and abs(AXIS_DIL * (t - mid)) < SIDE]

            def axis_conv(n, a, offsets):
                dst, name = ((hor, "dilh"), (ver, "dilv"))[a]
                body = dst[:, 1:1 + SIDE, 1:1 + SIDE]
                for off in offsets:
                    weight = col(name, off // AXIS_DIL + mid)
                    if off == 0:
                        pool.wait_ge(act_sb, 2 * n + 2)
                        pool.sem_inc(pool_turns)
                        pool.wait_ge(hv_sb, n)
                        pool.sem_inc(pool_turns)
                        pool.tensor_scalar(body, act_in, weight, 1.0, ALU.mult, ALU.mult)
                        continue
                    lo, hi = max(0, -off), min(SIDE, SIDE - off)
                    if a == 0:
                        part = (slice(None), slice(None), slice(lo, hi))
                        of = act_in[:, :, lo + off:hi + off]
                    else:
                        part = (slice(None), slice(lo, hi))
                        of = act_in[:, lo + off:hi + off]
                    pool.drain()
                    pool.tensor_scalar(axis_part[part], of, weight, 1.0, ALU.mult, ALU.mult)
                    pool.drain()
                    last = pool.tensor_tensor(body[part], body[part], axis_part[part], ALU.add)
                    if off == OFFSETS[-1]:
                        last.then_inc(axis_sb, 1)

            def mirrored(dst, op):
                d = dst.rearrange("p (a r k) -> p a r k", a=16, r=2)
                rows_, back, two = xs_hw[:, 1:16], xs_hw[:, 31:16:-1], xs_hw[:, 0:17:16]
                pool.tensor_tensor(d[:, 1:16, :, 1:32], rows_[:, :, 1:32].unsqueeze(2).broadcast_to([P, 15, 2, 31]),
                                   back[:, :, 31:0:-1].unsqueeze(2).broadcast_to([P, 15, 2, 31]), op)
                pool.tensor_tensor(d[:, 1:16, :, 0], rows_[:, :, 0:1].broadcast_to([P, 15, 2]),
                                   back[:, :, 0:1].broadcast_to([P, 15, 2]), op)
                m = d[:, 0, :, 2:32].rearrange("p r (m u) -> p r m u", u=2)
                pool.tensor_tensor(m, two[:, :, 1:16].unsqueeze(3).broadcast_to([P, 2, 15, 2]),
                                   two[:, :, 31:16:-1].unsqueeze(3).broadcast_to([P, 2, 15, 2]), op)
                return pool.tensor_tensor(d[:, 0, :, 0:2], two[:, :, 0:17:16], two[:, :, 0:17:16], op)

            def even_odd(n):
                pool.wait_ge(xs_sb, n + 1)
                pool.sem_inc(pool_turns)
                pool.wait_ge(r2_ps, 2 * n)
                pool.sem_inc(pool_turns)
                mirrored(xe[:], ALU.add).then_inc(xe_sb, 1)
                mirrored(xo[:], ALU.subtract).then_inc(xo_sb, 1)

            def even_bias(n):
                pool.wait_ge(r1_sb, 2 * n + 2)
                pool.sem_inc(pool_turns)
                f = fc.rearrange("p (g c) -> p g c", g=CH)
                pool.tensor_tensor(f, f, two_b1[:].unsqueeze(1).broadcast_to([P, CH, C]), ALU.add)

            def even_product(n):
                pool.wait_ge(w_sb, 2 * n + 2)
                pool.sem_inc(pool_turns)
                pool.drain()
                pool.tensor_tensor(fc, fc, fb, ALU.mult).then_inc(ge_sb, 1)

            def add_part(n, k):
                pool.drain()
                pool.wait_ge(part_sb, 9 * n + k + 1)
                pool.sem_inc(pool_turns)
                pool.tensor_tensor(py[:], py[:], grid(parts[k][:, 0:TOK]), ALU.add).then_inc(part_added, 1)
                if k == 8:
                    pool.drain()
                    pool.sem_inc(py_sb, 1)

            def gate_pyramid(n):
                pool.wait_ge(cut_sb, n + 1)
                pool.sem_inc(pool_turns)
                pool.wait_ge(xm_mixed, n + 1)
                pool.sem_inc(pool_turns)
                pool.tensor_tensor(py[:], py[:], edge_cut[:], ALU.mult)
                pool.drain()
                pool.tensor_tensor(py[:], py[:], grid(xm[:]), ALU.add).then_inc(pyramid_gated, 1)

            def gate_axes(n):
                pool.wait_ge(hv_sb, n + 1)
                pool.sem_inc(pool_turns)
                pool.wait_ge(edge_sb, 2 * n + 2)
                pool.sem_inc(pool_turns)
                pool.tensor_tensor(hv[:], hv[:], edge[:], ALU.mult)
                pool.drain()
                pool.tensor_tensor(hv[:], hv[:], py[:], ALU.add).then_inc(gated_sb, 1)

            def square_sum(n):
                pool.wait_ge(be_sb, 2 * n + 2)
                pool.sem_inc(pool_turns)
                pool.wait_ge(bo_sb, 2 * n + 2)
                pool.sem_inc(pool_turns)
                pool.tensor_tensor(fa, fa, fb, ALU.add).then_inc(sq_sb, 1)

            def swin_only(i):
                residual_in(i)
                less_max(i, 0)
                less_max(i, 1)
                for j in range(PAIRS):
                    normalise(i, j)
                    if j + 2 < PAIRS:
                        less_max(i, j + 2)

            def both(n, i):
                residual_in(i)
                axis_conv(n, 0, OFFSETS)
                even_odd(n)
                axis_conv(n, 1, OFFSETS[:2])
                less_max(i, 0)
                less_max(i, 1)
                for j in range(PAIRS):
                    normalise(i, j)
                    if j + 2 < PAIRS:
                        less_max(i, j + 2)
                    if j < 3:
                        axis_conv(n, 1, OFFSETS[2 + j:3 + j])
                    if j == 4:
                        even_bias(n)
                        even_product(n)
                    elif j >= 2:
                        add_part(n, (1, 2, 0, 3, 4, 5)[j - 2])
                add_part(n, 6)
                square_sum(n)
                add_part(n, 7)
                add_part(n, 8)
                gate_pyramid(n)
                gate_axes(n)

            def conv_only(n):
                axis_conv(n, 0, OFFSETS)
                even_odd(n)
                axis_conv(n, 1, OFFSETS)
                add_part(n, 1)
                add_part(n, 2)
                even_bias(n)
                even_product(n)
                for k in range(3, 9):
                    add_part(n, k)
                gate_pyramid(n)
                square_sum(n)
                gate_axes(n)

            swin_only(0)
            both(0, 1)
            with pool.Fori(1, IMAGES - 1) as n:
                both(n, n + 1)
            conv_only(IMAGES - 1)


def kernel(**inputs):
    import concourse.bacc as bacc
    from concourse.bass_utils import run_bass_kernel_spmd

    a = {k: np.asarray(v) for k, v in inputs.items()}
    swin = {k[8:]: v for k, v in a.items() if k.startswith("L0_conv_")}
    conv = {k[8:]: v for k, v in a.items() if k.startswith("L1_conv_")}

    cols = np.zeros((P, NCOLS), np.float32)

    def put(name, value):
        value = value.reshape(value.shape[0], -1)
        cols[:value.shape[0], COLS[name][0]:COLS[name][0] + value.shape[1]] = value

    put("ln1_g", swin["ln1_g"])
    put("ln1_b", swin["ln1_b"])
    for k, name in enumerate(("q_b", "k_b", "v_b")):
        put(name, swin["qkv_b"][k * C:(k + 1) * C])
    put("ln2_g", swin["ln2_g"])
    put("ln2_b", swin["ln2_b"])
    put("b1", swin["b1"].reshape(FC, P).T)
    put("b2", swin["b2"])
    for name in ("in_b", "out_b", "fac_b", "conv_b", "fuse_w", "fuse_b", "cr_b"):
        put(name, conv[name].T if name == "cr_b" else conv[name])
    put("alpha", conv["fgm_alpha"])
    put("beta", conv["fgm_beta"])
    put("dw_w", conv["dw11_w"])
    put("dw_b", conv["dw11_b"])
    put("pyr_b", conv["pyr_b"].reshape(-1))
    put("vis_b", np.repeat(conv["vis_b"], P))
    put("batt_b1", conv["batt_b1"])
    put("dilh", conv["dilh_w"])
    put("dilv", conv["dilv_w"])
    put("cr_w", conv["cr_w"].reshape(3, C, 9).transpose(1, 0, 2))
    rows = np.concatenate([swin["proj_b"], conv["fgm_b1"], conv["fgm_b2"], conv["fgm_boost"].reshape(-1),
                           conv["batt_b2"], conv["base_weights"]])[None]
    pyr = np.zeros((C, len(DILS), 9, 32), np.float32)
    for o in range(32):
        pyr[4 * o:4 * o + 4, :, :, o] = conv["pyr_w"][:, o].reshape(len(DILS), 4, 9).transpose(1, 0, 2)
    batt2 = np.zeros((P, ROUTES), np.float32)
    batt2[:BATT] = conv["batt_w2"].reshape(ROUTES, BATT).T
    table = np.zeros((2 * P, HEADS), np.float32)
    table[:REL] = swin["rpb_table"]
    mats = np.concatenate([
        swin["qkv_w"].T, swin["proj_w"].T, swin["w1"].T,
        swin["w2"].reshape(C, FC, P).transpose(2, 1, 0).reshape(P, -1),
        conv["in_w"].reshape(C, C).T, conv["out_w"].reshape(C, C).T, conv["fac_w"].reshape(C, C).T,
        conv["conv_w"].reshape(C, C).T, conv["fgm_w1"].reshape(C, C).T, conv["fgm_w2"].reshape(C, C).T,
        conv["vis_w"].reshape(C, 9), conv["batt_w1"].reshape(BATT, C).T, batt2, pyr.reshape(C, -1),
        table.reshape(2, P, HEADS).transpose(1, 0, 2).reshape(P, -1)], 1)
    arrays = {
        "x_dram": np.ascontiguousarray(a["x"].reshape(IMAGES, C, TOK)),
        "cols_dram": cols,
        "rows_dram": np.ascontiguousarray(rows),
        "mats_dram": np.ascontiguousarray(mats),
        "cons_dram": shape_constants(),
        "rel_dram": np.ascontiguousarray(swin["rpi"].T.reshape(1, WT * WT)),
    }
    nc = bacc.Bacc("TRN2", target_bir_lowering=False, num_devices=1)
    args = [nc.dram_tensor(k, v.shape, mybir.dt.from_np(v.dtype), kind="ExternalInput").ap()
            for k, v in arrays.items()]
    args.append(nc.dram_tensor("out_dram", (IMAGES, C, TOK), F32, kind="ExternalOutput").ap())
    x_, cols_, rows_, mats_, cons_, rel_, out_ = args
    swin_conv_kernel(nc, x_, cols_, rows_, mats_, cons_, rel_, out_)
    result = run_bass_kernel_spmd(nc, [arrays], core_ids=[0])
    return result.results[0]["out_dram"].reshape(IMAGES, C, SIDE, SIDE)
```

```python
from contextlib import ExitStack

import numpy as np
import concourse.bass as bass
from concourse import mybir

F32 = mybir.dt.float32
I32 = mybir.dt.int32
ALU = mybir.AluOpType
ACT = mybir.ActivationFunctionType
AX = mybir.AxisListType

IMAGES, C, SIDE = 16, 128, 32
TOK = SIDE * SIDE
P = 128
CH = TOK // P
HALF = TOK // 2
WS, HEADS = 8, 8
WT = WS * WS
HD = C // HEADS
WIN = TOK // WT
PAIRS = WIN // 2
HP = HEADS // 2
FF = 512
FC = FF // P
LN_EPS = 1e-5
DILS = (1, 6, 12, 20)
PAD = max(DILS)
SP = SIDE + 2 * PAD
S1 = SIDE + 2
AXIS_DIL, AXIS_TAPS = 11, 7
REL = (2 * WS - 1) ** 2
BATT = C // 8
ROUTES = 5


def layout(*entries):
    at, where = 0, {}
    for name, width in entries:
        where[name] = (at, width)
        at += width
    return where, at


COLS, NCOLS = layout(
    ("ln1_g", 1), ("ln1_b", 1), ("q_b", 1), ("k_b", 1), ("v_b", 1), ("ln2_g", 1), ("ln2_b", 1),
    ("b1", FC), ("b2", 1), ("in_b", 1), ("out_b", 1), ("fac_b", 1), ("conv_b", 1), ("alpha", 1),
    ("beta", 1), ("fuse_w", 1), ("fuse_b", 1), ("dw_w", 1), ("dw_b", 1), ("pyr_b", 1), ("vis_b", 1),
    ("batt_b1", 1), ("dilh", AXIS_TAPS), ("dilv", AXIS_TAPS), ("cr_w", 27), ("cr_b", 3))
ROWS, NROWS = layout(("proj_b", C), ("fgm_b1", C), ("fgm_b2", C), ("boost", C), ("batt_b2", ROUTES),
                     ("base", ROUTES))
MATS, NMATS = layout(
    ("qkv", 3 * C), ("proj", C), ("w1", FF), ("w2", FF), ("in", C), ("out", C), ("fac", C),
    ("conv", C), ("fgm1", C), ("fgm2", C), ("vis", 9), ("batt1", BATT), ("batt2", ROUTES),
    ("pyr", len(DILS) * 9 * 32), ("table", 2 * 32))
CONS, NCONS = layout(
    ("ident", P), ("sel", P), ("dft_h", P), ("dft_w0", P), ("dft_w", P), ("even0", P),
    ("even", P), ("odd0", P), ("odd", P), ("idft_h", P), ("head_mask", HEADS), ("high", CH), ("iota", 2))


def shape_constants():
    n = SIDE
    ang = 2 * np.pi * np.outer(np.arange(n), np.arange(n)) / n
    cos, sin = np.cos(ang), np.sin(ang)
    pack = np.zeros((n, n))
    pack[:, 0], pack[:, 1] = 1, cos[:, 16]
    pack[:, 2::2], pack[:, 3::2] = cos[:, 1:16], -sin[:, 1:16]
    unpack = np.zeros((n, n))
    unpack[0], unpack[1] = 1, cos[16]
    unpack[2::2], unpack[3::2] = 2 * cos[1:16], -2 * sin[1:16]
    unpack /= n
    full = np.block([[cos, -sin], [sin, cos]])
    inv = np.block([[cos, sin], [-sin, cos]]) / n

    def diag(*blocks):
        size = sum(len(b) for b in blocks)
        out, at = np.zeros((size, size)), 0
        for b in blocks:
            out[at:at + len(b), at:at + len(b)] = b
            at += len(b)
        return out

    inv_odd = np.concatenate([-inv[n:], inv[:n]])
    unpack_odd = np.zeros((n, n))
    unpack_odd[2::2], unpack_odd[3::2] = -unpack[3::2], unpack[2::2]
    c = np.zeros((P, NCONS))

    def put(name, value):
        at, width = CONS[name]
        c[:, at:at + width] = value

    put("ident", np.eye(P))
    sel = np.zeros((P, P))
    sel[[64, 96]] = 1
    put("sel", sel)
    put("dft_h", diag(pack, pack, pack, pack))
    put("dft_w0", diag(pack, pack, full))
    put("dft_w", diag(full, full))
    put("even0", 0.5 * diag(unpack, unpack, inv))
    put("even", 0.5 * diag(inv, inv))
    put("odd0", 0.5 * diag(unpack_odd, unpack_odd, inv_odd))
    put("odd", 0.5 * diag(inv_odd, inv_odd))
    idft = diag(unpack, unpack, unpack, unpack).reshape(P, 4, n)
    put("idft_h", idft.transpose(0, 2, 1).reshape(P, P))
    put("head_mask", np.arange(P)[:, None] // HD == np.arange(HEADS)[None])
    freq = np.minimum(np.arange(n), n - np.arange(n)) / n
    packed_k = np.array([0, 16] + [k for k in range(1, 16) for _ in range(2)])
    high = np.zeros((CH, 2, 2, n))
    for g in range(CH):
        for s in range(2):
            for r in range(2):
                kh = 2 * g + s
                kw = np.arange(n)
                if kh == 0:
                    kh, kw = 16 * r, packed_k
                high[g, s, r] = np.sqrt(freq[kh] ** 2 + freq[kw] ** 2) > 0.3
    put("high", high.reshape(CH, P).T)
    put("iota", np.stack([np.arange(P), np.arange(P) + P], 1))
    return c.astype(np.float32)


def swin_conv_kernel(nc, x, cols, rows, mats, cons, rel_index, out):
    with ExitStack() as ctx:
        def sb(name, *free, dt=F32):
            return ctx.enter_context(nc.sbuf_tensor(name, [P, *free], dt))

        def sem(name):
            return ctx.enter_context(nc.semaphore(name))

        cons_sb, cols_sb, mats_sb = sb("cons_sb", NCONS), sb("cols_sb", NCOLS), sb("mats_sb", NMATS)
        rows_sb = sb("rows_sb", NROWS)

        def con(name):
            at, width = CONS[name]
            return cons_sb[:, at:at + width]

        def col(name, k=0):
            return cols_sb[:, COLS[name][0] + k:COLS[name][0] + k + 1]

        def row(name):
            at, width = ROWS[name]
            return rows_sb[:, at:at + width]

        def mat(name):
            at, width = MATS[name]
            return mats_sb[:, at:at + width]

        ident = con("ident")
        w_qkv, w_proj, w_up, w_down = mat("qkv"), mat("proj"), mat("w1"), mat("w2")
        w_pyr = mat("pyr").rearrange("p (d t o) -> p d t o", d=len(DILS), t=9)
        ones = sb("ones", P)
        eps = sb("eps", 1)
        cut_bias = sb("cut_bias", 1)
        first_gelu = sb("first_gelu", 1)
        fold_b = sb("fold_b", 3 + FC)
        fuse_bias = sb("fuse_bias", 1)
        w_vis = sb("w_vis", 9, 32)
        proj_shift = sb("proj_shift", P)
        two_b1 = sb("two_b1", P)
        rel_bias = sb("rel_bias", HEADS * WT)
        boost = sb("boost", CH, C)
        base = sb("base", ROUTES)
        half_vis_b = sb("half_vis_b", 1)
        dc_b2 = sb("dc_b2", P)
        tiny = sb("tiny", 8)

        x_in = sb("x_in", TOK)
        xw = sb("xw", TOK)
        attn_out = xw
        xT = sb("xT", CH, C)
        x1T = xT
        resT = sb("resT", CH, C)
        nT = sb("nT", CH, C)
        nC = sb("nC", TOK)
        qC, kC = sb("qC", TOK), sb("kC", TOK)
        k_heads = sb("k_heads", WIN, HEADS, WT)
        hidden = k_heads[:, 0:8].rearrange("p a h k -> p (a h k)").rearrange("p (f t) -> p f t", f=FC)
        v_pair = sb("v_pair", WIN, HP, 2, HD)
        score = sb("score", 3, HEADS, WT)
        prob = sb("prob", 2, HEADS * WT)
        probT = sb("probT", 2, HP, P)
        stats, mv = sb("stats", CH, 6), sb("mv", CH, 2)
        std, rstd = sb("std", CH), sb("rstd", CH)
        row_max, row_sum, row_inv = sb("row_max", 3, HEADS), sb("row_sum", 3, HEADS), sb("row_inv", 3, HEADS)
        parts = (kC, nC, kC, nC, kC, k_heads[:, 14:16].rearrange("p w h k -> p (w h k)"), kC,
                 k_heads[:, 14:16].rearrange("p w h k -> p (w h k)"), kC)
        xm = sb("xm", TOK)
        act = sb("act", SP, SP)
        hor, ver, pyr = sb("hor", S1, S1), sb("ver", S1, S1), sb("pyr", S1, S1)
        hv, py = sb("hv", SIDE, SIDE), sb("py", SIDE, SIDE)
        xs = sb("xs", TOK)
        xe, xo = sb("xe", TOK), sb("xo", TOK)
        fft = sb("fft", 4, TOK)
        fa, fb, fc, fd = (fft[:, k] for k in range(4))
        relu = fb
        edge = sb("edge", SIDE, SIDE)
        axis_part = sb("axis_part", SIDE, SIDE)
        edge_cut = axis_part
        y_out = sb("y_out", TOK)
        rel_rows = xe
        sums = sb("sums", 4)
        vec = sb("vec", 16)
        batt_wide = sb("batt_wide", P)
        route = sb("route", 4, ROUTES)
        cr_scaled = sb("cr_scaled", 3, 9)
        cr_bias = sb("cr_bias", 3)
        mix = sb("mix", 8)

        bank = [ctx.enter_context(nc.psum_tensor(f"bank{i}", [P, HALF], F32)) for i in range(8)]

        rel_banks = (bank[0], bank[1], bank[5], bank[6])

        loaded = sem("loaded")
        index_low = sem("index_low")
        index_high = sem("index_high")
        weights_raw_used = sem("weights_raw_used")
        fold_ps = sem("fold_ps")
        folded = sem("folded")
        v_wide_ready = sem("v_wide_ready")
        shift_ps = sem("shift_ps")
        setup_exp = sem("setup_exp")
        setup_z = sem("setup_z")
        zeroed = sem("zeroed")
        onehot_ready = sem("onehot_ready")
        onehot_used = sem("onehot_used")
        rel_ps = sem("rel_ps")
        rel_rows_sb = sem("rel_rows_sb")
        setup_dve = sem("setup_dve")
        x_loaded = sem("x_loaded")
        stored = sem("stored")
        pool_turns = sem("pool_turns")
        xw_ready = sem("xw_ready")
        xT_ps = sem("xT_ps")
        xT_sb = sem("xT_sb")
        ln1_var = sem("ln1_var")
        ln1_std = sem("ln1_std")
        nT_sb = sem("nT_sb")
        res_sb = sem("res_sb")
        nT_ps = sem("nT_ps")
        nC_sb = sem("nC_sb")
        q_ps = sem("q_ps")
        k_ps = sem("k_ps")
        q_sb = sem("q_sb")
        k_sb = sem("k_sb")
        kh_dve = sem("kh_dve")
        kh_act = sem("kh_act")
        v_ps = sem("v_ps")
        v_sb = sem("v_sb")
        s_ps = sem("s_ps")
        s_biased = sem("s_biased")
        s_max = sem("s_max")
        s_sub = sem("s_sub")
        s_exp = sem("s_exp")
        s_inv = sem("s_inv")
        p_sb = sem("p_sb")
        pT_ps = sem("pT_ps")
        pT_sb = sem("pT_sb")
        o_ps = sem("o_ps")
        o_sb = sem("o_sb")
        proj_ps = sem("proj_ps")
        x1_sb = sem("x1_sb")
        ln2_var = sem("ln2_var")
        ln2_std = sem("ln2_std")
        n2T_sb = sem("n2T_sb")
        n2T_ps = sem("n2T_ps")
        n2C_sb = sem("n2C_sb")
        up_ps = sem("up_ps")
        up_sb = sem("up_sb")
        down_ps = sem("down_ps")
        xm_sb = sem("xm_sb")
        in_ps = sem("in_ps")
        act_sb = sem("act_sb")
        abs_sb = sem("abs_sb")
        gap_sb = sem("gap_sb")
        gap_ps = sem("gap_ps")
        mid_sb = sem("mid_sb")
        mid_ps = sem("mid_ps")
        route_z = sem("route_z")
        route_e = sem("route_e")
        route_d = sem("route_d")
        route_f = sem("route_f")
        cw_sb = sem("cw_sb")
        xs_sb = sem("xs_sb")
        edge_ps = sem("edge_ps")
        edge_parts = sem("edge_parts")
        eb_ps = sem("eb_ps")
        edge_sb = sem("edge_sb")
        pyr_ps = sem("pyr_ps")
        pyr_sb = sem("pyr_sb")
        xe_sb = sem("xe_sb")
        xo_sb = sem("xo_sb")
        x2_ps = sem("x2_ps")
        x2_sb = sem("x2_sb")
        h_ps = sem("h_ps")
        h_sb = sem("h_sb")
        t_ps = sem("t_ps")
        t_sb = sem("t_sb")
        r1_ps = sem("r1_ps")
        r1_sb = sem("r1_sb")
        w_ps = sem("w_ps")
        w_sb = sem("w_sb")
        r2_ps = sem("r2_ps")
        ge_sb = sem("ge_sb")
        go_sb = sem("go_sb")
        axis_sb = sem("axis_sb")
        xm_mixed = sem("xm_mixed")
        pyramid_gated = sem("pyramid_gated")
        cut_sb = sem("cut_sb")
        ae_ps = sem("ae_ps")
        ae_sb = sem("ae_sb")
        ao_ps = sem("ao_ps")
        ao_sb = sem("ao_sb")
        te_ps = sem("te_ps")
        te_sb = sem("te_sb")
        to_ps = sem("to_ps")
        to_sb = sem("to_sb")
        be_ps = sem("be_ps")
        be_sb = sem("be_sb")
        bo_ps = sem("bo_ps")
        bo_sb = sem("bo_sb")
        sq_sb = sem("sq_sb")
        mag_sb = sem("mag_sb")
        hv_sb = sem("hv_sb")
        py_sb = sem("py_sb")
        part_sb = sem("part_sb")
        part_added = sem("part_added")
        gated_sb = sem("gated_sb")
        mixed_sb = sem("mixed_sb")
        relu_sb = sem("relu_sb")
        out_ps = sem("out_ps")
        out_sb = sem("out_sb")

        def grid(ap):
            return ap.rearrange("p (h w) -> p h w", w=SIDE)

        def natural_windows(ap, a):
            return ap.rearrange("p (a r b s) -> p a b r s", a=4, r=WS, b=4)[:, a]

        def windows(ap, a):
            return ap[:, 256 * a:256 * a + 256].rearrange("p (b r s) -> p b r s", b=4, r=WS)

        xs_hw = xs.rearrange("p (w h) -> p h w", w=SIDE)
        act_in = act[:, PAD:PAD + SIDE, PAD:PAD + SIDE]

        DVE_HEADS, ACT_HEADS = range(0, 6), range(6, HEADS)

        def head_mask(h):
            at = CONS["head_mask"][0] + h
            return cons_sb[:, at:at + 1]

        block = ctx.enter_context(nc.Block())
        LOADS = 4
        PYR_TAPS = (0, 0, 1, 3, 4, 5, 6, 6, 7)
        SLOT_TAPS = (0, 0, 0, 2, 4, 4, 5, 7, 9)

        @block.sync
        def _(sp):
            sp.dma_start(mats_sb[:], mats).then_inc(loaded, 16)
            sp.dma_start(cols_sb[:], cols).then_inc(loaded, 16)
            sp.dma_start(cons_sb[:], cons).then_inc(loaded, 16)
            sp.dma_start(rows_sb[:], rows.broadcast_to([P, NROWS])).then_inc(loaded, 16)
            sp.dma_start(x_in[:], x[0]).then_inc(x_loaded, 16)
            index = k_heads[:, 0:8].rearrange("p a h k -> p (a h k)").bitcast(I32)
            low, high = slice(0, WT * WT // 2), slice(WT * WT // 2, WT * WT)
            sp.dma_start(index[:, low], rel_index[:, low].broadcast_to([P, WT * WT // 2])).then_inc(index_low, 16)
            sp.dma_start(index[:, high], rel_index[:, high].broadcast_to([P, WT * WT // 2])).then_inc(index_high, 16)

            def load(i):
                sp.wait_ge(xw_ready, i)
                sp.dma_start(x_in[:], x[i]).then_inc(x_loaded, 16)

            def store(n):
                sp.wait_ge(out_sb, 2 * n + 2)
                sp.dma_start(out[n], y_out[:]).then_inc(stored, 16)

            load(1)
            with sp.Fori(0, IMAGES - 2) as n:
                load(n + 2)
                store(n)
            store(IMAGES - 2)
            store(IMAGES - 1)
            sp.wait_ge(stored, 16 * IMAGES)

        @block.tensor
        def _(pe):
            def turn4(dst, src, k):
                for c in range(4):
                    at = (4 * k + c) * P
                    last = pe.transpose(dst[:, c * P:(c + 1) * P], src[:, at:at + P], ident)
                return last

            def multiply4(dst, src, k, weights, first=None):
                for c in range(4):
                    at = (4 * k + c) * P
                    rhs = first if first is not None and at == 0 else weights
                    last = pe.matmul(dst[:, c * P:(c + 1) * P], src[:, at:at + P], rhs, start=True, stop=True)
                return last

            nT_flat = nT[:].rearrange("p c d -> p (c d)")

            def x_transposes(i):
                pe.wait_ge(xw_ready, i + 1)
                pe.wait_ge(up_sb, 8 * i)
                pe.wait_ge(xm_sb, 2 * i)
                for k in range(2):
                    turn4(bank[k], xw, k).then_inc(xT_ps, 1)

            def n_transposes(i):
                for k in range(2):
                    pe.wait_ge(nT_sb, 2 * i + k + 1)
                    turn4(bank[2 + k], nT_flat, k).then_inc(nT_ps, 1)

            def queries_keys(i):
                for k in range(2):
                    pe.wait_ge(nC_sb, 2 * i + k + 1)
                    pe.matmul(bank[2 + k][:], w_qkv[:, C:2 * C], nC[:, HALF * k:HALF * k + HALF],
                              start=True, stop=True).then_inc(k_ps, 1)
                for k in range(2):
                    pe.wait_ge(xT_sb, 2 * i + k + 1)
                    pe.matmul(bank[k][:], w_qkv[:, 0:C], nC[:, HALF * k:HALF * k + HALF],
                              start=True, stop=True).then_inc(q_ps, 1)

            def v(i):
                wv = w_qkv[:, 2 * C:3 * C].rearrange("p (g e d) -> p e g d", g=HP, e=2)
                for k in range(2):
                    pe.wait_ge(q_sb, 2 * i + k + 1)
                    for w in range(8):
                        t = nC[:, (8 * k + w) * WT:(8 * k + w + 1) * WT]
                        for e in range(2):
                            last = pe.matmul(bank[k][64 * e:64 * e + 64, w * 64:w * 64 + 64], t, wv[:, e],
                                             start=True, stop=True)
                    last.then_inc(v_ps, 1)

            def scores(i, j):
                if j == 0:
                    pe.wait_ge(kh_dve, i + 1)
                    pe.wait_ge(kh_act, i + 1)
                    pe.wait_ge(q_sb, 2 * i + 2)
                if j < 2:
                    pe.wait_ge(k_sb, 2 * i + j + 1)
                else:
                    pe.wait_ge(s_biased, 8 * i + j - 1)
                for e in range(2):
                    w = 2 * j + e
                    last = pe.matmul(bank[2 + j % 2][64 * e:64 * e + 64, :], qC[:, w * WT:(w + 1) * WT],
                                     k_heads[:, w].rearrange("p h k -> p (h k)"), start=True, stop=True)
                last.then_inc(s_ps, 1)

            def prob_transposes(i, j):
                pe.wait_ge(p_sb, 8 * i + j + 1)
                if j == 0:
                    pe.wait_ge(v_sb, 2 * i + 2)
                else:
                    pe.wait_ge(pT_sb, 8 * i + j)
                for g in range(HP):
                    last = pe.transpose(bank[0][:, g * P:(g + 1) * P], prob[:, j % 2, g * P:(g + 1) * P], ident)
                last.then_inc(pT_ps, 1)

            def values(i, j):
                pe.wait_ge(pT_sb, 8 * i + j + 1)
                if j == 4:
                    pe.wait_ge(o_sb, 2 * i + 1)
                for e in range(2):
                    w = 2 * j + e
                    for g in range(HP):
                        last = pe.matmul(bank[1][32 * g:32 * g + 32, (w % 8) * WT:(w % 8 + 1) * WT],
                                         v_pair[:, w, g].rearrange("p e d -> p (e d)"),
                                         probT[:, j % 2, g, e * WT:(e + 1) * WT], start=True, stop=True)
                last.then_inc(o_ps, 1)

            def project(i, k):
                pe.wait_ge(o_sb, 2 * i + k + 1)
                pe.wait_ge(s_biased, 8 * i + 7 + k)
                multiply4(bank[2 + k], attn_out, k, w_proj).then_inc(proj_ps, 1)

            def n2_transposes(i, k):
                pe.wait_ge(n2T_sb, 2 * i + k + 1)
                pe.wait_ge(pT_sb, 8 * i + 8)
                pe.wait_ge(o_sb, 2 * i + 2)
                turn4(bank[k], nT_flat, k).then_inc(n2T_ps, 1)

            def mlp(i):
                def up(t):
                    k, f = divmod(t, FC)
                    b = (2, 3, 0, 1, 2, 3, 1, 2)[t]
                    if t < 2:
                        pe.wait_ge(x1_sb, 2 * i + t + 1)
                    elif t < 4:
                        pe.wait_ge(n2C_sb, 2 * i + t - 1)
                    else:
                        pe.wait_ge(up_sb, 8 * i + (1, 2, 4, 5)[t - 4])
                    pe.wait_ge(n2C_sb, 2 * i + k + 1)
                    pe.matmul(bank[b][:], w_up[:, f * P:(f + 1) * P], nC[:, HALF * k:HALF * k + HALF],
                              start=True, stop=True).then_inc(up_ps, 1)

                def down(k):
                    b = (0, 3)[k]
                    pe.wait_ge(up_sb, 8 * i + 4 + 4 * k)
                    for c in range(4):
                        pe.matmul(bank[b][:, c * P:(c + 1) * P], x1T[:, 4 * k + c], ident, is_transpose=True,
                                  start=(c == 0), stop=False)
                    for f in range(FC):
                        last = pe.matmul(bank[b][:], w_down[:, f * P:(f + 1) * P],
                                         hidden[:, f, HALF * k:HALF * k + HALF], start=False, stop=(f == FC - 1))
                    last.then_inc(down_ps, 1)

                for t in range(3):
                    up(t)
                n2_transposes(i, 1)
                for t in range(3, 6):
                    up(t)
                down(0)
                up(6)
                up(7)
                down(1)

            def in_conv(n):
                for k in range(2):
                    pe.wait_ge(xm_sb, 2 * n + k + 1)
                    pe.wait_ge(bo_sb, 2 * n)
                    pe.matmul(bank[4 + k][:], mat("in"), xm[:, HALF * k:HALF * k + HALF],
                              start=True, stop=True).then_inc(in_ps, 1)

            def tap(rows0, nrows, dil, t):
                y, x_ = rows0 + PAD + (t // 3 - 1) * dil, PAD + (t % 3 - 1) * dil
                return act[:, y:y + nrows, x_:x_ + SIDE]

            def gap_products(n):
                pe.wait_ge(gap_sb, n + 1)
                pe.wait_ge(out_sb, 2 * n)
                pe.matmul(bank[6][:, 0:1], mat("fac"), vec[:, 0:1], start=True, stop=True)
                pe.matmul(bank[6][0:BATT, 1:2], mat("batt1"), vec[:, 0:1], start=True, stop=True)\
                  .then_inc(gap_ps, 1)

            def mid_products(n):
                pe.wait_ge(mid_sb, n + 1)
                pe.matmul(bank[6][:, 2:3], mat("conv"), vec[:, 5:6], start=True, stop=True)
                pe.matmul(bank[6][:, 8:8 + ROUTES], batt_wide[0:BATT, :], mat("batt2")[0:BATT], start=True,
                          stop=True).then_inc(mid_ps, 1)

            def edge_spread(n):
                pe.wait_ge(go_sb, 2 * n + 2)
                pe.wait_ge(edge_parts, 2 * n + 2)
                for k in range(2):
                    pe.matmul(bank[4 + k][:], con("sel"), edge[:, 16 * k:16 * k + 16], start=True, stop=True)\
                      .then_inc(eb_ps, 1)

            EDGE_TAPS = (((0,), (4,)), ((), (5,)), ((1,), ()), ((), (6,)), ((2,), ()), ((), (7,)), ((3,), ()),
                         ((), (8,)), ((), ()))
            PYR_ORDER = (4, 0, 1, 2, 5, 6, 7, 8, 3)

            def inside(first, count, off):
                return max(first, -off), min(first + count, SIDE - off)

            def pyramid(n, k, steps):
                pe.wait_ge(act_sb, 2 * n + 2)
                if k == 0:
                    pe.wait_ge(out_sb, 2 * n)
                else:
                    pe.wait_ge(route_z, n + 1)
                    pe.wait_ge(xs_sb, n + 1)
                grids = bank[4 + k].rearrange("p (h w) -> p h w", w=SIDE)
                for step in steps:
                    t = PYR_ORDER[step]
                    for d, dil in enumerate(DILS):
                        dy, dx = (t // 3 - 1) * dil, (t % 3 - 1) * dil
                        y0, y1, x0, x1 = 16 * k, 16 * k + 16, 0, SIDE
                        if step not in (0, 8):
                            (y0, y1), (x0, x1) = inside(16 * k, 16, dy), inside(0, SIDE, dx)
                        if y1 > y0:
                            last = pe.matmul(grids[32 * d:32 * d + 32, y0 - 16 * k:y1 - 16 * k, x0:x1], w_pyr[:, d, t],
                                             act[:, PAD + y0 + dy:PAD + y1 + dy, PAD + x0 + dx:PAD + x1 + dx],
                                             start=(step == 0), stop=(step == 8))
                        if step == 8 and d == len(DILS) - 1:
                            last.then_inc(pyr_ps, 1)
                    for g in range(2):
                        for e in EDGE_TAPS[step][g]:
                            first, final = e in (0, 4), e in (3, 8)
                            last = pe.matmul(bank[7 - k][64 + 32 * g:96 + 32 * g, :], w_vis[:, e], tap(16 * k, 16, 1, e),
                                             start=first, stop=final)
                            if final:
                                last.then_inc(edge_ps, 1)

            def x2_conv(n):
                for k in range(2):
                    pe.wait_ge(edge_parts, 2 * n + 2)
                    pe.wait_ge(xs_sb, n + 1)
                    multiply4(bank[6 + k], xs, k, mat("fgm2")).then_inc(x2_ps, 1)

            def dft_rows(n):
                for k in range(2):
                    pe.wait_ge(x2_sb, 2 * n + k + 1)
                    pe.wait_ge(pyr_sb, 2 * n + k + 1)
                    multiply4(bank[4 + k], fa, k, con("dft_h")).then_inc(h_ps, 1)

            def turn_spectrum(n):
                for k in range(2):
                    pe.wait_ge(h_sb, 2 * n + 2)
                    turn4(bank[6 + k], fb, k).then_inc(t_ps, 1)

            def r_even(n):
                for k in range(2):
                    pe.wait_ge(xe_sb, n + 1)
                    pe.wait_ge(h_sb, 2 * n + k + 1)
                    multiply4(bank[4 + k], xe, k, mat("fgm1")).then_inc(r1_ps, 1)

            def dft_columns(n):
                for k in range(2):
                    pe.wait_ge(t_sb, 2 * n + k + 1)
                    if k == 0:
                        pe.matmul(bank[6][:, 0:P], con("dft_w0"), fa[:, 0:P], start=True, stop=True)
                        last = pe.matmul(bank[6][:, P:4 * P], con("dft_w"), fa[:, P:4 * P], start=True, stop=True)
                    else:
                        last = pe.matmul(bank[7][:], con("dft_w"), fa[:, 4 * P:8 * P], start=True, stop=True)
                    last.then_inc(w_ps, 1)

            def r_odd(n):
                for k in range(2):
                    pe.wait_ge(xo_sb, n + 1)
                    pe.wait_ge(r1_sb, 2 * n + k + 1)
                    multiply4(bank[4 + k], xo, k, mat("fgm1")).then_inc(r2_ps, 1)

            def inverse_even(n):
                for k in range(2):
                    pe.wait_ge(ge_sb, n + 1)
                    pe.wait_ge(w_sb, 2 * n + 2)
                    multiply4(bank[6 + k], fc, k, con("even"), con("even0")).then_inc(ae_ps, 1)

            def inverse_odd(n):
                for k in range(2):
                    pe.wait_ge(edge_sb, 2 * n + k + 1)
                    multiply4(bank[4 + k], fd, k, con("odd"), con("odd0")).then_inc(ao_ps, 1)

            def turn_even(n):
                for k in range(2):
                    pe.wait_ge(ae_sb, 2 * n + 2)
                    turn4(bank[6 + k], fa, k).then_inc(te_ps, 1)

            def turn_odd(n):
                for k in range(2):
                    pe.wait_ge(ao_sb, 2 * n + 2)
                    turn4(bank[4 + k], fb, k).then_inc(to_ps, 1)

            def last_even(n):
                for k in range(2):
                    pe.wait_ge(te_sb, 2 * n + k + 1)
                    multiply4(bank[6 + k], fc, k, con("idft_h")).then_inc(be_ps, 1)

            def last_odd(n):
                for k in range(2):
                    pe.wait_ge(to_sb, 2 * n + k + 1)
                    multiply4(bank[4 + k], fd, k, con("idft_h")).then_inc(bo_ps, 1)

            def out_conv(n):
                for k in range(2):
                    pe.wait_ge(relu_sb, n + 1)
                    pe.wait_ge(be_sb, 2 * n + k + 1)
                    pe.matmul(bank[6 + k][:], mat("out"), relu[:, HALF * k:HALF * k + HALF],
                              start=True, stop=True).then_inc(out_ps, 1)

            def conv_early(n, j):
                if j == 1:
                    pyramid(n, 1, range(6, 9))
                elif j == 2:
                    dft_rows(n)
                elif j == 3:
                    r_even(n)
                elif j == 6:
                    inverse_odd(n)
                elif j == 7:
                    turn_odd(n)

            def conv_late(n, j):
                if j == 0:
                    pyramid(n, 1, range(5, 6))
                elif j == 1:
                    x2_conv(n)
                elif j == 2:
                    turn_spectrum(n)
                elif j == 3:
                    dft_columns(n)
                elif j == 4:
                    r_odd(n)
                elif j == 5:
                    inverse_even(n)
                    edge_spread(n)
                elif j == 6:
                    turn_even(n)
                elif j == 7:
                    last_even(n)

            def swin_rest(i):
                queries_keys(i)
                v(i)
                scores(i, 0)
                scores(i, 1)
                for j in range(PAIRS):
                    if j + 2 < PAIRS:
                        scores(i, j + 2)
                    prob_transposes(i, j)
                    values(i, j)
                project(i, 0)
                project(i, 1)
                n2_transposes(i, 0)
                mlp(i)

            def both(n, i):
                in_conv(n)
                x_transposes(i)
                pyramid(n, 0, range(0, 2))
                gap_products(n)
                pyramid(n, 0, range(2, 7))
                n_transposes(i)
                mid_products(n)
                queries_keys(i)
                v(i)
                pyramid(n, 0, range(7, 9))
                scores(i, 0)
                scores(i, 1)
                pyramid(n, 1, range(0, 5))
                for j in range(PAIRS):
                    if j == PAIRS - 1:
                        project(i, 0)
                    if j + 2 < PAIRS:
                        scores(i, j + 2)
                    conv_early(n, j)
                    prob_transposes(i, j)
                    conv_late(n, j)
                    values(i, j)
                last_odd(n)
                project(i, 1)
                n2_transposes(i, 0)
                mlp(i)
                out_conv(n)

            def conv_only(n):
                in_conv(n)
                gap_products(n)
                pyramid(n, 0, range(0, 9))
                mid_products(n)
                pyramid(n, 1, range(0, 5))
                for j in range(PAIRS):
                    conv_early(n, j)
                    conv_late(n, j)
                last_odd(n)
                out_conv(n)

            pe.wait_ge(loaded, 16 * LOADS)
            for k in range(3):
                pe.matmul(bank[4][:, k:k + 1], w_qkv[:, k * C:(k + 1) * C], col("ln1_b"), start=True, stop=True)
            for f in range(FC):
                last = pe.matmul(bank[4][:, 3 + f:4 + f], w_up[:, f * P:(f + 1) * P], col("ln2_b"),
                                 start=True, stop=True)
            last.then_inc(fold_ps, 1)
            x_transposes(0)

            table = mat("table").rearrange("p (c h) -> p c h", c=2)
            oh = [k_heads[:, 8:16].rearrange("p a h k -> p (a h k)"), fft[:].rearrange("p a t -> p (a t)")]

            def bias_rows(half):
                pe.wait_ge(onehot_ready, 2 * half + 2)
                for c in range(2):
                    for g in range(4):
                        at = (4 * half + g) * HALF
                        last = pe.matmul(bank[6 + half][32 * g:32 * g + 32, :], table[:, c], oh[c][:, at:at + HALF],
                                         start=(c == 0), stop=(c == 1))
                last.then_inc(rel_ps, 1)

            def bias_turns(half):
                pe.wait_ge(rel_rows_sb, half + 1)
                pe.wait_ge(xT_sb, 2)
                for u in range(2):
                    for r in range(4):
                        for w in range(2):
                            at = half * HALF + (4 * u + r) * WT
                            last = pe.matmul(rel_banks[2 * half + u][64 * w:64 * w + 64, r * P:(r + 1) * P],
                                             rel_rows[:, at:at + WT], ident, start=True, stop=True)
                    last.then_inc(rel_ps, 1)

            bias_rows(0)
            bias_rows(1)
            pe.wait_ge(v_wide_ready, 1)
            pe.matmul(bank[4][:, P:2 * P], y_out[:, 0:P], w_proj, start=True, stop=True).then_inc(shift_ps, 1)
            n_transposes(0)
            bias_turns(0)
            bias_turns(1)
            pe.wait_ge(setup_dve, 1)

            swin_rest(0)
            both(0, 1)
            with pe.Fori(1, IMAGES - 1) as n:
                both(n, n + 1)
            conv_only(IMAGES - 1)

        @block.vector
        def _(dve):
            dve.memset(ones[:], 1.0)
            dve.memset(eps[:], LN_EPS)
            dve.memset(cut_bias[:], 0.85)
            dve.memset(edge[:], 0.0)
            def norm_stats(source, done, chunks=range(CH)):
                for c in chunks:
                    dve.bn_stats(stats[:, c], source(c))
                dve.drain()
                for c in chunks:
                    last = dve.bn_aggr(mv[:, c], stats[:, c])
                last.then_inc(done, 1)

            def normalise(source, done, chunks=range(CH)):
                part = slice(chunks[0], chunks[-1] + 1)
                dve.reciprocal(rstd[:, part], std[:, part])
                dve.drain()
                for c in chunks:
                    last = dve.tensor_scalar(nT[:, c], source[:, c], mv[:, c, 0:1], rstd[:, c:c + 1],
                                             ALU.subtract, ALU.mult)
                    if c % 4 == 3:
                        last.then_inc(done, 1)

            def norm1_stats(i):
                dve.wait_ge(xT_sb, 2 * i + 2)
                norm_stats(lambda c: xT[:, c], ln1_var)

            def norm1(i):
                dve.wait_ge(ln1_std, i + 1)
                dve.wait_ge(xT_sb, 2 * i + 2)
                dve.wait_ge(n2T_ps, 2 * i)
                normalise(xT, nT_sb)

            def keys(i):
                for k in range(2):
                    dve.wait_ge(k_ps, 2 * i + k + 1)
                    dve.wait_ge(kh_act, i)
                    dve.tensor_scalar(kC[:, HALF * k:HALF * k + HALF], bank[2 + k][:], fold_b[:, 1:2], None,
                                      ALU.add).then_inc(k_sb, 1)

            def key_heads(i):
                dve.drain()
                dve.wait_ge(down_ps, 2 * i)
                for h in DVE_HEADS:
                    last = dve.tensor_scalar(k_heads[:, :, h], kC.rearrange("p (w k) -> p w k", w=WIN),
                                             head_mask(h), None, ALU.mult)
                last.then_inc(kh_dve, 1)

            def bias_max(i, j):
                dve.wait_ge(s_ps, 8 * i + j + 1)
                if j >= 3:
                    dve.wait_ge(p_sb, 8 * i + j - 2)
                dve.tensor_tensor(score[:, j % 3].rearrange("p h k -> p (h k)"), bank[2 + j % 2][:], rel_bias[:],
                                  ALU.add).then_inc(s_biased, 1)
                dve.drain()
                dve.tensor_reduce(row_max[:, j % 3], score[:, j % 3], AX.X, ALU.max).then_inc(s_max, 1)

            def row_sums(i, j):
                dve.wait_ge(s_exp, 8 * i + j + 1)
                dve.tensor_reduce(row_sum[:, j % 3], score[:, j % 3], AX.X, ALU.add)
                dve.drain()
                dve.reciprocal(row_inv[:, j % 3], row_sum[:, j % 3]).then_inc(s_inv, 1)

            def residual_stats(i, k):
                dve.wait_ge(proj_ps, 2 * i + k + 1)
                dve.wait_ge(res_sb, i + 1)
                dve.tensor_tensor(x1T[:, 4 * k:4 * k + 4].rearrange("p c d -> p (c d)"), bank[2 + k][:],
                                  resT[:, 4 * k:4 * k + 4].rearrange("p c d -> p (c d)"), ALU.add)\
                   .then_inc(x1_sb, 1)
                dve.drain()
                norm_stats(lambda c: x1T[:, c], ln2_var, range(4 * k, 4 * k + 4))

            def norm2(i, k):
                dve.wait_ge(ln2_std, 2 * i + k + 1)
                normalise(x1T, n2T_sb, range(4 * k, 4 * k + 4))

            def swin_out(i, k):
                dve.wait_ge(down_ps, 2 * i + k + 1)
                dve.wait_ge(in_ps, 2 * i)
                dve.wait_ge(pyramid_gated, i)
                for a in range(2):
                    last = dve.tensor_scalar(natural_windows(xm[:], 2 * k + a), windows(bank[(0, 3)[k]][:], a),
                                             col("b2"), None, ALU.add)
                last.then_inc(xm_sb, 1)

            def gap(n):
                dve.wait_ge(act_sb, 2 * n + 2)
                dve.tensor_scalar(vec[:, 0:1], sums[:, 0:1], sums[:, 1:2], 1.0 / TOK, ALU.add, ALU.mult)\
                   .then_inc(gap_sb, 1)

            def attention_vectors(n):
                dve.wait_ge(gap_ps, n + 1)
                dve.wait_ge(abs_sb, n + 1)
                dve.tensor_scalar(vec[:, 1:2], bank[6][:, 0:1], col("fac_b"), None, ALU.add)
                dve.tensor_scalar(vec[0:BATT, 4:5], bank[6][0:BATT, 1:2], col("batt_b1")[0:BATT], 0.0,
                                  ALU.add, ALU.max)
                dve.drain()
                dve.tensor_scalar(vec[:, 2:3], vec[:, 1:2], -1.0, None, ALU.mult)
                dve.tensor_scalar(batt_wide[0:BATT], ones[0:BATT], vec[0:BATT, 4:5], None, ALU.mult)
                dve.drain()
                dve.tensor_tensor(vec[:, 3:4], vec[:, 1:2], vec[:, 2:3], ALU.max)
                dve.drain()
                dve.tensor_scalar(vec[:, 5:6], sums[:, 2:3], vec[:, 3:4], 1.0 / TOK, ALU.mult, ALU.mult)\
                   .then_inc(mid_sb, 1)

            def scaled_input(n):
                dve.wait_ge(mid_ps, n + 1)
                dve.tensor_tensor(route[:, 0], bank[6][:, 8:8 + ROUTES], row("batt_b2"), ALU.add)\
                   .then_inc(route_z, 1)
                dve.tensor_scalar(vec[:, 6:7], bank[6][:, 2:3], col("conv_b"), vec[:, 3:4], ALU.add, ALU.mult)
                dve.drain()
                dve.tensor_scalar(xs[:], xs[:], vec[:, 6:7], None, ALU.mult).then_inc(xs_sb, 1)

            def mirrored(dst, op):
                d = dst.rearrange("p (a r k) -> p a r k", a=16, r=2)
                rows_, back, two = xs_hw[:, 1:16], xs_hw[:, 31:16:-1], xs_hw[:, 0:17:16]
                dve.tensor_tensor(d[:, 1:16, :, 1:32], rows_[:, :, 1:32].unsqueeze(2).broadcast_to([P, 15, 2, 31]),
                                   back[:, :, 31:0:-1].unsqueeze(2).broadcast_to([P, 15, 2, 31]), op)
                dve.tensor_tensor(d[:, 1:16, :, 0], rows_[:, :, 0:1].broadcast_to([P, 15, 2]),
                                   back[:, :, 0:1].broadcast_to([P, 15, 2]), op)
                m = d[:, 0, :, 2:32].rearrange("p r (m u) -> p r m u", u=2)
                dve.tensor_tensor(m, two[:, :, 1:16].unsqueeze(3).broadcast_to([P, 2, 15, 2]),
                                   two[:, :, 31:16:-1].unsqueeze(3).broadcast_to([P, 2, 15, 2]), op)
                return dve.tensor_tensor(d[:, 0, :, 0:2], two[:, :, 0:17:16], two[:, :, 0:17:16], op)

            def even_part(n):
                dve.drain()
                dve.wait_ge(r1_ps, 2 * n)
                mirrored(xe[:], ALU.add).then_inc(xe_sb, 1)

            def odd_part(n):
                dve.wait_ge(r2_ps, 2 * n)
                mirrored(xo[:], ALU.subtract).then_inc(xo_sb, 1)

            def route_logits(n):
                dve.wait_ge(route_e, n + 1)
                dve.scalar_tensor_tensor(route[:, 2], route[:, 1], 1.0, base[:], ALU.add, ALU.mult)
                dve.drain()
                dve.tensor_reduce(vec[:, 7:8], route[:, 2], AX.X, ALU.max)
                dve.drain()
                dve.tensor_scalar(route[:, 0], route[:, 2], vec[:, 7:8], None, ALU.subtract)\
                   .then_inc(route_d, 1)

            def route_weights(n):
                dve.wait_ge(route_f, n + 1)
                dve.tensor_reduce(vec[:, 8:9], route[:, 1], AX.X, ALU.add)
                dve.drain()
                dve.reciprocal(vec[:, 9:10], vec[:, 8:9])
                dve.drain()
                cw = route[:, 3]
                dve.tensor_scalar(cw, route[:, 1], vec[:, 9:10], None, ALU.mult)
                dve.drain()
                dve.wait_ge(py_sb, n)
                at = COLS["cr_w"][0]
                dve.tensor_tensor(cr_scaled[:], cols_sb[:, at:at + 27].rearrange("p (a t) -> p a t", a=3),
                                  cw[:, 0:3].unsqueeze(2).broadcast_to([P, 3, 9]), ALU.mult)
                at = COLS["cr_b"][0]
                dve.tensor_tensor(cr_bias[:], cols_sb[:, at:at + 3], cw[:, 0:3], ALU.mult)
                dve.drain()
                dve.tensor_scalar(cr_scaled[:, 0:2], cr_scaled[:, 0:2], 0.5, None, ALU.mult)
                dve.tensor_tensor(mix[:, 0:1], col("dw_w"), cw[:, 3:4], ALU.mult)
                dve.tensor_tensor(mix[:, 1:2], col("dw_b"), cw[:, 3:4], ALU.mult)
                dve.tensor_tensor(mix[:, 2:3], col("alpha"), cw[:, 4:5], ALU.mult)
                dve.tensor_tensor(mix[:, 3:4], col("beta"), cw[:, 4:5], ALU.mult)
                dve.drain()
                dve.tensor_scalar(mix[:, 4:5], cr_bias[:, 0:1], cr_bias[:, 1:2], 0.5, ALU.add, ALU.mult).then_inc(cw_sb, 1)

            def taps(n, which):
                for t in which:
                    a, k = divmod(t, 9)
                    src = (hor, ver)[a][:, k // 3:k // 3 + SIDE, k % 3:k % 3 + SIDE]
                    dve.drain()
                    if t == 9:
                        dve.wait_ge(axis_sb, 2 * n + 2)
                    if t == 0:
                        dve.wait_ge(axis_sb, 2 * n + 1)
                        dve.wait_ge(relu_sb, n)
                        last = dve.tensor_scalar(hv[:], src, cr_scaled[:, a, k:k + 1], mix[:, 4:5], ALU.mult, ALU.add)
                    else:
                        last = dve.scalar_tensor_tensor(hv[:], src, cr_scaled[:, a, k:k + 1], hv[:], ALU.mult,
                                                        ALU.add)
                    if t == 17:
                        last.then_inc(hv_sb, 1)

            def r_even_bias(n):
                for k in range(2):
                    dve.wait_ge(r1_ps, 2 * n + k + 1)
                    dve.tensor_tensor(fc[:, HALF * k:HALF * k + HALF].rearrange("p (g c) -> p g c", g=4),
                                      bank[4 + k].rearrange("p (g c) -> p g c", g=4),
                                      two_b1[:].unsqueeze(1).broadcast_to([P, 4, C]), ALU.add).then_inc(r1_sb, 1)

            def boosted(n):
                for k in range(2):
                    dve.wait_ge(w_ps, 2 * n + k + 1)
                    dve.wait_ge(t_ps, 2 * n + 2)
                    last = dve.tensor_tensor(fb[:, HALF * k:HALF * k + HALF], bank[6 + k][:],
                                             boost[:, 4 * k:4 * k + 4].rearrange("p g c -> p (g c)"), ALU.mult)
                last.then_inc(w_sb, 1)
                dve.drain()
                dve.tensor_tensor(fb[0:1, 0:C], fb[0:1, 0:C], dc_b2[0:1], ALU.add).then_inc(w_sb, 1)

            def even_product(n):
                dve.drain()
                dve.tensor_tensor(fc, fc, fb, ALU.mult).then_inc(ge_sb, 1)

            def odd_product(n):
                dve.drain()
                for k in range(2):
                    h = slice(HALF * k, HALF * k + HALF)
                    dve.wait_ge(r2_ps, 2 * n + k + 1)
                    dve.tensor_tensor(fd[:, h], bank[4 + k][:], fb[:, h], ALU.mult).then_inc(go_sb, 1)

            def mix_input(n):
                dve.wait_ge(abs_sb, n + 1)
                dve.scalar_tensor_tensor(grid(xm[:]), act_in, mix[:, 0:1], grid(xm[:]), ALU.mult, ALU.add)
                dve.drain()
                dve.scalar_tensor_tensor(grid(xm[:]), xs_hw, mix[:, 3:4], grid(xm[:]), ALU.mult, ALU.add)\
                   .then_inc(xm_mixed, 1)

            def gate_axes(n):
                dve.drain()
                dve.wait_ge(edge_sb, 2 * n + 2)
                dve.scalar_tensor_tensor(hv[:], edge[:], 3.0, hv[:], ALU.add, ALU.mult).then_inc(gated_sb, 1)

            def add_magnitude(n):
                dve.drain()
                dve.wait_ge(mag_sb, n + 1)
                dve.scalar_tensor_tensor(hv[:], grid(fa), mix[:, 2:3], hv[:], ALU.mult, ALU.add)

            def mixture(n):
                dve.drain()
                dve.wait_ge(pyramid_gated, n + 1)
                dve.tensor_tensor(hv[:], hv[:], py[:], ALU.add).then_inc(mixed_sb, 1)

            def conv_slot(n, j):
                if j == 0:
                    mix_input(n)
                elif j == 1:
                    odd_part(n)
                elif j == 5:
                    even_product(n)
                    odd_product(n)
                taps(n, range(SLOT_TAPS[j], SLOT_TAPS[j + 1]))
                if j == 4:
                    boosted(n)

            def swin_rest(i):
                keys(i)
                key_heads(i)
                bias_max(i, 0)
                bias_max(i, 1)
                for j in range(PAIRS):
                    row_sums(i, j)
                    if j + 2 < PAIRS:
                        bias_max(i, j + 2)
                residual_stats(i, 0)
                norm2(i, 0)
                residual_stats(i, 1)
                norm2(i, 1)
                swin_out(i, 0)
                swin_out(i, 1)

            def both(n, i):
                gap(n)
                norm1_stats(i)
                attention_vectors(n)
                norm1(i)
                keys(i)
                key_heads(i)
                scaled_input(n)
                even_part(n)
                bias_max(i, 0)
                route_logits(n)
                bias_max(i, 1)
                for j in range(PAIRS):
                    row_sums(i, j)
                    if j == 0:
                        route_weights(n)
                    conv_slot(n, j)
                    if j + 2 < PAIRS:
                        bias_max(i, j + 2)
                    if j == 3:
                        r_even_bias(n)
                residual_stats(i, 0)
                norm2(i, 0)
                residual_stats(i, 1)
                norm2(i, 1)
                taps(n, range(SLOT_TAPS[PAIRS], 18))
                gate_axes(n)
                add_magnitude(n)
                mixture(n)
                swin_out(i, 0)
                swin_out(i, 1)

            def conv_only(n):
                gap(n)
                attention_vectors(n)
                scaled_input(n)
                even_part(n)
                route_logits(n)
                route_weights(n)
                for j in range(PAIRS):
                    conv_slot(n, j)
                    if j == 3:
                        r_even_bias(n)
                taps(n, range(SLOT_TAPS[PAIRS], 18))
                gate_axes(n)
                add_magnitude(n)
                mixture(n)

            dve.wait_ge(loaded, 16 * LOADS)
            dve.tensor_reduce(tiny[:, 0:1], row("base"), AX.X, ALU.max)
            dve.drain()
            dve.tensor_scalar(base[:], row("base"), tiny[:, 0:1], None, ALU.subtract).then_inc(setup_z, 1)
            dve.wait_ge(fold_ps, 1)
            scale = float(HD) ** -0.5
            dve.tensor_scalar(fold_b[:, 0:1], bank[4][:, 0:1], col("q_b"), scale, ALU.add, ALU.mult)
            dve.tensor_scalar(fold_b[:, 1:2], bank[4][:, 1:2], col("k_b"), None, ALU.add)
            dve.tensor_scalar(fold_b[:, 2:3], bank[4][:, 2:3], col("v_b"), None, ALU.add)
            dve.tensor_tensor(fold_b[:, 3:3 + FC], bank[4][:, 3:3 + FC],
                              cols_sb[:, COLS["b1"][0]:COLS["b1"][0] + FC], ALU.add)
            dve.drain()
            dve.tensor_scalar(y_out[:, 0:P], ones[:], fold_b[:, 2:3], None, ALU.mult)\
               .then_inc(v_wide_ready, 1)

            index = k_heads[:, 0:8].rearrange("p a h k -> p (a h k)").bitcast(I32)
            oh = [k_heads[:, 8:16].rearrange("p a h k -> p (a h k)"), fft[:].rearrange("p a t -> p (a t)")]

            def onehot(half):
                part = slice(half * WT * WT // 2, (half + 1) * WT * WT // 2)
                for c in range(2):
                    at = CONS["iota"][0] + c
                    dve.tensor_scalar(oh[c][:, part], index[:, part], cons_sb[:, at:at + 1], None, ALU.is_equal)\
                       .then_inc(onehot_ready, 1)

            dve.wait_ge(index_low, 16)
            onehot(0)
            dve.wait_ge(index_high, 16)
            onehot(1)
            norm1_stats(0)
            norm1(0)
            for half in range(2):
                dve.wait_ge(rel_ps, half + 1)
                dve.tensor_copy(rel_rows[:, half * HALF:half * HALF + HALF], bank[6 + half][:])\
                   .then_inc(rel_rows_sb, 1)
            dve.tensor_scalar(half_vis_b[:], col("vis_b"), 0.5, None, ALU.mult)
            dve.tensor_copy(w_vis[:], mat("vis").unsqueeze(2).broadcast_to([P, 9, 32]))
            dve.tensor_scalar(fuse_bias[:], col("pyr_b"), col("fuse_w"), col("fuse_b"), ALU.mult, ALU.add)
            dve.tensor_scalar(two_b1[:], row("fgm_b1"), 2.0, None, ALU.mult)
            dve.tensor_scalar(dc_b2[:], row("fgm_b2"), float(TOK), None, ALU.mult)
            for g in range(CH):
                at = CONS["high"][0] + g
                dve.tensor_scalar(boost[:, g], row("boost"), cons_sb[:, at:at + 1], 1.0, ALU.mult, ALU.add)
            dve.tensor_scalar(w_qkv[:, 0:C], w_qkv[:, 0:C], col("ln1_g"), scale, ALU.mult, ALU.mult)
            dve.tensor_scalar(w_qkv[:, C:3 * C], w_qkv[:, C:3 * C], col("ln1_g"), None, ALU.mult)
            dve.tensor_scalar(w_up, w_up, col("ln2_g"), None, ALU.mult)
            dve.wait_ge(setup_exp, 1)
            dve.tensor_reduce(tiny[:, 1:2], base[:], AX.X, ALU.add)
            dve.drain()
            dve.reciprocal(tiny[:, 2:3], tiny[:, 1:2])
            dve.drain()
            dve.tensor_scalar(base[:], base[:], tiny[:, 2:3], 0.5, ALU.mult, ALU.mult)
            dve.wait_ge(shift_ps, 1)
            dve.tensor_tensor(proj_shift[:], bank[4][:, P:2 * P], row("proj_b"), ALU.add)
            to = rel_bias.rearrange("p (h a g u r) -> p a u h g r", h=HEADS, a=2, g=4, u=2)
            for half in range(2):
                for u in range(2):
                    dve.wait_ge(rel_ps, 3 + 2 * half + u)
                    of = rel_banks[2 * half + u].rearrange("p (r g h) -> p h g r", r=4, g=4)
                    dve.tensor_copy(to[:, half, u], of[:, 0:HEADS])
            dve.drain()
            dve.sem_inc(setup_dve, 1)

            swin_rest(0)
            both(0, 1)
            with dve.Fori(1, IMAGES - 1) as n:
                both(n, n + 1)
            conv_only(IMAGES - 1)

        @block.scalar
        def _(act_):
            act_.wait_ge(setup_z, 1)
            act_.activation(base[:], base[:], ACT.Exp).then_inc(setup_exp, 1)

            def to_windows(i):
                act_.wait_ge(x_loaded, 16 * i + 16)
                act_.wait_ge(proj_ps, 2 * i)
                for a in range(4):
                    last = act_.activation(windows(xw[:], a), natural_windows(x_in[:], a), ACT.Copy)
                last.then_inc(xw_ready, 1)

            def x_copy(i):
                for k in range(2):
                    act_.wait_ge(xT_ps, 2 * i + k + 1)
                    act_.wait_ge(down_ps, 2 * i)
                    act_.activation(xT[:, 4 * k:4 * k + 4].rearrange("p c d -> p (c d)"), bank[k][:], ACT.Copy)\
                        .then_inc(xT_sb, 1)

            def deviation1(i):
                act_.wait_ge(ln1_var, i + 1)
                act_.activation(std[:], mv[:, :, 1], ACT.Sqrt, bias=eps[:]).then_inc(ln1_std, 1)

            def deviation2(i, k):
                act_.wait_ge(ln2_var, 2 * i + k + 1)
                act_.activation(std[:, 4 * k:4 * k + 4], mv[:, 4 * k:4 * k + 4, 1], ACT.Sqrt, bias=eps[:])\
                    .then_inc(ln2_std, 1)

            def copy(dst, src):
                return act_.activation(dst, src, ACT.Copy)

            def half(ap, k):
                return ap[:, HALF * k:HALF * k + HALF]

            def n_copy(i):
                for k in range(2):
                    act_.wait_ge(nT_ps, 2 * i + k + 1)
                    copy(half(nC, k), bank[2 + k][:]).then_inc(nC_sb, 1)

            def n2_copy(i, k):
                act_.wait_ge(n2T_ps, 2 * i + k + 1)
                copy(half(nC, k), bank[k][:]).then_inc(n2C_sb, 1)

            def queries(i):
                for k in range(2):
                    act_.wait_ge(q_ps, 2 * i + k + 1)
                    act_.activation(qC[:, HALF * k:HALF * k + HALF], bank[k][:], ACT.Identity, bias=fold_b[:, 0:1])\
                        .then_inc(q_sb, 1)

            def key_heads(i):
                act_.wait_ge(k_sb, 2 * i + 2)
                act_.wait_ge(down_ps, 2 * i)
                for h in ACT_HEADS:
                    last = act_.activation(k_heads[:, :, h], kC.rearrange("p (w k) -> p w k", w=WIN), ACT.Copy,
                                           scale=head_mask(h))
                last.then_inc(kh_act, 1)

            def v_copy(i):
                for k in range(2):
                    act_.wait_ge(v_ps, 2 * i + k + 1)
                    for e in range(2):
                        dst = v_pair[64 * e:64 * e + 64, 8 * k:8 * k + 8, :, e].rearrange("p w g d -> p (w g) d")
                        src = bank[k][64 * e:64 * e + 64, :].rearrange("p (w d) -> p w d", d=HD)
                        last = act_.activation(dst, src, ACT.Copy)
                    last.then_inc(v_sb, 1)

            def exponent(i, j):
                act_.wait_ge(s_sub, 8 * i + j + 1)
                act_.activation(score[:, j % 3].rearrange("p h k -> p (h k)"),
                                score[:, j % 3].rearrange("p h k -> p (h k)"), ACT.Exp).then_inc(s_exp, 1)

            def prob_copy(i, j):
                act_.wait_ge(pT_ps, 8 * i + j + 1)
                act_.activation(probT[:, j % 2].rearrange("p g t -> p (g t)"), bank[0][:], ACT.Copy)\
                    .then_inc(pT_sb, 1)

            def attention_copy(i, k):
                act_.wait_ge(o_ps, 8 * i + 4 * k + 4)
                act_.activation(attn_out[:, HALF * k:HALF * k + HALF], bank[1][:], ACT.Copy).then_inc(o_sb, 1)

            def mlp_gelu(i, n=None):
                act_.activation(first_gelu[:], ones[:, 0:1], ACT.Gelu)
                for t in range(2 * FC):
                    k, f = divmod(t, FC)
                    act_.wait_ge(up_ps, 8 * i + t + 1)
                    act_.activation(hidden[:, f, HALF * k:HALF * k + HALF], bank[(2, 3, 0, 1, 2, 3, 1, 2)[t]][:],
                                    ACT.Gelu, bias=fold_b[:, 3 + f:4 + f]).then_inc(up_sb, 1)
                    if t == 1 and n is not None:
                        pyr_tap(n, 8)

            def in_gelu(n):
                for k in range(2):
                    act_.wait_ge(in_ps, 2 * n + k + 1)
                    act_.activation(act[:, PAD + 16 * k:PAD + 16 * k + 16, PAD:PAD + SIDE],
                                    bank[4 + k].rearrange("p (h w) -> p h w", w=SIDE), ACT.Gelu, bias=col("in_b"),
                                    accum_out=sums[:, k:k + 1]).then_inc(act_sb, 1)

            def magnitudes(n):
                act_.drain()
                act_.wait_ge(mixed_sb, n)
                act_.activation(xs_hw, act_in, ACT.Abs, accum_out=sums[:, 2:3]).then_inc(abs_sb, 1)

            def edge_parts_copy(n, k):
                act_.wait_ge(edge_ps, 4 * n + 2 * k + 2)
                act_.wait_ge(gated_sb, n)
                act_.activation(edge[64:P, 16 * k:16 * k + 16],
                                bank[7 - k][64:P, :].rearrange("p (h w) -> p h w", w=SIDE), ACT.Copy)\
                    .then_inc(edge_parts, 1)

            def route_tanh(n):
                act_.wait_ge(route_z, n + 1)
                act_.activation(route[:, 1], route[:, 0], ACT.Tanh, scale=0.5).then_inc(route_e, 1)

            def route_exponent(n):
                act_.wait_ge(route_d, n + 1)
                act_.activation(route[:, 1], route[:, 0], ACT.Exp).then_inc(route_f, 1)

            def edge_tanh(n):
                for k in range(2):
                    act_.wait_ge(eb_ps, 2 * n + k + 1)
                    act_.activation(edge[:, 16 * k:16 * k + 16], bank[4 + k].rearrange("p (h w) -> p h w", w=SIDE),
                                    ACT.Tanh, bias=half_vis_b[:], scale=0.5).then_inc(edge_sb, 1)

            def edge_cuts(n):
                act_.drain()
                act_.wait_ge(axis_sb, 2 * n + 2)
                act_.activation(edge_cut[:], edge[:], ACT.Identity, bias=cut_bias[:], scale=-0.15).then_inc(cut_sb, 1)

            def pyr_copy(n, k):
                act_.wait_ge(pyr_ps, 2 * n + k + 1)
                act_.wait_ge(py_sb, n)
                act_.activation(pyr[:, 1 + 16 * k:17 + 16 * k, 1:1 + SIDE],
                                bank[4 + k].rearrange("p (h w) -> p h w", w=SIDE), ACT.Identity, bias=fuse_bias[:],
                                scale=col("fuse_w")).then_inc(pyr_sb, 1)

            def pyr_tap(n, k):
                src = pyr[:, k // 3:k // 3 + SIDE, k % 3:k % 3 + SIDE]
                if k == 0:
                    act_.drain()
                    act_.wait_ge(mixed_sb, n)
                    act_.wait_ge(cw_sb, n + 1)
                    act_.activation(py[:], src, ACT.Identity, bias=cr_bias[:, 2:3], scale=cr_scaled[:, 2, 0:1])\
                        .then_inc(part_sb, 1)
                    return
                if k > 2:
                    act_.wait_ge(part_added, 8 * n + k - 2)
                act_.activation(grid(parts[k][:, 0:TOK]), src, ACT.Copy, scale=cr_scaled[:, 2, k:k + 1])\
                    .then_inc(part_sb, 1)

            def other_order(dst, k):
                return dst.rearrange("c (a b) -> c b a", b=SIDE)[:, 16 * k:16 * k + 16]

            def rows_of(ps):
                return ps.rearrange("c (b a) -> c b a", a=SIDE)

            def square(dst, ps, k):
                to = dst.rearrange("c (h j w) -> c j h w", j=CH, w=4)[:, 4 * k:4 * k + 4]
                return act_.activation(to, ps.rearrange("c (j h w) -> c j h w", j=4, w=4), ACT.Square)

            def x2_copy(n):
                for k in range(2):
                    act_.wait_ge(x2_ps, 2 * n + k + 1)
                    copy(half(fa, k), bank[6 + k][:]).then_inc(x2_sb, 1)

            def row_spectrum_copy(n):
                for k in range(2):
                    act_.wait_ge(h_ps, 2 * n + k + 1)
                    copy(other_order(fb, k), rows_of(bank[4 + k])).then_inc(h_sb, 1)

            def spectrum_turn_copy(n):
                for k in range(2):
                    act_.wait_ge(t_ps, 2 * n + k + 1)
                    copy(half(fa, k), bank[6 + k][:]).then_inc(t_sb, 1)

            def inverse_even_copy(n):
                for k in range(2):
                    act_.wait_ge(ae_ps, 2 * n + k + 1)
                    copy(other_order(fa, k), rows_of(bank[6 + k])).then_inc(ae_sb, 1)

            def inverse_odd_copy(n):
                act_.wait_ge(go_sb, 2 * n + 2)
                for k in range(2):
                    act_.wait_ge(ao_ps, 2 * n + k + 1)
                    copy(other_order(fb, k), rows_of(bank[4 + k])).then_inc(ao_sb, 1)

            def turn_even_copy(n):
                for k in range(2):
                    act_.wait_ge(te_ps, 2 * n + k + 1)
                    copy(half(fc, k), bank[6 + k][:]).then_inc(te_sb, 1)

            def turn_odd_copy(n):
                for k in range(2):
                    act_.wait_ge(to_ps, 2 * n + k + 1)
                    copy(half(fd, k), bank[4 + k][:]).then_inc(to_sb, 1)

            def square_even(n):
                for k in range(2):
                    act_.wait_ge(be_ps, 2 * n + k + 1)
                    square(fa, bank[6 + k], k).then_inc(be_sb, 1)

            def square_odd(n):
                for k in range(2):
                    act_.wait_ge(bo_ps, 2 * n + k + 1)
                    square(fb, bank[4 + k], k).then_inc(bo_sb, 1)

            def magnitude(n):
                act_.wait_ge(sq_sb, n + 1)
                act_.activation(fa, fa, ACT.Sqrt).then_inc(mag_sb, 1)

            def rectify(n):
                act_.wait_ge(mixed_sb, n + 1)
                act_.activation(grid(relu), hv[:], ACT.Relu, bias=mix[:, 1:2]).then_inc(relu_sb, 1)

            def out_copy(n):
                for k in range(2):
                    act_.wait_ge(out_ps, 2 * n + k + 1)
                    act_.wait_ge(stored, 16 * n)
                    act_.activation(y_out[:, HALF * k:HALF * k + HALF], bank[6 + k][:], ACT.Identity,
                                    bias=col("out_b")).then_inc(out_sb, 1)

            def conv_early(n, j):
                if j == 0:
                    edge_parts_copy(n, 0)
                    pyr_copy(n, 0)
                elif j == 1:
                    edge_parts_copy(n, 1)
                elif j == 2:
                    row_spectrum_copy(n)
                elif j == 6:
                    inverse_odd_copy(n)
                elif j == 7:
                    turn_odd_copy(n)

            def conv_late(n, j):
                if j == 1:
                    pyr_copy(n, 1)
                    x2_copy(n)
                elif j == 2:
                    spectrum_turn_copy(n)
                elif j == 5:
                    inverse_even_copy(n)
                    edge_tanh(n)
                elif j == 6:
                    turn_even_copy(n)
                    edge_cuts(n)

            def pyr_taps(n, j):
                for k in range(PYR_TAPS[j], PYR_TAPS[j + 1]):
                    pyr_tap(n, k)

            def swin_rest(i):
                queries(i)
                key_heads(i)
                v_copy(i)
                exponent(i, 0)
                exponent(i, 1)
                for j in range(PAIRS):
                    prob_copy(i, j)
                    if j + 2 < PAIRS:
                        exponent(i, j + 2)
                    if j == 4:
                        attention_copy(i, 0)
                deviation2(i, 0)
                attention_copy(i, 1)
                n2_copy(i, 0)
                deviation2(i, 1)
                n2_copy(i, 1)
                mlp_gelu(i)

            def both(n, i):
                to_windows(i)
                in_gelu(n)
                x_copy(i)
                magnitudes(n)
                deviation1(i)
                n_copy(i)
                queries(i)
                key_heads(i)
                route_tanh(n)
                v_copy(i)
                exponent(i, 0)
                route_exponent(n)
                exponent(i, 1)
                for j in range(PAIRS):
                    conv_early(n, j)
                    prob_copy(i, j)
                    if j == 4:
                        attention_copy(i, 0)
                    conv_late(n, j)
                    if j + 2 < PAIRS:
                        exponent(i, j + 2)
                    if j == PAIRS - 1:
                        deviation2(i, 0)
                        attention_copy(i, 1)
                    pyr_taps(n, j)
                square_even(n)
                square_odd(n)
                n2_copy(i, 0)
                deviation2(i, 1)
                pyr_tap(n, 7)
                magnitude(n)
                n2_copy(i, 1)
                mlp_gelu(i, n)
                rectify(n)
                out_copy(n)

            def conv_only(n):
                in_gelu(n)
                magnitudes(n)
                route_tanh(n)
                route_exponent(n)
                for j in range(PAIRS):
                    conv_early(n, j)
                    conv_late(n, j)
                    pyr_taps(n, j)
                pyr_tap(n, 7)
                pyr_tap(n, 8)
                square_even(n)
                square_odd(n)
                magnitude(n)
                rectify(n)
                out_copy(n)

            to_windows(0)
            x_copy(0)
            deviation1(0)
            n_copy(0)
            act_.wait_ge(setup_dve, 1)
            act_.wait_ge(zeroed, 1)
            swin_rest(0)
            both(0, 1)
            with act_.Fori(1, IMAGES - 1) as n:
                both(n, n + 1)
            conv_only(IMAGES - 1)

        @block.gpsimd
        def _(pool):
            pool.memset(act[:], 0.0)
            for padded in (hor, ver, pyr):
                pool.memset(padded[:], 0.0)
            pool.memset(v_pair[:], 0.0)
            pool.drain()
            pool.sem_inc(zeroed, 1)
            pool.wait_ge(setup_dve, 1)

            def residual_in(i):
                pool.wait_ge(xT_sb, 2 * i + 2)
                pool.sem_inc(pool_turns)
                pool.wait_ge(x1_sb, 2 * i)
                pool.sem_inc(pool_turns)
                pool.tensor_tensor(resT[:], xT[:], proj_shift[:].unsqueeze(1).broadcast_to([P, CH, C]), ALU.add)\
                    .then_inc(res_sb, 1)

            def less_max(i, j):
                pool.wait_ge(s_max, 8 * i + j + 1)
                pool.sem_inc(pool_turns)
                pool.tensor_tensor(score[:, j % 3], score[:, j % 3],
                                   row_max[:, j % 3].unsqueeze(2).broadcast_to([P, HEADS, WT]), ALU.subtract)\
                    .then_inc(s_sub, 1)

            def normalise(i, j):
                pool.wait_ge(s_inv, 8 * i + j + 1)
                pool.sem_inc(pool_turns)
                if j >= 2:
                    pool.wait_ge(pT_ps, 8 * i + j - 1)
                    pool.sem_inc(pool_turns)
                pool.tensor_tensor(prob[:, j % 2].rearrange("p (h k) -> p h k", h=HEADS), score[:, j % 3],
                                   row_inv[:, j % 3].unsqueeze(2).broadcast_to([P, HEADS, WT]), ALU.mult)\
                    .then_inc(p_sb, 1)

            mid = AXIS_TAPS // 2
            OFFSETS = [0] + [AXIS_DIL * (t - mid) for t in range(AXIS_TAPS)
                             if t != mid and abs(AXIS_DIL * (t - mid)) < SIDE]

            def axis_conv(n, a, offsets):
                dst, name = ((hor, "dilh"), (ver, "dilv"))[a]
                body = dst[:, 1:1 + SIDE, 1:1 + SIDE]
                for off in offsets:
                    weight = col(name, off // AXIS_DIL + mid)
                    if off == 0:
                        pool.wait_ge(act_sb, 2 * n + 2)
                        pool.sem_inc(pool_turns)
                        pool.wait_ge(hv_sb, n)
                        pool.sem_inc(pool_turns)
                        pool.tensor_scalar(body, act_in, weight, 1.0, ALU.mult, ALU.mult)
                        continue
                    lo, hi = max(0, -off), min(SIDE, SIDE - off)
                    if a == 0:
                        part = (slice(None), slice(None), slice(lo, hi))
                        of = act_in[:, :, lo + off:hi + off]
                    else:
                        part = (slice(None), slice(lo, hi))
                        of = act_in[:, lo + off:hi + off]
                    pool.drain()
                    pool.tensor_scalar(axis_part[part], of, weight, 1.0, ALU.mult, ALU.mult)
                    pool.drain()
                    last = pool.tensor_tensor(body[part], body[part], axis_part[part], ALU.add)
                    if off == OFFSETS[-1]:
                        last.then_inc(axis_sb, 1)

            def add_part(n, k):
                pool.drain()
                pool.wait_ge(part_sb, 9 * n + k + 1)
                pool.sem_inc(pool_turns)
                pool.tensor_tensor(py[:], py[:], grid(parts[k][:, 0:TOK]), ALU.add).then_inc(part_added, 1)
                if k == 8:
                    pool.drain()
                    pool.sem_inc(py_sb, 1)

            def gate_pyramid(n):
                pool.wait_ge(cut_sb, n + 1)
                pool.sem_inc(pool_turns)
                pool.wait_ge(xm_mixed, n + 1)
                pool.sem_inc(pool_turns)
                pool.tensor_tensor(py[:], py[:], edge_cut[:], ALU.mult)
                pool.drain()
                pool.tensor_tensor(py[:], py[:], grid(xm[:]), ALU.add).then_inc(pyramid_gated, 1)

            def square_sum(n):
                pool.wait_ge(be_sb, 2 * n + 2)
                pool.sem_inc(pool_turns)
                pool.wait_ge(bo_sb, 2 * n + 2)
                pool.sem_inc(pool_turns)
                pool.tensor_tensor(fa, fa, fb, ALU.add).then_inc(sq_sb, 1)

            def swin_only(i):
                residual_in(i)
                less_max(i, 0)
                less_max(i, 1)
                for j in range(PAIRS):
                    normalise(i, j)
                    if j + 2 < PAIRS:
                        less_max(i, j + 2)

            def both(n, i):
                axis_conv(n, 0, OFFSETS)
                axis_conv(n, 1, OFFSETS[:3])
                residual_in(i)
                less_max(i, 0)
                less_max(i, 1)
                for j in range(PAIRS):
                    normalise(i, j)
                    if j < 2:
                        axis_conv(n, 1, OFFSETS[3 + j:4 + j])
                    elif j >= 3:
                        add_part(n, j - 2)
                    if j + 2 < PAIRS:
                        less_max(i, j + 2)
                add_part(n, 6)
                square_sum(n)
                add_part(n, 7)
                add_part(n, 8)
                gate_pyramid(n)

            def conv_only(n):
                axis_conv(n, 0, OFFSETS)
                axis_conv(n, 1, OFFSETS)
                add_part(n, 1)
                add_part(n, 2)
                for k in range(3, 7):
                    add_part(n, k)
                square_sum(n)
                add_part(n, 7)
                add_part(n, 8)
                gate_pyramid(n)

            swin_only(0)
            both(0, 1)
            with pool.Fori(1, IMAGES - 1) as n:
                both(n, n + 1)
            conv_only(IMAGES - 1)


def kernel(**inputs):
    import concourse.bacc as bacc
    from concourse.bass_utils import run_bass_kernel_spmd

    a = {k: np.asarray(v) for k, v in inputs.items()}
    swin = {k[8:]: v for k, v in a.items() if k.startswith("L0_conv_")}
    conv = {k[8:]: v for k, v in a.items() if k.startswith("L1_conv_")}

    cols = np.zeros((P, NCOLS), np.float32)

    def put(name, value):
        value = value.reshape(value.shape[0], -1)
        cols[:value.shape[0], COLS[name][0]:COLS[name][0] + value.shape[1]] = value

    put("ln1_g", swin["ln1_g"])
    put("ln1_b", swin["ln1_b"])
    for k, name in enumerate(("q_b", "k_b", "v_b")):
        put(name, swin["qkv_b"][k * C:(k + 1) * C])
    put("ln2_g", swin["ln2_g"])
    put("ln2_b", swin["ln2_b"])
    put("b1", swin["b1"].reshape(FC, P).T)
    put("b2", swin["b2"])
    for name in ("in_b", "out_b", "fac_b", "conv_b", "fuse_w", "fuse_b", "cr_b"):
        put(name, conv[name].T if name == "cr_b" else conv[name])
    put("alpha", conv["fgm_alpha"])
    put("beta", conv["fgm_beta"])
    put("dw_w", conv["dw11_w"])
    put("dw_b", conv["dw11_b"])
    put("pyr_b", conv["pyr_b"].reshape(-1))
    put("vis_b", np.repeat(conv["vis_b"], P))
    put("batt_b1", conv["batt_b1"])
    put("dilh", conv["dilh_w"])
    put("dilv", conv["dilv_w"])
    put("cr_w", conv["cr_w"].reshape(3, C, 9).transpose(1, 0, 2))
    rows = np.concatenate([swin["proj_b"], conv["fgm_b1"], conv["fgm_b2"], conv["fgm_boost"].reshape(-1),
                           conv["batt_b2"], conv["base_weights"]])[None]
    pyr = np.zeros((C, len(DILS), 9, 32), np.float32)
    for o in range(32):
        pyr[4 * o:4 * o + 4, :, :, o] = conv["pyr_w"][:, o].reshape(len(DILS), 4, 9).transpose(1, 0, 2)
    batt2 = np.zeros((P, ROUTES), np.float32)
    batt2[:BATT] = conv["batt_w2"].reshape(ROUTES, BATT).T
    table = np.zeros((2 * P, 32), np.float32)
    table[:REL, :HEADS] = swin["rpb_table"]
    mats = np.concatenate([
        swin["qkv_w"].T, swin["proj_w"].T, swin["w1"].T,
        swin["w2"].reshape(C, FC, P).transpose(2, 1, 0).reshape(P, -1),
        conv["in_w"].reshape(C, C).T, conv["out_w"].reshape(C, C).T, conv["fac_w"].reshape(C, C).T,
        conv["conv_w"].reshape(C, C).T, conv["fgm_w1"].reshape(C, C).T, conv["fgm_w2"].reshape(C, C).T,
        conv["vis_w"].reshape(C, 9), conv["batt_w1"].reshape(BATT, C).T, batt2, pyr.reshape(C, -1),
        table.reshape(2, P, 32).transpose(1, 0, 2).reshape(P, -1)], 1)
    arrays = {
        "x_dram": np.ascontiguousarray(a["x"].reshape(IMAGES, C, TOK)),
        "cols_dram": cols,
        "rows_dram": np.ascontiguousarray(rows),
        "mats_dram": np.ascontiguousarray(mats),
        "cons_dram": shape_constants(),
        "rel_dram": np.ascontiguousarray(swin["rpi"].T.reshape(1, WT * WT)),
    }
    nc = bacc.Bacc("TRN2", target_bir_lowering=False, num_devices=1)
    args = [nc.dram_tensor(k, v.shape, mybir.dt.from_np(v.dtype), kind="ExternalInput").ap()
            for k, v in arrays.items()]
    args.append(nc.dram_tensor("out_dram", (IMAGES, C, TOK), F32, kind="ExternalOutput").ap())
    x_, cols_, rows_, mats_, cons_, rel_, out_ = args
    swin_conv_kernel(nc, x_, cols_, rows_, mats_, cons_, rel_, out_)
    result = run_bass_kernel_spmd(nc, [arrays], core_ids=[0])
    return result.results[0]["out_dram"].reshape(IMAGES, C, SIDE, SIDE)
```
